# Optimizing a Trainium2 kernel written in Bass

```python
import numpy as np
import jax
import jax.numpy as jnp

def _softmax(x, axis=-1):
    return jax.nn.softmax(x, axis=axis)

def _gelu(x):
    return jax.nn.gelu(x, approximate=True)

def _silu(x):
    return jax.nn.silu(x)

def _sigmoid(x):
    return jax.nn.sigmoid(x)

def _layernorm(x, axis=-1, eps=1e-05):
    m = jnp.mean(x, axis=axis, keepdims=True)
    v = jnp.var(x, axis=axis, keepdims=True)
    return (x - m) / jnp.sqrt(v + eps)

def _scatter_add(tgt, idx, src, axis=0):
    return tgt.at[idx].add(src)

def _segment_sum(src, seg, n):
    return jax.ops.segment_sum(src, seg, n)
kernel_name = 'mk_prb_d1_jaxref_r4_a4ab2a'

def setup_inputs(seed: int=0):
    np.random.seed(seed)
    _w = jnp.asarray

    def _L0_attn_setup():
        import jax, jax.numpy as jnp
        import numpy as np
        B, S, D = (8, 256, 256)
        H, HD = (8, 64)
        HID = H * HD
        P = 2 * D
        K = 4
        EPS = 1e-06
        CAP = 15.0

        def _layernorm(x, g, b):
            mu = jnp.mean(x, -1, keepdims=True)
            var = jnp.var(x, -1, keepdims=True)
            return (x - mu) * jax.lax.rsqrt(var + EPS) * g + b

        def _soft_cap(v):
            return CAP * jnp.tanh(v / CAP)

        def _causal_conv_feat(x, w, b):
            L = x.shape[-1]
            xp = jnp.pad(x, ((0, 0), (0, 0), (K - 1, 0)))
            out = b
            for m in range(K):
                out = out + w[m] * xp[..., m:m + L]
            return out

        def _forward(x, ln_g, ln_b, mh_g, mh_b, W_up_l, b_up_l, W_up_r, b_up_r, W_down, b_down, conv_w, conv_b, W_skip, b_skip, W_i, b_i, W_f, b_f, W_o, b_o, W_q, b_q, W_k, b_k, W_v, b_v):
            Bs, Sl, _ = x.shape
            xn = _layernorm(x, ln_g, ln_b)
            x_t = xn @ W_up_l.T + b_up_l
            r_t = xn @ W_up_r.T + b_up_r
            x_c = jax.nn.silu(_causal_conv_feat(x_t, conv_w, conv_b))
            x_skip = x_c @ W_skip.T + b_skip
            q = (x_c @ W_q.T + b_q).reshape(Bs, Sl, H, HD)
            k = (x_c @ W_k.T + b_k).reshape(Bs, Sl, H, HD) / float(np.sqrt(HD))
            v = (x_t @ W_v.T + b_v).reshape(Bs, Sl, H, HD)
            i_pre = _soft_cap(x_c @ W_i.T + b_i)
            f_pre = _soft_cap(x_c @ W_f.T + b_f)
            o = jax.nn.sigmoid(x_t @ W_o.T + b_o)

            def step(carry, inp):
                c, n, m = carry
                qt, kt, vt, it, ft = inp
                m_t = jnp.maximum(ft + m, it)
                ie = jnp.exp(it - m_t)
                fe = jnp.exp(ft - m_t + m)
                c = fe[:, :, None, None] * c + ie[:, :, None, None] * jnp.einsum('bhd,bhe->bhde', vt, kt)
                n = fe[:, :, None] * n + ie[:, :, None] * kt
                num = jnp.einsum('bhde,bhe->bhd', c, qt)
                den = jnp.maximum(jnp.sum(n * qt, -1, keepdims=True), 1.0)
                return ((c, n, m_t), num / den)
            c0 = jnp.zeros((Bs, H, HD, HD), x.dtype)
            n0 = jnp.ones((Bs, H, HD), x.dtype)
            m0 = jnp.zeros((Bs, H), x.dtype)
            seq = tuple((jnp.moveaxis(a, 1, 0) for a in (q, k, v, i_pre, f_pre)))
            _, hs = jax.lax.scan(step, (c0, n0, m0), seq)
            h = o * jnp.moveaxis(hs, 0, 1).reshape(Bs, Sl, HID)
            hn = _layernorm(h.reshape(Bs, Sl, H, HD), mh_g, mh_b).reshape(Bs, Sl, HID)
            out = (hn + x_skip) * jax.nn.silu(r_t)
            return out @ W_down.T + b_down + x
        key = jax.random.key(seed)
        ks = jax.random.split(key, 16)

        def w(kk, shape):
            return jax.random.normal(kk, shape, jnp.float32) / np.sqrt(shape[-1]).astype(np.float32)
        return {'x': jax.random.normal(ks[0], (B, S, D), jnp.float32), 'ln_g': jnp.ones((D,), jnp.float32), 'ln_b': jnp.zeros((D,), jnp.float32), 'mh_g': jnp.ones((H, HD), jnp.float32), 'mh_b': jnp.zeros((H, HD), jnp.float32), 'W_up_l': w(ks[1], (P, D)), 'b_up_l': jnp.zeros((P,), jnp.float32), 'W_up_r': w(ks[2], (HID, D)), 'b_up_r': jnp.zeros((HID,), jnp.float32), 'W_down': w(ks[3], (D, HID)), 'b_down': jnp.zeros((D,), jnp.float32), 'conv_w': jax.random.normal(ks[4], (K,), jnp.float32) * 0.3, 'conv_b': jnp.zeros((), jnp.float32), 'W_skip': w(ks[5], (HID, P)), 'b_skip': jnp.zeros((HID,), jnp.float32), 'W_i': w(ks[6], (H, P)), 'b_i': jnp.zeros((H,), jnp.float32), 'W_f': w(ks[7], (H, P)), 'b_f': jnp.zeros((H,), jnp.float32), 'W_o': w(ks[8], (HID, P)), 'b_o': jnp.zeros((HID,), jnp.float32), 'W_q': w(ks[9], (HID, P)), 'b_q': jnp.zeros((HID,), jnp.float32), 'W_k': w(ks[10], (HID, P)), 'b_k': jnp.zeros((HID,), jnp.float32), 'W_v': w(ks[11], (HID, P)), 'b_v': jnp.zeros((HID,), jnp.float32)}
    _L0_attn_in = _L0_attn_setup()

    def _L0_ffn_setup():
        import jax, jax.numpy as jnp
        import numpy as np
        DIM = 256

        def _reference_tuple_inner(x, W_r, W_k, W_v, mu_r, mu_k):
            B, T, C = x.shape
            x_prev = jnp.concatenate([jnp.zeros((B, 1, C), x.dtype), x[:, :-1, :]], axis=1)
            xr = mu_r * x + (1.0 - mu_r) * x_prev
            xk = mu_k * x + (1.0 - mu_k) * x_prev
            r = jax.nn.sigmoid(jnp.einsum('btc,dc->btd', xr, W_r))
            k = jnp.einsum('btc,dc->btd', xk, W_k)
            k_act = jnp.square(jax.nn.relu(k))
            out = r * jnp.einsum('btc,dc->btd', k_act, W_v)
            new_state = x[:, -1, :]
            return (out, new_state)
        key = jax.random.key(seed)
        ks = jax.random.split(key, 6)
        B, T, C = (8, 512, DIM)
        x = jax.random.normal(ks[0], (B, T, C), dtype=jnp.float32)
        s = 1.0 / np.sqrt(C)
        W_r = jax.random.uniform(ks[1], (C, C), jnp.float32, -s, s)
        W_k = jax.random.uniform(ks[2], (C, C), jnp.float32, -s, s)
        W_v = jax.random.uniform(ks[3], (C, C), jnp.float32, -s, s)
        mu_r = jax.random.uniform(ks[4], (C,), jnp.float32)
        mu_k = jax.random.uniform(ks[5], (C,), jnp.float32)
        return {'x': x, 'W_r': W_r, 'W_k': W_k, 'W_v': W_v, 'mu_r': mu_r, 'mu_k': mu_k}
    _L0_ffn_in = _L0_ffn_setup()
    _d = {'L0_attn_x': _L0_attn_in['x'], 'L0_attn_ln_g': _L0_attn_in['ln_g'], 'L0_attn_ln_b': _L0_attn_in['ln_b'], 'L0_attn_mh_g': _L0_attn_in['mh_g'], 'L0_attn_mh_b': _L0_attn_in['mh_b'], 'L0_attn_W_up_l': _L0_attn_in['W_up_l'], 'L0_attn_b_up_l': _L0_attn_in['b_up_l'], 'L0_attn_W_up_r': _L0_attn_in['W_up_r'], 'L0_attn_b_up_r': _L0_attn_in['b_up_r'], 'L0_attn_W_down': _L0_attn_in['W_down'], 'L0_attn_b_down': _L0_attn_in['b_down'], 'L0_attn_conv_w': _L0_attn_in['conv_w'], 'L0_attn_conv_b': _L0_attn_in['conv_b'], 'L0_attn_W_skip': _L0_attn_in['W_skip'], 'L0_attn_b_skip': _L0_attn_in['b_skip'], 'L0_attn_W_i': _L0_attn_in['W_i'], 'L0_attn_b_i': _L0_attn_in['b_i'], 'L0_attn_W_f': _L0_attn_in['W_f'], 'L0_attn_b_f': _L0_attn_in['b_f'], 'L0_attn_W_o': _L0_attn_in['W_o'], 'L0_attn_b_o': _L0_attn_in['b_o'], 'L0_attn_W_q': _L0_attn_in['W_q'], 'L0_attn_b_q': _L0_attn_in['b_q'], 'L0_attn_W_k': _L0_attn_in['W_k'], 'L0_attn_b_k': _L0_attn_in['b_k'], 'L0_attn_W_v': _L0_attn_in['W_v'], 'L0_attn_b_v': _L0_attn_in['b_v'], 'L0_ffn_W_r': _L0_ffn_in['W_r'], 'L0_ffn_W_k': _L0_ffn_in['W_k'], 'L0_ffn_W_v': _L0_ffn_in['W_v'], 'L0_ffn_mu_r': _L0_ffn_in['mu_r'], 'L0_ffn_mu_k': _L0_ffn_in['mu_k']}
    _x0 = _d['L0_attn_x']
    _d['L0_attn_x'] = jax.random.normal(jax.random.fold_in(jax.random.key(seed), 1), (16, 512, 256), dtype=_x0.dtype)
    del _x0
    return _d

def reference(L0_attn_x, L0_attn_ln_g, L0_attn_ln_b, L0_attn_mh_g, L0_attn_mh_b, L0_attn_W_up_l, L0_attn_b_up_l, L0_attn_W_up_r, L0_attn_b_up_r, L0_attn_W_down, L0_attn_b_down, L0_attn_conv_w, L0_attn_conv_b, L0_attn_W_skip, L0_attn_b_skip, L0_attn_W_i, L0_attn_b_i, L0_attn_W_f, L0_attn_b_f, L0_attn_W_o, L0_attn_b_o, L0_attn_W_q, L0_attn_b_q, L0_attn_W_k, L0_attn_b_k, L0_attn_W_v, L0_attn_b_v, L0_ffn_W_r, L0_ffn_W_k, L0_ffn_W_v, L0_ffn_mu_r, L0_ffn_mu_k):

    def _L0_attn_ref(x, ln_g, ln_b, mh_g, mh_b, W_up_l, b_up_l, W_up_r, b_up_r, W_down, b_down, conv_w, conv_b, W_skip, b_skip, W_i, b_i, W_f, b_f, W_o, b_o, W_q, b_q, W_k, b_k, W_v, b_v):
        import jax, jax.numpy as jnp
        import numpy as np
        B, S, D = (8, 256, 256)
        H, HD = (8, 64)
        HID = H * HD
        P = 2 * D
        K = 4
        EPS = 1e-06
        CAP = 15.0

        def _layernorm(x, g, b):
            mu = jnp.mean(x, -1, keepdims=True)
            var = jnp.var(x, -1, keepdims=True)
            return (x - mu) * jax.lax.rsqrt(var + EPS) * g + b

        def _soft_cap(v):
            return CAP * jnp.tanh(v / CAP)

        def _causal_conv_feat(x, w, b):
            L = x.shape[-1]
            xp = jnp.pad(x, ((0, 0), (0, 0), (K - 1, 0)))
            out = b
            for m in range(K):
                out = out + w[m] * xp[..., m:m + L]
            return out

        def _forward(x, ln_g, ln_b, mh_g, mh_b, W_up_l, b_up_l, W_up_r, b_up_r, W_down, b_down, conv_w, conv_b, W_skip, b_skip, W_i, b_i, W_f, b_f, W_o, b_o, W_q, b_q, W_k, b_k, W_v, b_v):
            Bs, Sl, _ = x.shape
            xn = _layernorm(x, ln_g, ln_b)
            x_t = xn @ W_up_l.T + b_up_l
            r_t = xn @ W_up_r.T + b_up_r
            x_c = jax.nn.silu(_causal_conv_feat(x_t, conv_w, conv_b))
            x_skip = x_c @ W_skip.T + b_skip
            q = (x_c @ W_q.T + b_q).reshape(Bs, Sl, H, HD)
            k = (x_c @ W_k.T + b_k).reshape(Bs, Sl, H, HD) / float(np.sqrt(HD))
            v = (x_t @ W_v.T + b_v).reshape(Bs, Sl, H, HD)
            i_pre = _soft_cap(x_c @ W_i.T + b_i)
            f_pre = _soft_cap(x_c @ W_f.T + b_f)
            o = jax.nn.sigmoid(x_t @ W_o.T + b_o)

            def step(carry, inp):
                c, n, m = carry
                qt, kt, vt, it, ft = inp
                m_t = jnp.maximum(ft + m, it)
                ie = jnp.exp(it - m_t)
                fe = jnp.exp(ft - m_t + m)
                c = fe[:, :, None, None] * c + ie[:, :, None, None] * jnp.einsum('bhd,bhe->bhde', vt, kt)
                n = fe[:, :, None] * n + ie[:, :, None] * kt
                num = jnp.einsum('bhde,bhe->bhd', c, qt)
                den = jnp.maximum(jnp.sum(n * qt, -1, keepdims=True), 1.0)
                return ((c, n, m_t), num / den)
            c0 = jnp.zeros((Bs, H, HD, HD), x.dtype)
            n0 = jnp.ones((Bs, H, HD), x.dtype)
            m0 = jnp.zeros((Bs, H), x.dtype)
            seq = tuple((jnp.moveaxis(a, 1, 0) for a in (q, k, v, i_pre, f_pre)))
            _, hs = jax.lax.scan(step, (c0, n0, m0), seq)
            h = o * jnp.moveaxis(hs, 0, 1).reshape(Bs, Sl, HID)
            hn = _layernorm(h.reshape(Bs, Sl, H, HD), mh_g, mh_b).reshape(Bs, Sl, HID)
            out = (hn + x_skip) * jax.nn.silu(r_t)
            return out @ W_down.T + b_down + x
        return _forward(x, ln_g, ln_b, mh_g, mh_b, W_up_l, b_up_l, W_up_r, b_up_r, W_down, b_down, conv_w, conv_b, W_skip, b_skip, W_i, b_i, W_f, b_f, W_o, b_o, W_q, b_q, W_k, b_k, W_v, b_v)

    def _L0_ffn_ref(x, W_r, W_k, W_v, mu_r, mu_k):
        import jax, jax.numpy as jnp
        import numpy as np
        DIM = 256

        def _reference_tuple_inner(x, W_r, W_k, W_v, mu_r, mu_k):
            B, T, C = x.shape
            x_prev = jnp.concatenate([jnp.zeros((B, 1, C), x.dtype), x[:, :-1, :]], axis=1)
            xr = mu_r * x + (1.0 - mu_r) * x_prev
            xk = mu_k * x + (1.0 - mu_k) * x_prev
            r = jax.nn.sigmoid(jnp.einsum('btc,dc->btd', xr, W_r))
            k = jnp.einsum('btc,dc->btd', xk, W_k)
            k_act = jnp.square(jax.nn.relu(k))
            out = r * jnp.einsum('btc,dc->btd', k_act, W_v)
            new_state = x[:, -1, :]
            return (out, new_state)
        return _reference_tuple_inner(x, W_r, W_k, W_v, mu_r, mu_k)[0]
    x = L0_attn_x
    xn = _layernorm(x, axis=-1)
    x = x + _L0_attn_ref(xn, L0_attn_ln_g, L0_attn_ln_b, L0_attn_mh_g, L0_attn_mh_b, L0_attn_W_up_l, L0_attn_b_up_l, L0_attn_W_up_r, L0_attn_b_up_r, L0_attn_W_down, L0_attn_b_down, L0_attn_conv_w, L0_attn_conv_b, L0_attn_W_skip, L0_attn_b_skip, L0_attn_W_i, L0_attn_b_i, L0_attn_W_f, L0_attn_b_f, L0_attn_W_o, L0_attn_b_o, L0_attn_W_q, L0_attn_b_q, L0_attn_W_k, L0_attn_b_k, L0_attn_W_v, L0_attn_b_v) + _L0_ffn_ref(xn, L0_ffn_W_r, L0_ffn_W_k, L0_ffn_W_v, L0_ffn_mu_r, L0_ffn_mu_k)
    return x

_drawn_inputs = setup_inputs


def setup_inputs(seed=0):
    import zlib

    import numpy as np

    out = dict(_drawn_inputs(seed))
    spreads = {'L0_attn_ln_g': (1.0, 0.2),
     'L0_attn_ln_b': (0.0, 0.1),
     'L0_attn_mh_g': (1.0, 0.2),
     'L0_attn_mh_b': (0.0, 0.1),
     'L0_attn_b_up_l': (0.0, 0.1),
     'L0_attn_b_up_r': (0.0, 0.1),
     'L0_attn_b_down': (0.0, 0.1),
     'L0_attn_b_skip': (0.0, 0.267),
     'L0_attn_b_i': (0.0, 0.8),
     'L0_attn_b_f': (0.0, 0.1),
     'L0_attn_b_o': (0.0, 0.713),
     'L0_attn_b_q': (0.0, 0.1),
     'L0_attn_b_k': (0.0, 0.1),
     'L0_attn_b_v': (0.0, 0.1)}
    factors = {'L0_ffn_W_r': 6.696, 'L0_ffn_mu_r': 8.0}
    for name, (base, spread) in spreads.items():
        noise = np.random.default_rng([zlib.crc32(name.encode()), seed]).standard_normal(out[name].shape)
        drawn = base * np.exp(spread * noise) if base else spread * noise
        out[name] = jnp.asarray(drawn.astype(out[name].dtype))
    for name, factor in factors.items():
        out[name] = (out[name] * factor).astype(out[name].dtype)
    return out
```

```python
from contextlib import ExitStack

import concourse.bass as bass
from concourse import mybir

F32 = mybir.dt.float32
F32R = mybir.dt.float32r
BF16 = mybir.dt.bfloat16
ALU = mybir.AluOpType
ACT = mybir.ActivationFunctionType

EPS_OUTER = 1e-5
EPS_ATTN = 1e-6
CAP = 15.0
TAPS = 4

RING = 4
FRONT = ["conv0", "conv1", "ffn_k", "ffn_r", "gates", "q0", "q1", "ffn_v", "k0", "k1", "cols"]
HALF_END = [None, None, ("gt", 0), None, ("down", 0), None, None, None, None, None, None, ("gt", 1), None, None,
            ("down", 1)]


def ring_order(kind):
    if kind == "first":
        return [(p, 0, 0) for p in ["xf", "xa"] + FRONT]
    out = []
    for h in range(2):
        front = kind == "body" or h == 0
        out += [(p, h, 0) for p in ("o", "r", "skip", "decay", "kt", "v")]
        out += [(p, h, 1) for p in ("o", "r", "skip", "decay", "kt")]
        out += [(p, h + 1, 0) for p in ("xf", "xa")] if front else []
        out += [("v", h, 1)]
        ahead = iter(FRONT)
        for end in HALF_END:
            if end:
                out += [(end[0], h, end[1])]
            elif front:
                out += [(next(ahead), h + 1, 0)]
    return out


def ring_places(kind):
    at, out = [0] * RING, {}
    for i, use in enumerate(ring_order(kind)):
        out[use] = (i % RING, at[i % RING])
        at[i % RING] += 1
    return out, at


FIRST_PLACES, FIRST_USES = ring_places("first")
BODY_PLACES, BODY_USES = ring_places("body")
LAST_PLACES, _ = ring_places("last")


def ring_use(kind, b, use):
    if kind == "first":
        return FIRST_PLACES[use]
    bank, before = (BODY_PLACES if kind == "body" else LAST_PLACES)[use]
    return bank, b * BODY_USES[bank] + (FIRST_USES[bank] + before)


def mlstm_rwkv_block(nc, x, ln_g, ln_b, mh_g, mh_b, W_up_l, b_up_l, W_up_r, b_up_r, W_down, b_down,
                     conv_w, conv_b, W_skip, b_skip, W_i, b_i, W_f, b_f, W_o, b_o, W_q, b_q, W_k, b_k,
                     W_v, b_v, F_r, F_k, F_v, mu_r, mu_k, out):
    B, S, D = x.shape
    P = W_up_l.shape[0]
    H, HD = mh_g.shape
    HID = H * HD
    T = 128
    KD, KP = D // T, P // T
    HALF = 2 * T
    HALVES = S // HALF
    PAIRS = H // 2
    PW = 2 * (HD + 1)
    assert HALVES == 2 and D == 256 and P == 512 and HID == 512 and HD == 64 and H == 8

    x_dram = x.rearrange("b (h c p) d -> (b h) p c d", c=2, p=T)
    out_dram = out.rearrange("b (t p) d -> (b t) p d", p=T)

    keep = ExitStack()
    with keep:
        def sb(name, shape, dt=F32, stack=keep):
            return stack.enter_context(nc.sbuf_tensor(name, shape, dt))

        def sem(name):
            return keep.enter_context(nc.semaphore(name))

        ring = keep.enter_context(nc.psum_tensor("ring", [T, RING, 512], F32))
        sc_ps = keep.enter_context(nc.psum_tensor("sc_ps", [T, 2, 512], F32))
        num_ps = keep.enter_context(nc.psum_tensor("num_ps", [T, 2, 512], F32))

        def halves(name, shape):
            return sb(name + "_hi", shape, F32R), sb(name + "_lo", shape, F32R)

        wc = halves("wc", [T, KD, P])
        wv = halves("wv", [T, KD, HID])
        wo = halves("wo", [T, KD, HID])
        wr = halves("wr", [T, KD, HID])
        wq = halves("wq", [T, KP, HID])
        wk = halves("wk", [T, KP, HID])
        ws = halves("ws", [T, KP, HID])
        wif = halves("wif", [T, KP, 40])
        wd = sb("wd", [T, KP, D])
        fr = sb("fr", [T, KD, D])
        fk = sb("fk", [T, KD, D])
        fv = sb("fv", [T, KD, D])

        ident = sb("ident", [T, T])
        sel_m = sb("sel_m", [72, H, T], BF16)
        sel_g = sb("sel_g", [72, PAIRS, T], BF16)
        ones_r = sb("ones_r", [T, HALF], F32R)
        bias_rows = sb("bias_rows", [T, 3, 512], F32R)
        bv_all = sb("bv_all", [T, HID])
        bs_all = sb("bs_all", [T, HID])
        mhg_all = sb("mhg_all", [T, HID])
        bd_all = sb("bd_all", [T, D])
        q_bias = sb("q_bias", [T, KP])
        k_bias = sb("k_bias", [T, KP])
        if_bias = sb("if_bias", [40, 1])
        mu = sb("mu", [T, 2, KD])
        one_mu = sb("one_mu", [T, 2, KD])
        chunk_keep = sb("chunk_keep", [H, HALF])
        zero2 = sb("zero2", [T, KD, 1])
        minus_half = sb("minus_half", [T, H])
        CB, OB, RB = 0, 1, 2

        small_loaded = sem("small_loaded")
        rows_loaded = sem("rows_loaded")
        const_ready = sem("const_ready")
        dve_prep = sem("dve_prep")
        prep_filled = sem("prep_filled")
        prep_hi = sem("prep_hi")
        prep_act = sem("prep_act")
        prep_dve = sem("prep_dve")

        prep = ExitStack()
        with prep:
            def tmp(name, shape, dt=F32):
                return sb(name, shape, dt, prep)

            ul = tmp("ul", [T, KP, D])
            stage = tmp("stage", [T, 2, 2048])
            wt = tmp("wt", [T, KP, 512])
            ult = tmp("ult", [T, KD, 3 + P])
            bl = tmp("bl", [T, 3 + P])
            bl_t = tmp("bl_t", [T, KP, T])
            lnb_rep = tmp("lnb_rep", [T, KD, T])
            lng = tmp("lng", [T, KD])
            lnb = tmp("lnb", [T, KD])
            cw = tmp("cw", [T, TAPS])
            cb = tmp("cb", [T, 1])
            fold = tmp("fold", [T, P])
            row = tmp("row", [2, P])
            row2 = tmp("row2", [2, P])
            row_hi = tmp("row_hi", [2, P], F32R)
            bup_l_all = tmp("bup_l_all", [T, P])
            b0_all = tmp("b0_all", [T, 3, HID])
            mhb_all = tmp("mhb_all", [T, HID])

            TURNS = [("ult", 0, "dve"), ("ult", 1, "dve"), ("bl", 0, "dve"), ("bl_t", 0, "dve")]
            for w in ("v", "o"):
                TURNS += [("wt_" + w, k, "act") for k in range(KP)]
                TURNS += [("fold_" + w, k, "split") for k in range(KD)]
                TURNS += [("bias_" + w, 0, "dve")]
            TURNS += [("wt_r", k, "split") for k in range(KD)] + [("bias_r", 0, "dve")]
            for w in ("q", "k", "s"):
                TURNS += [("wt_" + w, k, "split") for k in range(KP)]
            TURNS += [("wt_if", 0, "split"), ("wt_d", 0, "act"), ("wt_d", 1, "act")]
            TURNS += [("wt_fr", 0, "act"), ("wt_fk", 0, "act"), ("wt_fv", 0, "act")]

            act_count, dve_count, hi_count = [], [], []
            a = d = hi = 0
            for _, _, last in TURNS:
                a += last == "act"
                d += last in ("dve", "split")
                hi += last == "split"
                act_count.append(a)
                dve_count.append(d)
                hi_count.append(hi)

            def turn_of(what, which=0):
                return next(i for i, t in enumerate(TURNS) if t[:2] == (what, which))

            def wait_emptied(eng, i):
                if TURNS[i][2] == "act":
                    eng.wait_ge(prep_act, act_count[i])
                else:
                    eng.wait_ge(prep_dve, dve_count[i])

            STAGED = ["v", "o", "r", "q", "k", "s", "if", "d", "fr", "fk", "fv"]
            SOURCE = {"v": W_v, "o": W_o, "r": W_up_r, "q": W_q, "k": W_k, "s": W_skip, "d": W_down,
                      "fr": F_r, "fk": F_k, "fv": F_v}
            LAST_TURN = {"v": ("wt_v", 3), "o": ("wt_o", 3), "r": ("wt_r", 1), "q": ("wt_q", 3),
                         "k": ("wt_k", 3), "s": ("wt_s", 3), "if": ("wt_if", 0), "d": ("wt_d", 1),
                         "fr": ("wt_fr", 0), "fk": ("wt_fk", 0), "fv": ("wt_fv", 0)}
            def staged(name):
                slot = stage[:, STAGED.index(name) % 2, :]
                if name == "if":
                    return slot[0:40, 0:P]
                o, i = SOURCE[name].shape
                return slot[:, 0:o // T * i].rearrange("p (o i) -> p o i", i=i)

            ul_loaded = sem("ul_loaded")
            stage_loaded = {name: sem("stage_loaded_" + name) for name in STAGED}

            def split_source(what, bank):
                return bank[:, 0:KP * 40] if what == "wt_if" else bank

            def split_target(what, k, part):
                if what == "fold_v":
                    return wv[part][:, k, :], lng[:, k:k + 1]
                if what == "fold_o":
                    return wo[part][:, k, :], lng[:, k:k + 1]
                if what == "wt_r":
                    return wr[part][:, k, :], lng[:, k:k + 1]
                if what == "wt_if":
                    return wif[part][:].rearrange("p k o -> p (k o)"), 0.5
                w, scale = {"wt_q": (wq, 0.5), "wt_k": (wk, 0.5 / HD ** 0.5), "wt_s": (ws, 0.5)}[what]
                return w[part][:, k, :], scale

            block = prep.enter_context(nc.Block())

            @block.sync
            def _(sp):
                sp.dma_start(ul[:], W_up_l.rearrange("(o p) i -> p o i", p=T)).then_inc(ul_loaded, 16)
                for k, name in enumerate(STAGED):
                    if k >= 2:
                        i = turn_of(*LAST_TURN[STAGED[k - 2]])
                        sp.wait_ge(prep_filled, i + 1)
                    if name == "if":
                        sp.dma_start(staged(name)[0:H, :], W_i).then_inc(stage_loaded[name], 16)
                        sp.dma_start(staged(name)[32:32 + H, :], W_f).then_inc(stage_loaded[name], 16)
                    else:
                        sp.dma_start(staged(name), SOURCE[name].rearrange("(o p) i -> p o i", p=T)
                                     ).then_inc(stage_loaded[name], 16)

            @block.gpsimd
            def _(pool):
                nc.gpsimd.memset(ident[:], 0.0).then_inc(const_ready, 1)
                nc.gpsimd.memset(sel_m[:], 0.0).then_inc(const_ready, 1)
                nc.gpsimd.memset(sel_g[:], 0.0).then_inc(const_ready, 1)
                pool.wait_ge(const_ready, 3)
                nc.gpsimd.affine_select(out=ident[:], in_=ident[:], compare_op=ALU.not_equal, fill=1.0, base=0,
                                        pattern=[[-1, T]], channel_multiplier=1).then_inc(const_ready, 1)
                done = 4
                for part in range(3):
                    nc.gpsimd.affine_select(out=sel_m[:], in_=sel_m[:], compare_op=ALU.not_equal, fill=1.0,
                                            base=-32 * part, pattern=[[-1, H], [0, T]],
                                            channel_multiplier=1)
                    last = nc.gpsimd.affine_select(
                        out=sel_g[:].rearrange("p j (s e) -> p j s e", s=2),
                        in_=sel_g[:].rearrange("p j (s e) -> p j s e", s=2), compare_op=ALU.not_equal,
                        fill=1.0, base=-32 * part, pattern=[[-2, PAIRS], [-1, 2], [0, HD]],
                        channel_multiplier=1)
                    if part < 2:
                        last.then_inc(const_ready, 1)
                        done += 1
                        pool.wait_ge(const_ready, done)
                def col(v, n):
                    return v.rearrange("(k p) -> p k", p=T)

                for dst, src in ((lng[:], col(ln_g, KD)), (lnb[:], col(ln_b, KD)), (mu[:, 0, :], col(mu_r, KD)),
                                 (mu[:, 1, :], col(mu_k, KD)), (q_bias[:], col(b_q, KP)),
                                 (k_bias[:], col(b_k, KP)),
                                 (if_bias[0:H, :], b_i.rearrange("(h a) -> h a", a=1)),
                                 (if_bias[32:32 + H, :], b_f.rearrange("(h a) -> h a", a=1)),
                                 (cw[:], conv_w.partition_broadcast(T)),
                                 (cb[:], conv_b.partition_broadcast(T))):
                    pool.dma_start(dst, src, allow_slow_non_contiguous=True).then_inc(small_loaded, 16)

            @block.scalar
            def _(act):
                def rows(v, n):
                    return v.partition_broadcast(T)

                for dst, src in ((bup_l_all[:], rows(b_up_l, P)), (b0_all[:, 0, :], rows(b_v, HID)),
                                 (b0_all[:, 1, :], rows(b_o, HID)), (b0_all[:, 2, :], rows(b_up_r, HID)),
                                 (bs_all[:], rows(b_skip, HID)),
                                 (mhb_all[:], rows(mh_b.rearrange("h d -> (h d)"), HID)),
                                 (mhg_all[:], rows(mh_g.rearrange("h d -> (h d)"), HID)),
                                 (bd_all[:], rows(b_down, D))):
                    act.dma_start(dst, src).then_inc(rows_loaded, 16)
                for i, (what, k, last) in enumerate(TURNS):
                    if last == "dve":
                        continue
                    act.wait_ge(prep_filled, i + 1)
                    bank = ring[:, i % RING, :]
                    if last == "split":
                        dst, scale = split_target(what, k, 0)
                        if what in ("fold_v", "fold_o", "wt_r"):
                            act.wait_ge(small_loaded, 160)
                        nc.scalar.activation(dst, split_source(what, bank), ACT.Copy, scale=scale).then_inc(prep_hi, 1)
                        continue
                    if what in ("wt_v", "wt_o"):
                        if what == "wt_o":
                            act.wait_ge(prep_filled, turn_of("bias_v") + 1)
                        dst, scale = wt[:, k, :], 1.0
                    elif what == "wt_d":
                        dst, scale = wd[:, 2 * k:2 * k + 2, :].rearrange("p k o -> p (k o)"), 0.5
                    else:
                        m = {"wt_fr": fr, "wt_fk": fk, "wt_fv": fv}[what]
                        dst, scale = m[:].rearrange("p k o -> p (k o)"), 0.5 if what == "wt_fv" else 1.0
                    nc.scalar.activation(dst, bank, ACT.Copy, scale=scale).then_inc(prep_act, 1)

            @block.tensor
            def _(pe):
                pe.wait_ge(const_ready, 4)
                for i, (what, k, last) in enumerate(TURNS):
                    if i >= RING:
                        wait_emptied(pe, i - RING)
                    bank = ring[:, i % RING, :]
                    if what == "ult":
                        pe.wait_ge(ul_loaded, 16)
                        for o in range(KP):
                            mm = pe.transpose(bank[:, o * T:(o + 1) * T], ul[:, o, k * T:(k + 1) * T], ident[:])
                    elif what == "bl":
                        pe.wait_ge(prep_dve, dve_count[turn_of("ult", 1)])
                        for j in range(KD):
                            mm = pe.matmul(bank, lnb_rep[:, j, :], ult[:, j, 3:], start=j == 0, stop=j == KD - 1)
                    elif what == "bl_t":
                        pe.wait_ge(prep_dve, dve_count[turn_of("bl")])
                        for o in range(KP):
                            mm = pe.transpose(bank[:, o * T:(o + 1) * T], bl[:, 3 + o * T:3 + (o + 1) * T], ident[:])
                    elif what in ("fold_v", "fold_o"):
                        pe.wait_ge(prep_act, act_count[turn_of("wt_" + what[-1], KP - 1)])
                        for j in range(KP):
                            mm = pe.matmul(bank, ul[:, j, k * T:(k + 1) * T], wt[:, j, :],
                                           start=j == 0, stop=j == KP - 1)
                    elif what in ("bias_v", "bias_o"):
                        pe.wait_ge(prep_dve, dve_count[turn_of("bl_t")])
                        for j in range(KP):
                            mm = pe.matmul(bank, bl_t[:, j, :], wt[:, j, :], start=j == 0, stop=j == KP - 1)
                    elif what == "bias_r":
                        pe.wait_ge(prep_dve, dve_count[turn_of("wt_r", 1)])
                        for j in range(KD):
                            mm = pe.matmul(bank, lnb_rep[:, j, :], wt[:, j, :], start=j == 0, stop=j == KD - 1)
                    else:
                        name = what[3:]
                        src = staged(name)
                        pe.wait_ge(stage_loaded[name], 32 if name == "if" else 16)
                        if name == "if":
                            for j in range(KP):
                                mm = pe.transpose(bank[:, j * 40:(j + 1) * 40], src[:, j * T:(j + 1) * T],
                                                  ident[0:40, 0:40])
                        elif name in ("d", "fr", "fk", "fv"):
                            for j in range(2):
                                for o in range(2):
                                    kk = 2 * k + j
                                    mm = pe.transpose(bank[:, j * D + o * T:j * D + (o + 1) * T],
                                                      src[:, o, kk * T:(kk + 1) * T], ident[:])
                        else:
                            for o in range(KP):
                                mm = pe.transpose(bank[:, o * T:(o + 1) * T], src[:, o, k * T:(k + 1) * T], ident[:])
                    mm.then_inc(prep_filled, 1)

            @block.vector
            def _(dve):
                steps = [0]

                def link(ins):
                    steps[0] += 1
                    ins.then_inc(dve_prep, 1)
                    dve.wait_ge(dve_prep, steps[0])

                nc.vector.memset(ult[:, :, 0:3], 0.0)
                nc.vector.memset(bl[:, 0:3], 0.0)
                nc.vector.memset(zero2[:], 0.0)
                nc.vector.memset(ones_r[:].bitcast(F32), 1.0)
                nc.vector.memset(bias_rows[:].bitcast(F32), 0.0)
                nc.vector.memset(minus_half[:], -0.5)
                nc.vector.memset(chunk_keep[:], 1.0)
                link(nc.vector.memset(wt[:, 0, 0:T], 1.0))
                nc.vector.memset(chunk_keep[:, 0:HALF:T], 0.0)
                dve.wait_ge(small_loaded, 160)
                for k in range(KD):
                    link(nc.vector.tensor_scalar(lnb_rep[:, k, :], wt[:, 0, 0:T], lnb[:, k:k + 1], None, ALU.mult))
                link(nc.vector.tensor_scalar(one_mu[:], mu[:], -1.0, 1.0, ALU.mult, ALU.add))
                link(nc.vector.tensor_scalar(k_bias[:], k_bias[:], HD ** -0.5, None, ALU.mult))
                link(nc.vector.tensor_scalar(if_bias[0:H, :], if_bias[0:H, :], 1.0 / CAP, None, ALU.mult))
                link(nc.vector.tensor_scalar(if_bias[32:32 + H, :], if_bias[32:32 + H, :], 1.0 / CAP, None, ALU.mult))
                dve.wait_ge(rows_loaded, 128)
                link(nc.vector.tensor_tensor(bs_all[:], bs_all[:], mhb_all[:], ALU.add))

                def bias_row(dst, src):
                    link(nc.vector.tensor_copy(row_hi[:], src))
                    link(nc.vector.tensor_tensor(row[:], src, row_hi[:].bitcast(F32), ALU.subtract))
                    link(nc.vector.tensor_scalar(row2[:], row_hi[:].bitcast(F32), ident[0:2, 0:1], None, ALU.mult))
                    link(nc.vector.scalar_tensor_tensor(out=bias_rows[0:2, dst, :], in0=row[:], scalar=ident[0:2, 1:2],
                                                        in1=row2[:], op0=ALU.mult, op1=ALU.add))

                dve.wait_ge(const_ready, 4)
                for i, (what, k, last) in enumerate(TURNS):
                    if last == "act":
                        continue
                    dve.wait_ge(prep_filled, i + 1)
                    bank = ring[:, i % RING, :]
                    if last == "split":
                        hi_dst, _ = split_target(what, k, 0)
                        lo_dst, scale = split_target(what, k, 1)
                        dve.wait_ge(prep_hi, hi_count[i])
                        if what == "wt_r":
                            nc.vector.tensor_copy(wt[:, k, :], bank)
                        nc.vector.scalar_tensor_tensor(out=lo_dst, in0=split_source(what, bank), scalar=scale,
                                                       in1=hi_dst.bitcast(F32), op0=ALU.mult,
                                                       op1=ALU.subtract).then_inc(prep_dve, 1)
                    elif what == "ult":
                        nc.vector.tensor_copy(ult[:, k, 3:], bank).then_inc(prep_dve, 1)
                    elif what == "bl":
                        nc.vector.tensor_tensor(bl[:, 3:], bank, bup_l_all[:], ALU.add).then_inc(prep_dve, 1)
                    elif what == "bl_t":
                        nc.vector.tensor_copy(bl_t[:].rearrange("p k j -> p (k j)"), bank).then_inc(prep_dve, 1)
                        for j in range(KD):
                            link(nc.vector.tensor_scalar(fold[:], ult[:, j, 0:P], cw[:, 0:1], None, ALU.mult))
                            for m in range(1, TAPS):
                                link(nc.vector.scalar_tensor_tensor(out=fold[:], in0=ult[:, j, m:m + P],
                                                                    scalar=cw[:, m:m + 1], in1=fold[:],
                                                                    op0=ALU.mult, op1=ALU.add))
                            link(nc.vector.tensor_scalar(fold[:], fold[:], lng[:, j:j + 1], None, ALU.mult))
                            link(nc.vector.tensor_copy(wc[0][:, j, :], fold[:]))
                            link(nc.vector.tensor_tensor(wc[1][:, j, :], fold[:], wc[0][:, j, :].bitcast(F32),
                                                         ALU.subtract))
                        link(nc.vector.tensor_scalar(fold[:], bl[:, 0:P], cw[:, 0:1], cb[:, 0:1], ALU.mult, ALU.add))
                        for m in range(1, TAPS):
                            link(nc.vector.scalar_tensor_tensor(out=fold[:], in0=bl[:, m:m + P],
                                                                scalar=cw[:, m:m + 1], in1=fold[:],
                                                                op0=ALU.mult, op1=ALU.add))
                        bias_row(CB, fold[0:2, :])
                    elif what == "bias_v":
                        nc.vector.tensor_tensor(bv_all[:], bank, b0_all[:, 0, :], ALU.add).then_inc(prep_dve, 1)
                    else:
                        src, dst = (1, OB) if what == "bias_o" else (2, RB)
                        nc.vector.tensor_tensor(fold[:], bank, b0_all[:, src, :], ALU.add).then_inc(prep_dve, 1)
                        dve.wait_ge(prep_dve, dve_count[i])
                        bias_row(dst, fold[0:2, :])

        xin = sb("xin", [T, 2, D])
        xf = sb("xf", [T, 2, D])
        xa = sb("xa", [T, 2, D])
        xa_t = [halves(f"xa_t{h}", [T, KD, HALF]) for h in range(2)]
        xf_t = sb("xf_t", [T, KD, 1 + HALF])
        mix_r = sb("mix_r", [T, KD, HALF])
        mix_k = sb("mix_k", [T, KD, HALF])
        kact = sb("kact", [T, KD, HALF])
        ffn = sb("ffn", [T, 2, D])
        base = [sb(f"base{h}", [T, 2, D]) for h in range(2)]
        conv_act = [sb(f"conv_act{j}", [T, 2 * HALF]) for j in range(2)]
        xc = halves("xc", [T, KP, HALF])
        q_t = sb("q_t", [T, PAIRS, HALF])
        k_t = sb("k_t", [T, PAIRS, HALF])
        q_dec = sb("q_dec", [T, PAIRS, T])
        k_w = sb("k_w", [T, HID])
        dec = sb("dec", [T, 2, PAIRS, T])
        v_sb = sb("v_sb", [T, H * PW + HD + 1])
        th_o = [sb(f"th_o{c}", [T, HID]) for c in range(2)]
        sr = [sb(f"sr{c}", [T, HID]) for c in range(2)]
        sk = [sb(f"sk{c}", [T, HID]) for c in range(2)]
        hid = [sb(f"hid{c}", [T, H, HD]) for c in range(2)]
        gt = sb("gt", [T, KP, T])
        res = [sb(f"res{c}", [T, D]) for c in range(2)]
        state = sb("state", [T, PAIRS, PW])
        carry = sb("carry", [T, PAIRS])
        den = sb("den", [T, 2, 4])
        ln_st = sb("ln_st", [T, 2, 6])
        ln_mv = sb("ln_mv", [T, 2, 2])
        ln_sc = sb("ln_sc", [T, 4, 2])
        mh_st = sb("mh_st", [T, H, 6])
        mh_sc = sb("mh_sc", [T, 6, H])
        row_i = sb("row_i", [H, HALF])
        row_f = sb("row_f", [H, HALF])
        row_F = sb("row_F", [H, HALF])
        row_m = [sb(f"row_m{h}", [H, 1 + HALF]) for h in range(2)]
        row_M = sb("row_M", [H, HALF])
        row_g = sb("row_g", [H, HALF])
        row_rem = sb("row_rem", [H, HALF])
        row_mid = sb("row_mid", [H, HALF], BF16)
        rows_aw = sb("rows_aw", [40, HALF])
        cols_aw = sb("cols_aw", [T, 2, 40])
        m_parts = sb("m_parts", [72, HALF], BF16)
        g_parts = sb("g_parts", [72, HALF], BF16)

        x_loaded = sem("x_loaded")
        x_used = sem("x_used")
        stats_ready = sem("stats_ready")
        scale_ready = sem("scale_ready")
        xh_ready = sem("xh_ready")
        xa_hi_ready = sem("xa_hi_ready")
        xf_t_carried = sem("xf_t_carried")
        mix_prev_ready = sem("mix_prev_ready")
        mix_ready = sem("mix_ready")
        kact_ready = sem("kact_ready")
        base_ready = sem("base_ready")
        conv_tanh_ready = sem("conv_tanh_ready")
        xc_hi_ready = sem("xc_hi_ready")
        xc_lo_ready = sem("xc_lo_ready")
        exp_args_ready = sem("exp_args_ready")
        exp_rows_ready = sem("exp_rows_ready")
        parts_ready = sem("parts_ready")
        sc_filled = [sem(f"sc_filled{j}") for j in range(2)]
        sc_emptied = [sem(f"sc_emptied{j}") for j in range(2)]
        masked = sem("masked")
        num_filled = sem("num_filled")
        num_emptied = sem("num_emptied")
        state_reset = sem("state_reset")
        cols_ready = sem("cols_ready")
        r_tanh_ready = sem("r_tanh_ready")
        gated = [sem(f"gated{c}") for c in range(2)]
        mh_stats_ready = sem("mh_stats_ready")
        normed = sem("normed")
        out_ready = [sem(f"out_ready{c}") for c in range(2)]
        out_stored = [sem(f"out_stored{c}") for c in range(2)]
        buffers_cleared = sem("buffers_cleared")
        buffers_ready = sem("buffers_ready")
        pe_settled = sem("pe_settled")
        pool_settled = sem("pool_settled")
        dve_settled = sem("dve_settled")
        state_cleared = sem("state_cleared")
        ring_filled = [sem(f"ring_filled{j}") for j in range(RING)]
        ring_emptied = [sem(f"ring_emptied{j}") for j in range(RING)]
        dve_front_step = sem("dve_front_step")
        dve_tile_step = sem("dve_tile_step")
        pool_front_step = sem("pool_front_step")
        pool_tile_step = sem("pool_tile_step")

        SC_USES = 3 * 4 - 1

        def sc_use(b, h, c, k):
            return b * SC_USES + (3 * (2 * h + c) + k)

        def sc_free(b, h, c, k):
            return b * SC_USES + (3 * (2 * h + c) + k + 1)

        def tile_of(b, h, c):
            return b * 4 + (2 * h + c)

        main = nc.Block()
        block = keep.enter_context(main)

        def v_head(h, width):
            at = (HD + 1) + PW * h
            return v_sb[:, at:at + width]

        def settle(eng, count):
            eng.sem_inc(count, 1)

        @block.sync
        def _(sp):
            sp.dma_start(xin[:], x_dram[0]).then_inc(x_loaded, 16)

            def body(b, last):
                for h in range(2):
                    n = b * 2 + h
                    if not (last and h == 1):
                        sp.wait_ge(x_used, n + 1)
                        sp.dma_start(xin[:], x_dram[n + 1]).then_inc(x_loaded, 16)
                    for c in range(2):
                        bank, before = ring_use("last" if last else "body", b, ("down", h, c))
                        sp.wait_ge(ring_emptied[bank], before + 1)
                        sp.dma_start(out_dram[tile_of(b, h, c)], res[c][:]).then_inc(out_stored[c], 16)

            with sp.Fori(0, B - 1) as b:
                body(b, False)
            body(B - 1, True)
            for c in range(2):
                sp.wait_ge(out_stored[c], 16 * (2 * B + 1))

        @block.tensor
        def _(pe):
            def take(kind, b, use):
                bank, before = ring_use(kind, b, use)
                pe.wait_ge(ring_emptied[bank], before)
                return ring[:, bank, :], ring_filled[bank]

            def emptied(kind, b, use):
                bank, before = ring_use(kind, b, use)
                pe.wait_ge(ring_emptied[bank], before + 1)

            def transposes_x(kind, b, r, n):
                pe.wait_ge(xh_ready, n + 1)
                for use, src in (("xf", xf), ("xa", xa)):
                    bank, filled = take(kind, b, (use, r, 0))
                    for k in range(KD):
                        for c in range(2):
                            mm = pe.transpose(bank[:, k * HALF + c * T:k * HALF + (c + 1) * T],
                                              src[:, c, k * T:(k + 1) * T], ident[:])
                    mm.then_inc(filled, 1)

            def three(dst, w, act, first, last):
                pe.matmul(dst, w[0], act[0], start=first, stop=False, skip_group_check=True)
                pe.matmul(dst, w[0], act[1], start=False, stop=False, skip_group_check=True)
                return pe.matmul(dst, w[1], act[0], start=False, stop=last, skip_group_check=True)

            def conv(kind, b, r, h):
                emptied(kind, b, ("xa", r, 0))
                for j in range(2):
                    bank, filled = take(kind, b, (f"conv{j}", r, 0))
                    for m in range(2):
                        f = slice((2 * j + m) * T, (2 * j + m + 1) * T)
                        dst = bank[:, m * HALF:(m + 1) * HALF]
                        for k in range(KD):
                            three(dst, [w[:, k, f] for w in wc], [a[:, k, :] for a in xa_t[h]], m == 0 and k == 0, False)
                        mm = pe.matmul(dst, bias_rows[:, CB, f], ones_r[:], start=False, stop=True,
                                       skip_group_check=True)
                    mm.then_inc(filled, 1)

            def ffn_k(kind, b, r, n):
                pe.wait_ge(mix_ready, n + 1)
                bank, filled = take(kind, b, ("ffn_k", r, 0))
                for m in range(KD):
                    for k in range(KD):
                        mm = pe.matmul(bank[:, m * HALF:(m + 1) * HALF], fk[:, k, m * T:(m + 1) * T], mix_k[:, k, :],
                                       start=k == 0 and m == 0, stop=k == KD - 1, skip_group_check=True)
                mm.then_inc(filled, 1)

            def ffn_tokens(kind, b, r, use, act, w):
                bank, filled = take(kind, b, (use, r, 0))
                for c in range(2):
                    for k in range(KD):
                        mm = pe.matmul(bank[:, c * D:(c + 1) * D], act[:, k, c * T:(c + 1) * T], w[:, k, :],
                                       start=k == 0 and c == 0, stop=k == KD - 1, skip_group_check=True)
                mm.then_inc(filled, 1)

            def gates(kind, b, r, n):
                pe.wait_ge(xc_lo_ready, 2 * (n + 1))
                bank, filled = take(kind, b, ("gates", r, 0))
                for k in range(KP):
                    mm = three(bank[0:40, 0:HALF], [w[:, k, :] for w in wif], [a[:, k, :] for a in xc],
                               k == 0, k == KP - 1)
                mm.then_inc(filled, 1)

            def heads(kind, b, r, use, w, j):
                bank, filled = take(kind, b, (f"{use}{j}", r, 0))
                for m in range(2):
                    f = slice((2 * j + m) * T, (2 * j + m + 1) * T)
                    for k in range(KP):
                        mm = three(bank[:, m * HALF:(m + 1) * HALF], [p[:, k, f] for p in w],
                                   [a[:, k, :] for a in xc], m == 0 and k == 0, k == KP - 1)
                mm.then_inc(filled, 1)

            def cols(kind, b, r, n):
                pe.wait_ge(exp_rows_ready, 2 * n + 1)
                bank, filled = take(kind, b, ("cols", r, 0))
                settle(pe, pe_settled)
                for c in range(2):
                    mm = pe.transpose(bank[:, c * 40:(c + 1) * 40], rows_aw[:, c * T:(c + 1) * T], ident[0:40, 0:40])
                mm.then_inc(filled, 1)

            def tokens(kind, b, h, c, use, act, w, nk, bias):
                bank, filled = take(kind, b, (use, h, c))
                t = slice(c * T, (c + 1) * T)
                for k in range(nk):
                    lhs = [a[:, k, t] for a in act]
                    pe.matmul(bank, lhs[0], w[0][:, k, :], start=k == 0, stop=False)
                    pe.matmul(bank, lhs[0], w[1][:, k, :], start=False, stop=False)
                    mm = pe.matmul(bank, lhs[1], w[0][:, k, :], start=False, stop=k == nk - 1 and bias is None)
                if bias is not None:
                    mm = pe.matmul(bank, ones_r[:, 0:T], bias_rows[:, bias, :], start=False, stop=True)
                mm.then_inc(filled, 1)

            def maxima(b, h, c, n):
                pe.wait_ge(parts_ready, 2 * n + 1)
                for j in range(2):
                    pe.wait_ge(sc_emptied[j], sc_free(b, h, c, 0))
                    for i in range(4):
                        mm = pe.matmul(sc_ps[:, j, i * T:(i + 1) * T], sel_m[:, 2 * i + j, :],
                                       m_parts[:, c * T:(c + 1) * T], start=i == 0, stop=True, skip_group_check=True)
                    mm.then_inc(sc_filled[j], 1)

            def scores(b, h, c):
                t = slice(c * T, (c + 1) * T)
                for j in range(2):
                    pe.wait_ge(sc_emptied[j], sc_free(b, h, c, 1))
                for i in range(PAIRS):
                    for j in range(2):
                        p = slice(HD * j, HD * (j + 1))
                        mm = pe.matmul(sc_ps[:, j, i * T:(i + 1) * T], k_t[p, i, t], q_t[p, i, t],
                                       start=i == 0, stop=True, skip_group_check=True)
                        if i == PAIRS - 1:
                            mm.then_inc(sc_filled[j], 1)

            def decay(kind, b, h, c, n):
                pe.wait_ge(parts_ready, 2 * n + 2)
                bank, filled = take(kind, b, ("decay", h, c))
                for j in range(PAIRS):
                    mm = pe.matmul(bank[:, j * T:(j + 1) * T], sel_g[:, j, :], g_parts[:, c * T:(c + 1) * T],
                                   start=j == 0, stop=True, skip_group_check=True)
                mm.then_inc(filled, 1)

            def k_tokens(kind, b, h, c):
                bank, filled = take(kind, b, ("kt", h, c))
                for j in range(PAIRS):
                    mm = pe.transpose(bank[:, j * T:(j + 1) * T], k_t[:, j, c * T:(c + 1) * T], ident[:])
                mm.then_inc(filled, 1)

            def numerators(kind, b, h, c):
                t = tile_of(b, h, c)
                if h == 0 and c == 0:
                    pe.wait_ge(state_reset, b + 1)
                pe.wait_ge(num_emptied, t + 1)
                emptied(kind, b, ("decay", h, c))
                for j in range(PAIRS):
                    pe.matmul(num_ps[:, j // 2, j % 2 * PW:(j % 2 + 1) * PW], q_dec[:, j, :], state[:, j, :],
                              start=j % 2 == 0, stop=False, skip_group_check=True)
                emptied(kind, b, ("v", h, c))
                for i in range(2):
                    pe.wait_ge(sc_emptied[i], sc_free(b, h, c, 2))
                    for j in range(PAIRS):
                        hd = 2 * j + i
                        at = (HD + 1) + PW * hd - (HD + 1) * i
                        mm = pe.matmul(num_ps[:, j // 2, j % 2 * PW:(j % 2 + 1) * PW], dec[:, i, j, :],
                                       v_sb[:, at:at + PW], start=False, stop=i == 1, skip_group_check=True)
                mm.then_inc(num_filled, 1)

            def state_update(kind, b, h, c):
                emptied(kind, b, ("kt", h, c))
                for j in range(2):
                    for i in range(2):
                        pr = 2 * j + i
                        at = (HD + 1) + PW * 2 * pr
                        rhs = v_sb[:, at:at + 2 * PW].rearrange("p (s w) -> p s w", s=2)[:, :, 0:HD + 1]
                        mm = pe.matmul(sc_ps[:, j, i * PW:(i + 1) * PW], k_w[:, pr * T:(pr + 1) * T], rhs,
                                       start=i == 0, stop=True, skip_group_check=True)
                    mm.then_inc(sc_filled[j], 1)

            def gt_transposes(kind, b, h, c, n):
                pe.wait_ge(out_ready[c], n + 2)
                bank, filled = take(kind, b, ("gt", h, c))
                src = hid[c][:].rearrange("p h d -> p (h d)")
                for j in range(KP):
                    mm = pe.transpose(bank[:, j * T:(j + 1) * T], src[:, j * T:(j + 1) * T], ident[:])
                mm.then_inc(filled, 1)

            def down(kind, b, h, c):
                emptied(kind, b, ("gt", h, c))
                bank, filled = take(kind, b, ("down", h, c))
                for k in range(KP):
                    mm = pe.matmul(bank[:, 0:D], gt[:, k, :], wd[:, k, :], start=k == 0, stop=k == KP - 1)
                mm.then_inc(filled, 1)

            def ffn_v(kind, b, r, n):
                pe.wait_ge(kact_ready, n + 1)
                ffn_tokens(kind, b, r, "ffn_v", kact, fv)

            def half_end(kind, b, h, n):
                front = kind != "last" or h == 0
                ahead = (kind, b, h + 1)
                if front:
                    conv(*ahead, (h + 1) % 2)
                gt_transposes(kind, b, h, 0, n)
                if front:
                    ffn_k(*ahead, n + 1)
                down(kind, b, h, 0)
                if front:
                    ffn_tokens(*ahead, "ffn_r", mix_r, fr)
                    gates(*ahead, n + 1)
                    heads(*ahead, "q", wq, 0)
                    heads(*ahead, "q", wq, 1)
                    ffn_v(*ahead, n + 1)
                    heads(*ahead, "k", wk, 0)
                gt_transposes(kind, b, h, 1, n)
                if front:
                    heads(*ahead, "k", wk, 1)
                    cols(*ahead, n + 1)
                down(kind, b, h, 1)

            def first_front():
                first = ("first", 0, 0)
                transposes_x(*first, 0)
                conv(*first, 0)
                ffn_k(*first, 0)
                ffn_tokens(*first, "ffn_r", mix_r, fr)
                gates(*first, 0)
                heads(*first, "q", wq, 0)
                heads(*first, "q", wq, 1)
                ffn_v(*first, 0)
                heads(*first, "k", wk, 0)
                heads(*first, "k", wk, 1)
                cols(*first, 0)

            def body(b, last):
                kind = "last" if last else "body"
                for h in range(2):
                    n = b * 2 + h
                    front = not (last and h == 1)
                    for c in range(2):
                        tokens(kind, b, h, c, "o", xa_t[h], wo, KD, OB)
                        tokens(kind, b, h, c, "r", xa_t[h], wr, KD, RB)
                        maxima(b, h, c, n)
                        tokens(kind, b, h, c, "skip", xc, ws, KP, None)
                        decay(kind, b, h, c, n)
                        k_tokens(kind, b, h, c)
                        scores(b, h, c)
                        if c == 1 and front:
                            transposes_x(kind, b, h + 1, n + 1)
                        tokens(kind, b, h, c, "v", xa_t[h], wv, KD, None)
                        numerators(kind, b, h, c)
                        if not (h == 1 and c == 1):
                            state_update(kind, b, h, c)
                    half_end(kind, b, h, n)

            pe.wait_ge(buffers_ready, 1)
            first_front()
            with pe.Fori(0, B - 1) as b:
                body(b, False)
            body(B - 1, True)

        @block.scalar
        def _(act):
            def filled(kind, b, use):
                bank, before = ring_use(kind, b, use)
                act.wait_ge(ring_filled[bank], before + 1)
                return ring[:, bank, :], ring_emptied[bank]

            def front_x(kind, b, r, n, h):
                if kind != "first":
                    act.wait_ge(mix_ready, n)
                prev = zero2[:] if h == 0 else xf_t[:, :, HALF:HALF + 1]
                nc.scalar.activation(xf_t[:, :, 0:1], prev, ACT.Copy).then_inc(xf_t_carried, 1)
                bank, emptied = filled(kind, b, ("xf", r, 0))
                act.wait_ge(xf_t_carried, n + 1)
                nc.scalar.activation(xf_t[:, :, 1:1 + HALF], bank.rearrange("p (k t) -> p k t", k=KD),
                                     ACT.Copy).then_inc(emptied, 1)
                bank, _ = filled(kind, b, ("xa", r, 0))
                nc.scalar.activation(xa_t[h][0][:].rearrange("p k t -> p (k t)"), bank,
                                     ACT.Copy).then_inc(xa_hi_ready, 1)

            def front_conv(kind, b, r, n):
                for j in range(2):
                    bank, _ = filled(kind, b, (f"conv{j}", r, 0))
                    if kind != "first":
                        act.wait_ge(xc_lo_ready, 2 * n)
                    nc.scalar.activation(conv_act[j][:], bank, ACT.Tanh, scale=0.5).then_inc(conv_tanh_ready, 1)

            def front_conv_high(kind, b, r, n):
                for j in range(2):
                    bank, before = ring_use(kind, b, (f"conv{j}", r, 0))
                    act.wait_ge(ring_emptied[bank], before + 1)
                    nc.scalar.activation(xc[0][:, 2 * j:2 * j + 2, :].rearrange("p k t -> p (k t)"), conv_act[j][:],
                                         ACT.Copy).then_inc(xc_hi_ready, 1)

            def front_ffn(kind, b, r, n):
                if kind != "first":
                    act.wait_ge(base_ready, n)
                bank, emptied = filled(kind, b, ("ffn_k", r, 0))
                nc.scalar.activation(kact[:].rearrange("p k t -> p (k t)"), bank, ACT.Relu).then_inc(emptied, 1)
                bank, emptied = filled(kind, b, ("ffn_r", r, 0))
                nc.scalar.activation(ffn[:].rearrange("p c d -> p (c d)"), bank, ACT.Tanh,
                                     scale=0.5).then_inc(emptied, 1)

            def front_gates(kind, b, r, n):
                bank, emptied = filled(kind, b, ("gates", r, 0))
                nc.scalar.activation(row_i[:], bank[0:H, 0:HALF], ACT.Tanh, scale=1.0 / CAP,
                                     bias=if_bias[0:H, :])
                nc.scalar.activation(row_f[:], bank[32:32 + H, 0:HALF], ACT.Tanh, scale=1.0 / CAP,
                                     bias=if_bias[32:32 + H, :]).then_inc(emptied, 1)

            def front_exps(kind, b, r, n):
                act.wait_ge(exp_args_ready, n + 1)
                if kind != "first":
                    act.wait_ge(parts_ready, 2 * n)
                    act.wait_ge(cols_ready, n)
                nc.scalar.activation(rows_aw[32:32 + H, :], row_f[:], ACT.Exp).then_inc(exp_rows_ready, 1)
                nc.scalar.activation(row_g[:], row_i[:], ACT.Exp).then_inc(exp_rows_ready, 1)

            def front_q(kind, b, r, j):
                bank, emptied = filled(kind, b, (f"q{j}", r, 0))
                for m in range(2):
                    ins = nc.scalar.activation(q_t[:, 2 * j + m, :], bank[:, m * HALF:(m + 1) * HALF],
                                               ACT.Identity, bias=q_bias[:, 2 * j + m:2 * j + m + 1])
                ins.then_inc(emptied, 1)

            def front_rest(kind, b, r, n):
                front_gates(kind, b, r, n)
                front_q(kind, b, r, 0)
                front_exps(kind, b, r, n)
                front_q(kind, b, r, 1)

            def gt_copy(kind, b, h, c):
                bank, emptied = filled(kind, b, ("gt", h, c))
                nc.scalar.activation(gt[:].rearrange("p k t -> p (k t)"), bank, ACT.Copy).then_inc(emptied, 1)

            def tile(kind, b, h, c, n):
                bank, emptied = filled(kind, b, ("o", h, c))
                act.wait_ge(gated[c], n + 1)
                nc.scalar.activation(th_o[c][:], bank, ACT.Tanh, scale=0.5).then_inc(emptied, 1)
                bank, _ = filled(kind, b, ("r", h, c))
                act.wait_ge(out_ready[c], n + 1)
                nc.scalar.activation(sr[c][:], bank, ACT.Tanh, scale=0.5).then_inc(r_tanh_ready, 1)
                if c == 0:
                    act.wait_ge(cols_ready, n + 1)
                for j in range(2):
                    act.wait_ge(sc_filled[j], sc_use(b, h, c, 1))
                    for i in range(4):
                        hd = 2 * i + j
                        ins = nc.scalar.activation(dec[:, j, i, :], sc_ps[:, j, i * T:(i + 1) * T], ACT.Exp,
                                                   scale=-1.0, bias=cols_aw[:, c, hd:hd + 1])
                    ins.then_inc(sc_emptied[j], 1)

            def body(b, last):
                kind = "last" if last else "body"
                for h in range(2):
                    n = b * 2 + h
                    front = not (last and h == 1)
                    tile(kind, b, h, 0, n)
                    tile(kind, b, h, 1, n)
                    if front:
                        front_x(kind, b, h + 1, n + 1, (h + 1) % 2)
                        front_conv(kind, b, h + 1, n + 1)
                    gt_copy(kind, b, h, 0)
                    if front:
                        front_conv_high(kind, b, h + 1, n + 1)
                        front_ffn(kind, b, h + 1, n + 1)
                        front_rest(kind, b, h + 1, n + 1)
                    gt_copy(kind, b, h, 1)

            front_x("first", 0, 0, 0, 0)
            front_conv("first", 0, 0, 0)
            front_conv_high("first", 0, 0, 0)
            front_ffn("first", 0, 0, 0)
            front_rest("first", 0, 0, 0)
            with act.Fori(0, B - 1) as b:
                body(b, False)
            body(B - 1, True)

        @block.gpsimd
        def _(pool):
            FRONT_STEPS, TILE_STEPS = 7, 8

            def front_scale(kind, n):
                k = [0]

                def link(ins, settled=False):
                    k[0] += 1
                    ins.then_inc(pool_front_step, 1)
                    pool.wait_ge(pool_front_step, n * FRONT_STEPS + k[0])
                    if settled:
                        settle(pool, pool_settled)

                used = k
                pool.wait_ge(stats_ready, n + 1)
                settle(pool, pool_settled)
                var = ln_mv[:, :, 1]
                rstd, t, both, e = (ln_sc[:, i, :] for i in range(4))
                link(nc.gpsimd.tensor_scalar(t, var, EPS_OUTER, None, ALU.add))
                link(nc.gpsimd.tensor_tensor(rstd, t, minus_half[:, 0:2], ALU.pow))
                link(nc.gpsimd.tensor_tensor(t, rstd, rstd, ALU.mult))
                link(nc.gpsimd.tensor_tensor(t, t, var, ALU.mult), settled=True)
                link(nc.gpsimd.tensor_scalar(t, t, EPS_ATTN, None, ALU.add))
                link(nc.gpsimd.tensor_tensor(e, t, minus_half[:, 0:2], ALU.pow))
                nc.gpsimd.tensor_tensor(both, rstd, e, ALU.mult).then_inc(scale_ready, 1)
                return link, used

            def front_base(kind, n, h, link, used):
                pool.wait_ge(xh_ready, n + 1)
                nc.gpsimd.tensor_tensor(base[h][:], xin[:], xf[:], ALU.add).then_inc(x_used, 1)
                pool.wait_ge(x_used, n + 1)
                link(nc.gpsimd.tensor_tensor(base[h][:], base[h][:], bd_all[:].unsqueeze(1).to_broadcast([T, 2, D]),
                                             ALU.add))
                assert used[0] == FRONT_STEPS

            def front_mix(kind, b, r, n):
                bank, before = ring_use(kind, b, ("xf", r, 0))
                pool.wait_ge(ring_emptied[bank], before + 1)
                settle(pool, pool_settled)
                for i, dst in enumerate((mix_r, mix_k)):
                    for k in range(KD):
                        ins = nc.gpsimd.tensor_scalar(dst[:, k, :], xf_t[:, k, 0:HALF], one_mu[:, i, k:k + 1], 0.0,
                                                      ALU.mult, ALU.add)
                ins.then_inc(mix_prev_ready, 1)

            def front_kact(kind, b, r, n):
                bank, before = ring_use(kind, b, ("ffn_k", r, 0))
                pool.wait_ge(ring_emptied[bank], before + 1)
                nc.gpsimd.tensor_tensor(kact[:], kact[:], kact[:], ALU.mult).then_inc(kact_ready, 1)

            def front_add(kind, b, r, h):
                bank, before = ring_use(kind, b, ("ffn_v", r, 0))
                pool.wait_ge(ring_emptied[bank], before + 1)
                nc.gpsimd.tensor_tensor(base[h][:], base[h][:], ffn[:], ALU.add).then_inc(base_ready, 1)

            def mask(b, h, c):
                for j in range(2):
                    pool.wait_ge(sc_emptied[j], sc_free(b, h, c, 1))
                settle(pool, pool_settled)
                d = dec[:].rearrange("p j i t -> p (j i) t")
                nc.gpsimd.affine_select(out=d, in_=d, compare_op=ALU.is_ge, fill=0.0, base=0,
                                        pattern=[[0, H], [1, T]], channel_multiplier=-1).then_inc(masked, 1)

            def norm_scale(b, h, c):
                t = tile_of(b, h, c)
                k = [0]

                def link(ins, settled=False):
                    k[0] += 1
                    ins.then_inc(pool_tile_step, 1)
                    pool.wait_ge(pool_tile_step, t * TILE_STEPS + k[0])
                    if settled:
                        settle(pool, pool_settled)

                pool.wait_ge(mh_stats_ready, t + 1)
                s, d, q, mean, rstd, dd = (mh_sc[:, i, :] for i in range(6))
                mean_e, m2_e, mean_o, m2_o = (mh_st[:, :, i] for i in (1, 2, 4, 5))
                nc.gpsimd.tensor_tensor(s, mean_e, mean_o, ALU.add)
                nc.gpsimd.tensor_tensor(q, m2_e, m2_o, ALU.add)
                link(nc.gpsimd.tensor_tensor(d, mean_e, mean_o, ALU.subtract), settled=True)
                nc.gpsimd.tensor_scalar(mean, s, 0.5, 0.0, ALU.mult, ALU.add)
                nc.gpsimd.tensor_scalar(q, q, 1.0 / HD, 4.0 * EPS_ATTN, ALU.mult, ALU.add)
                link(nc.gpsimd.tensor_tensor(dd, d, d, ALU.mult), settled=True)
                link(nc.gpsimd.tensor_scalar(dd, dd, 0.25, 0.0, ALU.mult, ALU.add))
                link(nc.gpsimd.tensor_tensor(q, q, dd, ALU.add))
                link(nc.gpsimd.tensor_tensor(rstd, q, minus_half[:], ALU.pow))
                return link, k, mean, rstd

            def norm(c, link, k, mean, rstd):
                bc = [T, H, HD]
                link(nc.gpsimd.tensor_tensor(hid[c][:], hid[c][:], mean.unsqueeze(2).to_broadcast(bc), ALU.subtract))
                link(nc.gpsimd.tensor_tensor(hid[c][:], hid[c][:], rstd.unsqueeze(2).to_broadcast(bc), ALU.mult))
                flat = hid[c][:].rearrange("p h d -> p (h d)")
                link(nc.gpsimd.tensor_tensor(flat, flat, mhg_all[:], ALU.mult))
                nc.gpsimd.tensor_tensor(flat, flat, sk[c][:], ALU.add).then_inc(normed, 1)
                assert k[0] == TILE_STEPS

            def front_first():
                link, used = front_scale("first", 0)
                front_base("first", 0, 0, link, used)
                front_mix("first", 0, 0, 0)
                front_kact("first", 0, 0, 0)
                front_add("first", 0, 0, 0)

            def body(b, last):
                kind = "last" if last else "body"
                for h in range(2):
                    n = b * 2 + h
                    front = not (last and h == 1)
                    mask(b, h, 0)
                    if front:
                        link, used = front_scale(kind, n + 1)
                    scaled = norm_scale(b, h, 0)
                    mask(b, h, 1)
                    norm(0, *scaled)
                    if front:
                        front_base(kind, n + 1, (h + 1) % 2, link, used)
                        front_mix(kind, b, h + 1, n + 1)
                    norm(1, *norm_scale(b, h, 1))
                    if front:
                        front_kact(kind, b, h + 1, n + 1)
                        front_add(kind, b, h + 1, (h + 1) % 2)

            front_first()
            with pool.Fori(0, B - 1) as b:
                body(b, False)
            body(B - 1, True)

        @block.vector
        def _(dve):
            FRONT_STEPS, TILE_STEPS = 11, 2

            def filled(kind, b, use):
                bank, before = ring_use(kind, b, use)
                dve.wait_ge(ring_filled[bank], before + 1)
                return ring[:, bank, :], ring_emptied[bank]

            def front_link(n, used):
                def link(ins, settled=False):
                    used[0] += 1
                    ins.then_inc(dve_front_step, 1)
                    dve.wait_ge(dve_front_step, n * FRONT_STEPS + used[0])
                    if settled:
                        settle(dve, dve_settled)
                return link

            def x_stats(n, link):
                dve.wait_ge(x_loaded, 16 * n + 16)
                nc.vector.bn_stats(ln_st[:, 0, :], xin[:, 0, :])
                link(nc.vector.bn_stats(ln_st[:, 1, :], xin[:, 1, :]), settled=True)
                nc.vector.bn_aggr(ln_mv[:, 0, :], ln_st[:, 0, :])
                nc.vector.bn_aggr(ln_mv[:, 1, :], ln_st[:, 1, :]).then_inc(stats_ready, 1)

            def x_normalise(kind, n):
                dve.wait_ge(scale_ready, n + 1)
                if kind != "first":
                    dve.wait_ge(x_used, n)
                for c in range(2):
                    for dst, k in ((xf, 0), (xa, 2)):
                        ins = nc.vector.tensor_scalar(dst[:, c, :], xin[:, c, :], ln_mv[:, c, 0:1],
                                                      ln_sc[:, k, c:c + 1], ALU.subtract, ALU.mult)
                ins.then_inc(xh_ready, 1)

            def x_low(kind, b, r, n, h):
                bank, emptied = filled(kind, b, ("xa", r, 0))
                dve.wait_ge(xa_hi_ready, n + 1)
                hi, lo = (a[:].rearrange("p k t -> p (k t)") for a in xa_t[h])
                nc.vector.tensor_tensor(lo, bank, hi.bitcast(F32), ALU.subtract).then_inc(emptied, 1)

            def mix(n):
                dve.wait_ge(mix_prev_ready, n + 1)
                for i, dst in enumerate((mix_r, mix_k)):
                    for k in range(KD):
                        ins = nc.vector.scalar_tensor_tensor(out=dst[:, k, :], in0=xf_t[:, k, 1:1 + HALF],
                                                             scalar=mu[:, i, k:k + 1], in1=dst[:, k, :],
                                                             op0=ALU.mult, op1=ALU.add)
                ins.then_inc(mix_ready, 1)

            def conv_silu(kind, b, r, n):
                for j in range(2):
                    bank, emptied = filled(kind, b, (f"conv{j}", r, 0))
                    dve.wait_ge(conv_tanh_ready, 2 * n + j + 1)
                    nc.vector.scalar_tensor_tensor(out=conv_act[j][:], in0=conv_act[j][:], scalar=1.0, in1=bank,
                                                   op0=ALU.add, op1=ALU.mult).then_inc(emptied, 1)
                for j in range(2):
                    dve.wait_ge(xc_hi_ready, 2 * n + j + 1)
                    hi, lo = (a[:, 2 * j:2 * j + 2, :].rearrange("p k t -> p (k t)") for a in xc)
                    nc.vector.tensor_tensor(lo, conv_act[j][:], hi.bitcast(F32), ALU.subtract).then_inc(xc_lo_ready, 1)

            def gate_rows(kind, b, r, n, h, link):
                bank, before = ring_use(kind, b, ("gates", r, 0))
                dve.wait_ge(ring_emptied[bank], before + 1)
                nc.vector.tensor_scalar(row_i[:], row_i[:], CAP, None, ALU.mult)
                link(nc.vector.tensor_scalar(row_f[:], row_f[:], CAP, None, ALU.mult))
                if h == 1:
                    nc.vector.tensor_copy(row_m[1][:, 0:1], row_m[0][:, HALF:HALF + 1])
                link(nc.vector.tensor_tensor_scan(out=row_F[:], data0=chunk_keep[:], data1=row_f[:], initial=0.0,
                                                  op0=ALU.mult, op1=ALU.add))
                link(nc.vector.tensor_tensor_scan(out=row_m[h][:, 1:], data0=row_f[:], data1=row_i[:],
                                                  initial=row_m[h][:, 0:1], op0=ALU.add, op1=ALU.max))
                nc.vector.tensor_tensor(rows_aw[0:H, :], row_i[:], row_F[:], ALU.subtract)
                link(nc.vector.tensor_tensor(row_M[:], row_m[h][:, 1:], row_F[:], ALU.subtract))

                def chunks(a):
                    return a.rearrange("h (c t) -> h c t", c=2)

                def each_chunk(a):
                    return a.unsqueeze(2).to_broadcast([H, 2, T])

                nc.vector.tensor_tensor(chunks(row_f[:]), chunks(rows_aw[0:H, :]),
                                        each_chunk(row_M[:, T - 1:HALF:T]), ALU.subtract)
                nc.vector.tensor_tensor(chunks(row_i[:]), each_chunk(row_m[h][:, 0:HALF:T]), chunks(row_M[:]),
                                        ALU.subtract).then_inc(exp_args_ready, 1)

            def parts(dst, src, link):
                link(nc.vector.tensor_copy(dst[0:H, :], src))
                link(nc.vector.tensor_tensor(row_rem[:], src, dst[0:H, :], ALU.subtract))
                link(nc.vector.tensor_copy(row_mid[:], row_rem[:]))
                nc.vector.tensor_copy(dst[32:32 + H, :], row_mid[:])
                nc.vector.tensor_tensor(dst[64:64 + H, :], row_rem[:], row_mid[:], ALU.subtract).then_inc(parts_ready, 1)

            def ffn_gate(kind, b, r):
                rbank, before = ring_use(kind, b, ("ffn_r", r, 0))
                dve.wait_ge(ring_emptied[rbank], before + 1)
                bank, emptied = filled(kind, b, ("ffn_v", r, 0))
                f = ffn[:].rearrange("p c d -> p (c d)")
                nc.vector.scalar_tensor_tensor(out=f, in0=f, scalar=1.0, in1=bank, op0=ALU.add,
                                               op1=ALU.mult).then_inc(emptied, 1)

            def k_copy(kind, b, r, j):
                bank, emptied = filled(kind, b, (f"k{j}", r, 0))
                for m in range(2):
                    ins = nc.vector.tensor_scalar(k_t[:, 2 * j + m, :], bank[:, m * HALF:(m + 1) * HALF],
                                                  k_bias[:, 2 * j + m:2 * j + m + 1], None, ALU.add)
                ins.then_inc(emptied, 1)

            def cols_copy(kind, b, r, n):
                bank, emptied = filled(kind, b, ("cols", r, 0))
                nc.vector.tensor_copy(cols_aw[:, 0, :], bank[:, 0:40]).then_inc(cols_ready, 1)
                nc.vector.tensor_copy(cols_aw[:, 1, :], bank[:, 40:80]).then_inc(emptied, 1)

            def reset_state(b):
                nc.vector.memset(state[:], 0.0).then_inc(state_cleared, 1)
                dve.wait_ge(state_cleared, b + 1)
                nc.vector.memset(state[0:HD, :, HD:HD + 1], 1.0)
                nc.vector.memset(state[HD:T, :, PW - 1:PW], 1.0).then_inc(state_reset, 1)

            def silu_r(kind, b, h, c):
                bank, emptied = filled(kind, b, ("r", h, c))
                dve.wait_ge(r_tanh_ready, tile_of(b, h, c) + 1)
                nc.vector.scalar_tensor_tensor(out=sr[c][:], in0=sr[c][:], scalar=1.0, in1=bank, op0=ALU.add,
                                               op1=ALU.mult).then_inc(emptied, 1)

            def skip(kind, b, h, c):
                bank, emptied = filled(kind, b, ("skip", h, c))
                nc.vector.tensor_tensor(sk[c][:], bank, bs_all[:], ALU.add).then_inc(emptied, 1)

            def q_decayed(kind, b, h, c):
                bank, emptied = filled(kind, b, ("decay", h, c))
                d = bank.rearrange("p (j t) -> p j t", j=PAIRS)
                nc.vector.tensor_copy(carry[:], d[:, :, T - 1])
                nc.vector.tensor_tensor(q_dec[:], q_t[:, :, c * T:(c + 1) * T], d, ALU.mult).then_inc(emptied, 1)

            def k_weighted(kind, b, h, c):
                bank, emptied = filled(kind, b, ("kt", h, c))
                if c == 0:
                    dve.wait_ge(cols_ready, b * 2 + (h + 1))
                nc.vector.tensor_tensor(k_w[:].rearrange("p (h e) -> p h e", h=H),
                                        bank.rearrange("p (h e) -> p h e", h=H),
                                        cols_aw[:, c, 32:32 + H].unsqueeze(2).to_broadcast([T, H, HD]),
                                        ALU.mult).then_inc(emptied, 1)

            def weigh_scores(b, h, c):
                dve.wait_ge(masked, tile_of(b, h, c) + 1)
                for j in range(2):
                    dve.wait_ge(sc_filled[j], sc_use(b, h, c, 2))
                    nc.vector.tensor_tensor(dec[:, j], sc_ps[:, j, :].rearrange("p (i t) -> p i t", i=PAIRS),
                                            dec[:, j], ALU.mult).then_inc(sc_emptied[j], 1)

            def v_copy(kind, b, h, c):
                bank, emptied = filled(kind, b, ("v", h, c))
                dst = v_sb[:, HD + 1:].rearrange("p (h w) -> p h w", h=H)[:, :, 0:HD]
                nc.vector.tensor_tensor(dst, bank.rearrange("p (h d) -> p h d", h=H),
                                        bv_all[:].rearrange("p (h d) -> p h d", h=H), ALU.add).then_inc(emptied, 1)

            def divide_and_gate(kind, b, h, c):
                t = tile_of(b, h, c)
                used = [0]

                def link(ins):
                    used[0] += 1
                    ins.then_inc(dve_tile_step, 1)
                    dve.wait_ge(dve_tile_step, t * TILE_STEPS + used[0])

                dve.wait_ge(num_filled, t + 1)
                num = num_ps[:, :, 0:4 * (HD + 1)].rearrange("p j (i w) -> p j i w", i=4)
                link(nc.vector.tensor_scalar(den[:], num[:, :, :, HD], 1.0, None, ALU.max))
                link(nc.vector.reciprocal(den[:], den[:]))
                assert used[0] == TILE_STEPS
                nc.vector.tensor_tensor(hid[c][:].rearrange("p (j i) d -> p j i d", j=2), num[:, :, :, 0:HD],
                                        den[:].unsqueeze(3).to_broadcast([T, 2, 4, HD]),
                                        ALU.mult).then_inc(num_emptied, 1)
                dve.wait_ge(num_emptied, t + 2)
                obank, before = ring_use(kind, b, ("o", h, c))
                dve.wait_ge(ring_emptied[obank], before + 1)
                flat = hid[c][:].rearrange("p h d -> p (h d)")
                nc.vector.scalar_tensor_tensor(out=flat, in0=th_o[c][:], scalar=1.0, in1=flat, op0=ALU.add,
                                               op1=ALU.mult).then_inc(gated[c], 1)

            def update_state(b, h, c):
                for j in range(2):
                    dve.wait_ge(sc_filled[j], sc_use(b, h, c, 3))
                    for i in range(2):
                        pr = 2 * j + i
                        for s in range(2):
                            p = slice(s * HD, (s + 1) * HD)
                            w = slice(s * (HD + 1), (s + 1) * (HD + 1))
                            ins = nc.vector.scalar_tensor_tensor(
                                out=state[p, pr, w], in0=state[p, pr, w], scalar=carry[p, pr:pr + 1],
                                in1=sc_ps[p, j, i * PW + s * (HD + 1):i * PW + (s + 1) * (HD + 1)],
                                op0=ALU.mult, op1=ALU.add)
                    ins.then_inc(sc_emptied[j], 1)

            def head_stats(b, h, c):
                dve.wait_ge(gated[c], b * 2 + (h + 2))
                for i in range(H):
                    ins = nc.vector.bn_stats(mh_st[:, i, :], hid[c][:, i, :])
                ins.then_inc(mh_stats_ready, 1)

            def gate_out(b, h, c):
                dve.wait_ge(normed, tile_of(b, h, c) + 1)
                flat = hid[c][:].rearrange("p h d -> p (h d)")
                nc.vector.tensor_tensor(flat, flat, sr[c][:], ALU.mult).then_inc(out_ready[c], 1)

            def result(kind, b, h, c):
                bank, emptied = filled(kind, b, ("down", h, c))
                dve.wait_ge(base_ready, b * 2 + (h + 1))
                dve.wait_ge(out_stored[c], b * 32 + 16 * (h + 1))
                nc.vector.tensor_tensor(res[c][:], bank[:, 0:D], base[h][:, c, :], ALU.add).then_inc(emptied, 1)

            def front_gates(kind, b, r, n, h, link):
                gate_rows(kind, b, r, n, h, link)
                parts(m_parts, row_M[:], link)
                dve.wait_ge(exp_rows_ready, 2 * n + 2)
                parts(g_parts, row_g[:], link)

            def front_end(kind, b, r, n):
                ffn_gate(kind, b, r)
                k_copy(kind, b, r, 0)
                k_copy(kind, b, r, 1)
                cols_copy(kind, b, r, n)

            def body(b, last):
                kind = "last" if last else "body"
                reset_state(b)
                for h in range(2):
                    n = b * 2 + h
                    front = not (last and h == 1)
                    h2 = (h + 1) % 2
                    used = [0]
                    link = front_link(n + 1, used)
                    if front:
                        x_stats(n + 1, link)
                    for c in range(2):
                        silu_r(kind, b, h, c)
                        skip(kind, b, h, c)
                        if c == 1 and front:
                            x_normalise(kind, n + 1)
                        q_decayed(kind, b, h, c)
                        k_weighted(kind, b, h, c)
                        weigh_scores(b, h, c)
                        if c == 1 and front:
                            x_low(kind, b, h + 1, n + 1, h2)
                        v_copy(kind, b, h, c)
                        if c == 1:
                            gate_out(b, h, 0)
                        divide_and_gate(kind, b, h, c)
                        head_stats(b, h, c)
                        if c == 1 and front:
                            mix(n + 1)
                            conv_silu(kind, b, h + 1, n + 1)
                        if not (h == 1 and c == 1):
                            update_state(b, h, c)
                    result(kind, b, h, 0)
                    if front:
                        front_gates(kind, b, h + 1, n + 1, h2, link)
                    gate_out(b, h, 1)
                    if front:
                        front_end(kind, b, h + 1, n + 1)
                        assert used[0] == FRONT_STEPS, used
                    result(kind, b, h, 1)

            nc.vector.memset(rows_aw[:], 0.0)
            nc.vector.memset(m_parts[:], 0.0)
            nc.vector.memset(g_parts[:], 0.0)
            nc.vector.memset(row_m[0][:, 0:1], 0.0)
            nc.vector.memset(v_sb[:], 0.0).then_inc(buffers_cleared, 1)
            dve.wait_ge(buffers_cleared, 1)
            nc.vector.memset(v_sb[:, HD + 1:].rearrange("p (h w) -> p h w", h=H)[:, :, HD:HD + 1],
                             1.0).then_inc(buffers_ready, 1)
            for c in range(2):
                dve.sem_inc(sc_emptied[c], 1)
                dve.sem_inc(gated[c], 1)
                dve.sem_inc(out_ready[c], 1)
                dve.sem_inc(out_stored[c], 16)
            dve.sem_inc(num_emptied, 1)
            used = [0]
            link = front_link(0, used)
            x_stats(0, link)
            x_normalise("first", 0)
            x_low("first", 0, 0, 0, 0)
            mix(0)
            conv_silu("first", 0, 0, 0)
            front_gates("first", 0, 0, 0, 0, link)
            front_end("first", 0, 0, 0)
            with dve.Fori(0, B - 1) as b:
                body(b, False)
            body(B - 1, True)


_INS = ["L0_attn_x", "L0_attn_ln_g", "L0_attn_ln_b", "L0_attn_mh_g", "L0_attn_mh_b", "L0_attn_W_up_l",
        "L0_attn_b_up_l", "L0_attn_W_up_r", "L0_attn_b_up_r", "L0_attn_W_down", "L0_attn_b_down",
        "L0_attn_conv_w", "L0_attn_conv_b", "L0_attn_W_skip", "L0_attn_b_skip", "L0_attn_W_i", "L0_attn_b_i",
        "L0_attn_W_f", "L0_attn_b_f", "L0_attn_W_o", "L0_attn_b_o", "L0_attn_W_q", "L0_attn_b_q",
        "L0_attn_W_k", "L0_attn_b_k", "L0_attn_W_v", "L0_attn_b_v", "L0_ffn_W_r", "L0_ffn_W_k", "L0_ffn_W_v",
        "L0_ffn_mu_r", "L0_ffn_mu_k"]


def kernel(**inputs):
    import numpy as _np
    import concourse.bacc as _bacc
    from concourse import mybir as _mybir
    from concourse.bass_utils import run_bass_kernel_spmd as _run

    nc = _bacc.Bacc("TRN2", target_bir_lowering=False, num_devices=1)
    arrays, args = {}, []
    for name in _INS:
        a = _np.ascontiguousarray(inputs[name])
        arrays[f"in_{name}_dram"] = a
        args.append(nc.dram_tensor(f"in_{name}_dram", a.shape, _mybir.dt.from_np(a.dtype), kind="ExternalInput").ap())
    out = nc.dram_tensor("out_0_dram", arrays["in_L0_attn_x_dram"].shape, _mybir.dt.float32,
                         kind="ExternalOutput").ap()
    mlstm_rwkv_block(nc, *args, out)
    r = _run(nc, [arrays], core_ids=[0])
    return r.results[0]["out_0_dram"]
```

```python
from contextlib import ExitStack

import concourse.bass as bass
from concourse import mybir

F32 = mybir.dt.float32
F32R = mybir.dt.float32r
BF16 = mybir.dt.bfloat16
ALU = mybir.AluOpType
ACT = mybir.ActivationFunctionType

EPS_OUTER = 1e-5
EPS_ATTN = 1e-6
CAP = 15.0
TAPS = 4

RING = 4
FRONT = ["conv0", "conv1", "ffn_k", "ffn_r", "gates", "q0", "q1", "k0", "ffn_v", "k1", "cols"]
HALF_END = [("gt", 0), None, None, None, ("down", 0), None, None, None, None, None, None, ("gt", 1), None, None,
            ("down", 1)]


def ring_order(kind):
    if kind == "first":
        return [(p, 0, 0) for p in ["xf", "xa"] + FRONT]
    out = []
    for h in range(2):
        front = kind == "body" or h == 0
        out += [(p, h, 0) for p in ("o", "r", "skip", "decay", "kt", "v")]
        out += [(p, h, 1) for p in ("o", "r", "skip", "decay", "kt")]
        out += [(p, h + 1, 0) for p in ("xf", "xa")] if front else []
        out += [("v", h, 1)]
        ahead = iter(FRONT)
        for end in HALF_END:
            if end:
                out += [(end[0], h, end[1])]
            elif front:
                out += [(next(ahead), h + 1, 0)]
    return out


def ring_places(kind):
    at, out = [0] * RING, {}
    for i, use in enumerate(ring_order(kind)):
        out[use] = (i % RING, at[i % RING])
        at[i % RING] += 1
    return out, at


FIRST_PLACES, FIRST_USES = ring_places("first")
BODY_PLACES, BODY_USES = ring_places("body")
LAST_PLACES, _ = ring_places("last")


def ring_use(kind, b, use):
    if kind == "first":
        return FIRST_PLACES[use]
    bank, before = (BODY_PLACES if kind == "body" else LAST_PLACES)[use]
    return bank, b * BODY_USES[bank] + (FIRST_USES[bank] + before)


def mlstm_rwkv_block(nc, x, ln_g, ln_b, mh_g, mh_b, W_up_l, b_up_l, W_up_r, b_up_r, W_down, b_down,
                     conv_w, conv_b, W_skip, b_skip, W_i, b_i, W_f, b_f, W_o, b_o, W_q, b_q, W_k, b_k,
                     W_v, b_v, F_r, F_k, F_v, mu_r, mu_k, out):
    B, S, D = x.shape
    P = W_up_l.shape[0]
    H, HD = mh_g.shape
    HID = H * HD
    T = 128
    KD, KP = D // T, P // T
    HALF = 2 * T
    HALVES = S // HALF
    PAIRS = H // 2
    PW = 2 * (HD + 1)
    assert HALVES == 2 and D == 256 and P == 512 and HID == 512 and HD == 64 and H == 8

    x_dram = x.rearrange("b (h c p) d -> (b h) p c d", c=2, p=T)
    out_dram = out.rearrange("b (t p) d -> (b t) p d", p=T)

    keep = ExitStack()
    with keep:
        def sb(name, shape, dt=F32, stack=keep):
            return stack.enter_context(nc.sbuf_tensor(name, shape, dt))

        def sem(name):
            return keep.enter_context(nc.semaphore(name))

        ring = keep.enter_context(nc.psum_tensor("ring", [T, RING, 512], F32))
        sc_ps = keep.enter_context(nc.psum_tensor("sc_ps", [T, 2, 512], F32))
        num_ps = keep.enter_context(nc.psum_tensor("num_ps", [T, 2, 512], F32))

        def halves(name, shape):
            return sb(name + "_hi", shape, F32R), sb(name + "_lo", shape, F32R)

        wc = halves("wc", [T, KD, P])
        wv = halves("wv", [T, KD, HID])
        wo = halves("wo", [T, KD, HID])
        wr = halves("wr", [T, KD, HID])
        wq = halves("wq", [T, KP, HID])
        wk = halves("wk", [T, KP, HID])
        ws = halves("ws", [T, KP, HID])
        wif = halves("wif", [T, KP, 40])
        wd = halves("wd", [T, KP, D])
        fr = halves("fr", [T, KD, D])
        fk = halves("fk", [T, KD, D])
        fv = halves("fv", [T, KD, D])

        ident = sb("ident", [T, T])
        sel = sb("sel", [72, H * T], BF16)
        ones_r = sb("ones_r", [T, HALF], F32R)
        bias_rows = sb("bias_rows", [T, 512], F32R)
        bv_all = sb("bv_all", [T, HID])
        bs_all = sb("bs_all", [T, HID])
        mhg_all = sb("mhg_all", [T, HID])
        bd_all = sb("bd_all", [T, D])
        q_bias = sb("q_bias", [T, KP])
        k_bias = sb("k_bias", [T, KP])
        if_bias = sb("if_bias", [40, 1])
        mu = sb("mu", [T, 2, KD])
        one_mu = sb("one_mu", [T, 2, KD])
        chunk_keep = sb("chunk_keep", [H, HALF])
        zero2 = sb("zero2", [T, KD, 1])
        minus_half = sb("minus_half", [T, H])
        CB, OB, RB = (slice(32 * i, 32 * (i + 1)) for i in range(3))
        xin = sb("xin", [T, 2, D])

        small_loaded = sem("small_loaded")
        rows_loaded = sem("rows_loaded")
        up_bias_loaded = sem("up_bias_loaded")
        ln_b_ready = sem("ln_b_ready")
        pool_prep = sem("pool_prep")
        conv_bias_ready = sem("conv_bias_ready")
        x_loaded = sem("x_loaded")
        const_ready = sem("const_ready")
        dve_prep = sem("dve_prep")
        prep_filled = sem("prep_filled")
        prep_hi = sem("prep_hi")
        prep_act = sem("prep_act")
        prep_dve = sem("prep_dve")

        prep = ExitStack()
        with prep:
            def tmp(name, shape, dt=F32):
                return sb(name, shape, dt, prep)

            ul = tmp("ul", [T, KP, D])
            SLOTS = 5
            stage = tmp("stage", [T, SLOTS, KP * P])
            wt = tmp("wt", [T, KP, HID])
            wt2 = tmp("wt2", [T, KP, HID])
            ult = tmp("ult", [T, KD, 3 + P])
            bl = tmp("bl", [T, 3 + P])
            bl_t = tmp("bl_t", [T, KP, T])
            lnb_rep = tmp("lnb_rep", [T, KD, T])
            lng = tmp("lng", [T, KD])
            lnb = tmp("lnb", [T, KD])
            cw = tmp("cw", [T, TAPS])
            cb = tmp("cb", [T, 1])
            fold = tmp("fold", [T, P])
            tap = tmp("tap", [T, P])
            bias_sum = tmp("bias_sum", [T, P])
            row = tmp("row", [2, P])
            row_hi = tmp("row_hi", [2, P], F32R)
            bup_l_all = tmp("bup_l_all", [T, P])
            b0_all = tmp("b0_all", [T, 3, HID])
            mhb_all = tmp("mhb_all", [T, HID])

            def wt_turns(w, ks, last="split"):
                return [("wt_" + w, k, last) for k in ks]

            TURNS = [("ult", 0, "dve"), ("ult", 1, "dve")]
            TURNS += wt_turns("q", range(KP)) + wt_turns("k", range(KP)) + [("bl", 0, "dve")]
            TURNS += wt_turns("v", range(KP), "act") + [("bl_t", 0, "dve")] + wt_turns("o", range(KP), "act")
            TURNS += [("fold_v", 0, "split")] + wt_turns("s", [0]) + [("fold_v", 1, "split")] + wt_turns("s", [1])
            TURNS += [("bias_v", 0, "dve")] + wt_turns("s", [2]) + [("fold_o", 0, "split")] + wt_turns("s", [3])
            TURNS += [("fold_o", 1, "split")] + wt_turns("r", [0]) + [("bias_o", 0, "dve")] + wt_turns("r", [1])
            TURNS += wt_turns("if", [0]) + [("bias_r", 0, "dve")] + wt_turns("d", [0, 1])
            TURNS += wt_turns("fr", [0]) + wt_turns("fk", [0]) + wt_turns("fv", [0])

            act_count, dve_count, hi_count = [], [], []
            a = d = hi = 0
            for _, _, last in TURNS:
                a += last == "act"
                d += last in ("dve", "split")
                hi += last == "split"
                act_count.append(a)
                dve_count.append(d)
                hi_count.append(hi)

            def turn_of(what, which=0):
                return next(i for i, t in enumerate(TURNS) if t[:2] == (what, which))

            def wait_emptied(eng, i):
                if TURNS[i][2] == "act":
                    eng.wait_ge(prep_act, act_count[i])
                else:
                    eng.wait_ge(prep_dve, dve_count[i])

            STAGED = ["q", "k", "v", "o", "s", "r", "if", "d", "fr", "fk", "fv"]
            SOURCE = {"v": W_v, "o": W_o, "r": W_up_r, "q": W_q, "k": W_k, "s": W_skip, "d": W_down,
                      "fr": F_r, "fk": F_k, "fv": F_v}
            LAST_TURN = {"v": ("wt_v", 3), "o": ("wt_o", 3), "r": ("wt_r", 1), "q": ("wt_q", 3),
                         "k": ("wt_k", 3), "s": ("wt_s", 3), "if": ("wt_if", 0), "d": ("wt_d", 1),
                         "fr": ("wt_fr", 0), "fk": ("wt_fk", 0), "fv": ("wt_fv", 0)}
            def staged(name):
                slot = stage[:, STAGED.index(name) % SLOTS, :]
                if name == "if":
                    return slot[0:40, 0:P]
                o, i = SOURCE[name].shape
                return slot[:, 0:o // T * i].rearrange("p (o i) -> p o i", i=i)

            ul_loaded = sem("ul_loaded")
            stage_loaded = {name: sem("stage_loaded_" + name) for name in STAGED}

            def split_source(what, bank):
                return bank[:, 0:KP * 40] if what == "wt_if" else bank

            def split_target(what, k, part):
                if what == "fold_v":
                    return wv[part][:, k, :], lng[:, k:k + 1]
                if what == "fold_o":
                    return wo[part][:, k, :], lng[:, k:k + 1]
                if what == "wt_r":
                    return wr[part][:, k, :], lng[:, k:k + 1]
                if what == "wt_if":
                    return wif[part][:].rearrange("p k o -> p (k o)"), 0.5
                if what == "wt_d":
                    return wd[part][:, 2 * k:2 * k + 2, :].rearrange("p k o -> p (k o)"), 0.5
                if what in ("wt_fr", "wt_fk", "wt_fv"):
                    w, scale = {"wt_fr": (fr, 1.0), "wt_fk": (fk, 1.0), "wt_fv": (fv, 0.5)}[what]
                    return w[part][:].rearrange("p k o -> p (k o)"), scale
                w, scale = {"wt_q": (wq, 0.5), "wt_k": (wk, 0.5 / HD ** 0.5), "wt_s": (ws, 0.5)}[what]
                return w[part][:, k, :], scale

            block = prep.enter_context(nc.Block())

            @block.sync
            def _(sp):
                def rows(v):
                    return v.partition_broadcast(T)

                sp.dma_start(ul[:], W_up_l.rearrange("(o p) i -> p o i", p=T)).then_inc(ul_loaded, 16)
                for k, name in enumerate(STAGED):
                    if name == "k":
                        sp.wait_ge(small_loaded, 160)
                    if name == "v":
                        sp.dma_start(bup_l_all[:], rows(b_up_l)).then_inc(up_bias_loaded, 16)
                    if k == SLOTS:
                        for dst, src in ((b0_all[:, 0, :], b_v), (b0_all[:, 1, :], b_o), (b0_all[:, 2, :], b_up_r),
                                         (bs_all[:], b_skip), (mhb_all[:], mh_b.rearrange("h d -> (h d)")),
                                         (mhg_all[:], mh_g.rearrange("h d -> (h d)")), (bd_all[:], b_down)):
                            sp.dma_start(dst, rows(src)).then_inc(rows_loaded, 16)
                        sp.dma_start(xin[:], x_dram[0]).then_inc(x_loaded, 16)
                    if k >= SLOTS:
                        i = turn_of(*LAST_TURN[STAGED[k - SLOTS]])
                        sp.wait_ge(prep_filled, i + 1)
                    if name == "if":
                        sp.dma_start(staged(name)[0:H, :], W_i).then_inc(stage_loaded[name], 16)
                        sp.dma_start(staged(name)[32:32 + H, :], W_f).then_inc(stage_loaded[name], 16)
                    else:
                        sp.dma_start(staged(name), SOURCE[name].rearrange("(o p) i -> p o i", p=T)
                                     ).then_inc(stage_loaded[name], 16)

            @block.gpsimd
            def _(pool):
                nc.gpsimd.memset(ident[:], 0.0).then_inc(const_ready, 1)
                nc.gpsimd.memset(sel[:], 0.0).then_inc(const_ready, 1)
                pool.wait_ge(const_ready, 2)
                nc.gpsimd.affine_select(out=ident[:], in_=ident[:], compare_op=ALU.not_equal, fill=1.0, base=0,
                                        pattern=[[-1, T]], channel_multiplier=1).then_inc(const_ready, 1)
                for part in range(3):
                    nc.gpsimd.affine_select(out=sel[:], in_=sel[:], compare_op=ALU.not_equal, fill=1.0,
                                            base=-32 * part, pattern=[[-1, H], [0, T]],
                                            channel_multiplier=1).then_inc(const_ready, 1)
                    pool.wait_ge(const_ready, 4 + part)

                steps = [0]

                def link(ins):
                    steps[0] += 1
                    ins.then_inc(pool_prep, 1)
                    pool.wait_ge(pool_prep, steps[0])

                def convolve(src):
                    link(nc.gpsimd.tensor_scalar(fold[:], src[:, 0:P], cw[:, 0:1], 0.0, ALU.mult, ALU.add))
                    for m in range(1, TAPS):
                        link(nc.gpsimd.tensor_scalar(tap[:], src[:, m:m + P], cw[:, m:m + 1], 0.0, ALU.mult, ALU.add))
                        link(nc.gpsimd.tensor_tensor(fold[:], fold[:], tap[:], ALU.add))

                pool.wait_ge(small_loaded, 160)
                for j in range(KD):
                    pool.wait_ge(prep_dve, dve_count[turn_of("ult", j)])
                    convolve(ult[:, j, :])
                    link(nc.gpsimd.tensor_scalar(fold[:], fold[:], lng[:, j:j + 1], 0.0, ALU.mult, ALU.add))
                    link(nc.gpsimd.tensor_scalar(wc[0][:, j, :], fold[:], 1.0, 0.0, ALU.mult, ALU.add))
                    link(nc.gpsimd.tensor_tensor(wc[1][:, j, :], fold[:], wc[0][:, j, :].bitcast(F32), ALU.subtract))
                pool.wait_ge(prep_dve, dve_count[turn_of("bl")])
                convolve(bl[:])
                nc.gpsimd.tensor_scalar(fold[:], fold[:], cb[:, 0:1], 0.0, ALU.add, ALU.add).then_inc(conv_bias_ready, 1)

            @block.scalar
            def _(act):
                def col(v, n):
                    return v.rearrange("(k p) -> p k", p=T)

                for dst, src in ((lng[:], col(ln_g, KD)), (lnb[:], col(ln_b, KD)), (mu[:, 0, :], col(mu_r, KD)),
                                 (mu[:, 1, :], col(mu_k, KD)), (q_bias[:], col(b_q, KP)),
                                 (k_bias[:], col(b_k, KP)),
                                 (if_bias[0:H, :], b_i.rearrange("(h a) -> h a", a=1)),
                                 (if_bias[32:32 + H, :], b_f.rearrange("(h a) -> h a", a=1)),
                                 (cw[:], conv_w.partition_broadcast(T)),
                                 (cb[:], conv_b.partition_broadcast(T))):
                    act.dma_start(dst, src, allow_slow_non_contiguous=True).then_inc(small_loaded, 16)

                for i, (what, k, last) in enumerate(TURNS):
                    if last == "dve":
                        continue
                    act.wait_ge(prep_filled, i + 1)
                    bank = ring[:, i % RING, :]
                    if last == "split":
                        dst, scale = split_target(what, k, 0)
                        if what in ("fold_v", "fold_o", "wt_r"):
                            act.wait_ge(small_loaded, 160)
                        nc.scalar.activation(dst, split_source(what, bank), ACT.Copy, scale=scale).then_inc(prep_hi, 1)
                        continue
                    w = wt if what == "wt_v" else wt2
                    nc.scalar.activation(w[:, k, :], bank, ACT.Copy).then_inc(prep_act, 1)

            @block.tensor
            def _(pe):
                pe.wait_ge(const_ready, 3)
                for i, (what, k, last) in enumerate(TURNS):
                    if i >= RING:
                        wait_emptied(pe, i - RING)
                    bank = ring[:, i % RING, :]
                    if what == "ult":
                        pe.wait_ge(ul_loaded, 16)
                        for o in range(KP):
                            mm = pe.transpose(bank[:, o * T:(o + 1) * T], ul[:, o, k * T:(k + 1) * T], ident[:])
                    elif what == "bl":
                        pe.wait_ge(ln_b_ready, KD)
                        for j in range(KD):
                            mm = pe.matmul(bank, lnb_rep[:, j, :], ult[:, j, 3:], start=j == 0, stop=j == KD - 1)
                    elif what == "bl_t":
                        pe.wait_ge(prep_dve, dve_count[turn_of("bl")])
                        for o in range(KP):
                            mm = pe.transpose(bank[:, o * T:(o + 1) * T], bl[:, 3 + o * T:3 + (o + 1) * T], ident[:])
                    elif what in ("fold_v", "fold_o"):
                        pe.wait_ge(prep_act, act_count[turn_of("wt_" + what[-1], KP - 1)])
                        w = wt if what == "fold_v" else wt2
                        for j in range(KP):
                            mm = pe.matmul(bank, ul[:, j, k * T:(k + 1) * T], w[:, j, :],
                                           start=j == 0, stop=j == KP - 1)
                    elif what in ("bias_v", "bias_o"):
                        pe.wait_ge(prep_dve, dve_count[turn_of("bl_t")])
                        w = wt if what == "bias_v" else wt2
                        for j in range(KP):
                            mm = pe.matmul(bank, bl_t[:, j, :], w[:, j, :], start=j == 0, stop=j == KP - 1)
                    elif what == "bias_r":
                        pe.wait_ge(prep_dve, dve_count[turn_of("wt_r", 1)])
                        for j in range(KD):
                            mm = pe.matmul(bank, lnb_rep[:, j, :], wt[:, j, :], start=j == 0, stop=j == KD - 1)
                    else:
                        name = what[3:]
                        src = staged(name)
                        pe.wait_ge(stage_loaded[name], 32 if name == "if" else 16)
                        if name == "if":
                            for j in range(KP):
                                mm = pe.transpose(bank[:, j * 40:(j + 1) * 40], src[:, j * T:(j + 1) * T],
                                                  ident[0:40, 0:40])
                        elif name in ("d", "fr", "fk", "fv"):
                            for j in range(2):
                                for o in range(2):
                                    kk = 2 * k + j
                                    mm = pe.transpose(bank[:, j * D + o * T:j * D + (o + 1) * T],
                                                      src[:, o, kk * T:(kk + 1) * T], ident[:])
                        else:
                            for o in range(KP):
                                mm = pe.transpose(bank[:, o * T:(o + 1) * T], src[:, o, k * T:(k + 1) * T], ident[:])
                    mm.then_inc(prep_filled, 1)

            @block.vector
            def _(dve):
                steps = [0]

                def link(ins):
                    steps[0] += 1
                    ins.then_inc(dve_prep, 1)
                    dve.wait_ge(dve_prep, steps[0])

                nc.vector.memset(ult[:, :, 0:3], 0.0)
                nc.vector.memset(bl[:, 0:3], 0.0)
                nc.vector.memset(zero2[:], 0.0)
                nc.vector.memset(bias_rows[:].bitcast(F32), 0.0)
                nc.vector.memset(minus_half[:], -0.5)
                nc.vector.memset(chunk_keep[:], 1.0)
                link(nc.vector.memset(ones_r[:].bitcast(F32), 1.0))
                nc.vector.memset(chunk_keep[:, 0:HALF:T], 0.0)
                def small_vectors():
                    dve.wait_ge(small_loaded, 160)
                    for k in range(KD):
                        nc.vector.tensor_scalar(lnb_rep[:, k, :], ones_r[:, 0:T].bitcast(F32), lnb[:, k:k + 1], None,
                                                ALU.mult).then_inc(ln_b_ready, 1)
                    nc.vector.tensor_scalar(one_mu[:], mu[:], -1.0, 1.0, ALU.mult, ALU.add)
                    nc.vector.tensor_scalar(k_bias[:], k_bias[:], HD ** -0.5, None, ALU.mult)
                    nc.vector.tensor_scalar(if_bias[0:H, :], if_bias[0:H, :], 1.0 / CAP, None, ALU.mult)
                    nc.vector.tensor_scalar(if_bias[32:32 + H, :], if_bias[32:32 + H, :], 1.0 / CAP, None, ALU.mult)

                def bias_row(dst, src):
                    link(nc.vector.tensor_copy(row_hi[:], src))
                    link(nc.vector.tensor_tensor(src, src, row_hi[:].bitcast(F32), ALU.subtract))
                    link(nc.vector.tensor_scalar(row[:], row_hi[:].bitcast(F32), ident[0:2, 0:1], None, ALU.mult))
                    link(nc.vector.scalar_tensor_tensor(out=bias_rows[dst.start:dst.start + 2, :], in0=src,
                                                        scalar=ident[0:2, 1:2], in1=row[:], op0=ALU.mult,
                                                        op1=ALU.add))

                dve.wait_ge(const_ready, 3)
                for i, (what, k, last) in enumerate(TURNS):
                    if last == "act":
                        continue
                    if what == "bl":
                        small_vectors()
                    if what == "wt_if":
                        dve.wait_ge(conv_bias_ready, 1)
                        bias_row(CB, fold[0:2, :])
                    dve.wait_ge(prep_filled, i + 1)
                    bank = ring[:, i % RING, :]
                    if last == "split":
                        hi_dst, _ = split_target(what, k, 0)
                        lo_dst, scale = split_target(what, k, 1)
                        dve.wait_ge(prep_hi, hi_count[i])
                        if what == "wt_r":
                            nc.vector.tensor_copy(wt[:, k, :], bank)
                        nc.vector.scalar_tensor_tensor(out=lo_dst, in0=split_source(what, bank), scalar=scale,
                                                       in1=hi_dst.bitcast(F32), op0=ALU.mult,
                                                       op1=ALU.subtract).then_inc(prep_dve, 1)
                    elif what == "ult":
                        nc.vector.tensor_copy(ult[:, k, 3:], bank).then_inc(prep_dve, 1)
                    elif what == "bl":
                        dve.wait_ge(up_bias_loaded, 16)
                        nc.vector.tensor_tensor(bl[:, 3:], bank, bup_l_all[:], ALU.add).then_inc(prep_dve, 1)
                    elif what == "bl_t":
                        nc.vector.tensor_copy(bl_t[:].rearrange("p k j -> p (k j)"), bank).then_inc(prep_dve, 1)
                    elif what == "bias_v":
                        dve.wait_ge(rows_loaded, 7 * 16)
                        nc.vector.tensor_tensor(bv_all[:], bank, b0_all[:, 0, :], ALU.add).then_inc(prep_dve, 1)
                    else:
                        src, dst = (1, OB) if what == "bias_o" else (2, RB)
                        nc.vector.tensor_tensor(bias_sum[:], bank, b0_all[:, src, :], ALU.add).then_inc(prep_dve, 1)
                        dve.wait_ge(prep_dve, dve_count[i])
                        bias_row(dst, bias_sum[0:2, :])
                nc.vector.tensor_tensor(bs_all[:], bs_all[:], mhb_all[:], ALU.add)

        xf = sb("xf", [T, 2, D])
        xa = sb("xa", [T, 2, D])
        xa_t = [halves(f"xa_t{h}", [T, KD, HALF]) for h in range(2)]
        xf_t = sb("xf_t", [T, KD, 1 + HALF])

        def whole_and_halves(name, shape):
            hi = sb(name + "_hi", shape, F32R)
            with ExitStack() as place:
                whole = sb(name, shape, F32, place)
            return whole, (hi, sb(name + "_lo", shape, F32R))

        mix_r, mix_r_halves = whole_and_halves("mix_r", [T, KD, HALF])
        mix_k, mix_k_halves = whole_and_halves("mix_k", [T, KD, HALF])
        kact, kact_halves = whole_and_halves("kact", [T, KD, HALF])
        ffn = xa
        base = [sb(f"base{h}", [T, 2, D]) for h in range(2)]
        xc_whole, xc = whole_and_halves("xc", [T, KP, HALF])

        def flat(a):
            return a.rearrange("p k t -> p (k t)")

        conv_act = [flat(xc_whole[:, 2 * j:2 * j + 2, :]) for j in range(2)]
        q_t = sb("q_t", [T, PAIRS, HALF])
        k_t = sb("k_t", [T, PAIRS, HALF])
        q_dec = sb("q_dec", [T, PAIRS, T])
        k_w = sb("k_w", [T, HID])
        dec = sb("dec", [T, 2, PAIRS, T])
        v_sb = sb("v_sb", [T, H * PW + HD + 1])
        th_o = [sb(f"th_o{c}", [T, HID]) for c in range(2)]
        sr = [sb(f"sr{c}", [T, HID]) for c in range(2)]
        sk = [sb(f"sk{c}", [T, HID]) for c in range(2)]
        hid = [sb(f"hid{c}", [T, H, HD]) for c in range(2)]
        gt = halves("gt", [T, KP, T])
        state = sb("state", [T, PAIRS, PW])
        carry = sb("carry", [T, PAIRS])
        den = sb("den", [T, 2, 4])
        ln_st = sb("ln_st", [T, 2, 6])
        ln_mv = sb("ln_mv", [T, 2, 2])
        ln_sc = sb("ln_sc", [T, 4, 2])
        mh_st = sb("mh_st", [T, H, 6])
        mh_sc = sb("mh_sc", [T, 6, H])
        row_i = sb("row_i", [H, HALF])
        row_f = sb("row_f", [H, HALF])
        row_F = sb("row_F", [H, HALF])
        row_rem, row_g = row_F, row_i
        row_m = [sb(f"row_m{h}", [H, 1 + HALF]) for h in range(2)]
        row_M = sb("row_M", [H, HALF])
        row_mid = sb("row_mid", [H, HALF], BF16)
        rows_aw = sb("rows_aw", [40, HALF])
        cols_aw = sb("cols_aw", [T, 2, 40])
        m_parts = sb("m_parts", [72, HALF], BF16)
        g_parts = sb("g_parts", [72, HALF], BF16)

        x_used = sem("x_used")
        stats_ready = sem("stats_ready")
        scale_ready = sem("scale_ready")
        xh_ready = sem("xh_ready")
        xa_hi_ready = sem("xa_hi_ready")
        xf_t_carried = sem("xf_t_carried")
        mix_prev_ready = sem("mix_prev_ready")
        mix_ready = sem("mix_ready")
        mix_hi_ready = sem("mix_hi_ready")
        mix_lo_ready = sem("mix_lo_ready")
        kact_ready = sem("kact_ready")
        kact_hi_ready = sem("kact_hi_ready")
        kact_lo_ready = sem("kact_lo_ready")
        gt_hi_ready = sem("gt_hi_ready")
        base_ready = sem("base_ready")
        conv_tanh_ready = sem("conv_tanh_ready")
        xc_hi_ready = sem("xc_hi_ready")
        xc_lo_ready = sem("xc_lo_ready")
        exp_args_ready = sem("exp_args_ready")
        exp_rows_ready = sem("exp_rows_ready")
        parts_ready = sem("parts_ready")
        sc_filled = [sem(f"sc_filled{j}") for j in range(2)]
        sc_emptied = [sem(f"sc_emptied{j}") for j in range(2)]
        masked = sem("masked")
        num_filled = sem("num_filled")
        num_emptied = sem("num_emptied")
        state_reset = sem("state_reset")
        cols_ready = sem("cols_ready")
        r_tanh_ready = sem("r_tanh_ready")
        gated = [sem(f"gated{c}") for c in range(2)]
        mh_stats_ready = sem("mh_stats_ready")
        normed = sem("normed")
        out_ready = [sem(f"out_ready{c}") for c in range(2)]
        out_stored = [sem(f"out_stored{c}") for c in range(2)]
        buffers_cleared = sem("buffers_cleared")
        buffers_ready = sem("buffers_ready")
        pe_settled = sem("pe_settled")
        pool_settled = sem("pool_settled")
        dve_settled = sem("dve_settled")
        state_cleared = sem("state_cleared")
        ring_filled = [sem(f"ring_filled{j}") for j in range(RING)]
        ring_emptied = [sem(f"ring_emptied{j}") for j in range(RING)]
        dve_front_step = sem("dve_front_step")
        dve_tile_step = sem("dve_tile_step")
        pool_front_step = sem("pool_front_step")
        pool_tile_step = sem("pool_tile_step")

        SC_USES = 3 * 4 - 1

        def sc_use(b, h, c, k):
            return b * SC_USES + (3 * (2 * h + c) + k)

        def sc_free(b, h, c, k):
            return b * SC_USES + (3 * (2 * h + c) + k + 1)

        def tile_of(b, h, c):
            return b * 4 + (2 * h + c)

        main = nc.Block()
        block = keep.enter_context(main)

        def v_head(h, width):
            at = (HD + 1) + PW * h
            return v_sb[:, at:at + width]

        def settle(eng, count):
            eng.sem_inc(count, 1)

        @block.sync
        def _(sp):
            def body(b, last):
                for h in range(2):
                    n = b * 2 + h
                    if not (last and h == 1):
                        sp.wait_ge(x_used, n + 1)
                        sp.dma_start(xin[:], x_dram[n + 1]).then_inc(x_loaded, 16)
                    for c in range(2):
                        bank, before = ring_use("last" if last else "body", b, ("down", h, c))
                        sp.wait_ge(ring_emptied[bank], before + 1)
                        sp.dma_start(out_dram[tile_of(b, h, c)], base[h][:, c, :]).then_inc(out_stored[c], 16)

            with sp.Fori(0, B - 1) as b:
                body(b, False)
            body(B - 1, True)
            for c in range(2):
                sp.wait_ge(out_stored[c], 16 * (2 * B + 1))

        @block.tensor
        def _(pe):
            def take(kind, b, use):
                bank, before = ring_use(kind, b, use)
                pe.wait_ge(ring_emptied[bank], before)
                return ring[:, bank, :], ring_filled[bank]

            def emptied(kind, b, use):
                bank, before = ring_use(kind, b, use)
                pe.wait_ge(ring_emptied[bank], before + 1)

            def transposes_x(kind, b, r, n):
                pe.wait_ge(xh_ready, n + 1)
                for use, src in (("xf", xf), ("xa", xa)):
                    bank, filled = take(kind, b, (use, r, 0))
                    for k in range(KD):
                        for c in range(2):
                            mm = pe.transpose(bank[:, k * HALF + c * T:k * HALF + (c + 1) * T],
                                              src[:, c, k * T:(k + 1) * T], ident[:])
                    mm.then_inc(filled, 1)

            def three(dst, w, act, first, last):
                pe.matmul(dst, w[0], act[0], start=first, stop=False, skip_group_check=True)
                pe.matmul(dst, w[0], act[1], start=False, stop=False, skip_group_check=True)
                return pe.matmul(dst, w[1], act[0], start=False, stop=last, skip_group_check=True)

            def conv(kind, b, r, h):
                emptied(kind, b, ("xa", r, 0))
                for j in range(2):
                    bank, filled = take(kind, b, (f"conv{j}", r, 0))
                    for m in range(2):
                        f = slice((2 * j + m) * T, (2 * j + m + 1) * T)
                        dst = bank[:, m * HALF:(m + 1) * HALF]
                        for k in range(KD):
                            three(dst, [w[:, k, f] for w in wc], [a[:, k, :] for a in xa_t[h]], m == 0 and k == 0, False)
                        mm = pe.matmul(dst, bias_rows[CB, f], ones_r[CB, :], start=False, stop=True,
                                       skip_group_check=True)
                    mm.then_inc(filled, 1)

            def ffn_k(kind, b, r, n):
                pe.wait_ge(mix_lo_ready, 2 * n + 1)
                bank, filled = take(kind, b, ("ffn_k", r, 0))
                for m in range(KD):
                    for k in range(KD):
                        mm = three(bank[:, m * HALF:(m + 1) * HALF], [w[:, k, m * T:(m + 1) * T] for w in fk],
                                   [a[:, k, :] for a in mix_k_halves], k == 0 and m == 0, k == KD - 1)
                mm.then_inc(filled, 1)

            def ffn_tokens(kind, b, r, use, act, w):
                bank, filled = take(kind, b, (use, r, 0))
                for c in range(2):
                    for k in range(KD):
                        mm = three(bank[:, c * D:(c + 1) * D], [a[:, k, c * T:(c + 1) * T] for a in act],
                                   [p[:, k, :] for p in w], k == 0 and c == 0, k == KD - 1)
                mm.then_inc(filled, 1)

            def ffn_r(kind, b, r, n):
                pe.wait_ge(mix_lo_ready, 2 * n + 2)
                ffn_tokens(kind, b, r, "ffn_r", mix_r_halves, fr)

            def gates(kind, b, r, n):
                pe.wait_ge(xc_lo_ready, 2 * (n + 1))
                bank, filled = take(kind, b, ("gates", r, 0))
                for k in range(KP):
                    mm = three(bank[0:40, 0:HALF], [w[:, k, :] for w in wif], [a[:, k, :] for a in xc],
                               k == 0, k == KP - 1)
                mm.then_inc(filled, 1)

            def heads(kind, b, r, use, w, j):
                bank, filled = take(kind, b, (f"{use}{j}", r, 0))
                for m in range(2):
                    f = slice((2 * j + m) * T, (2 * j + m + 1) * T)
                    for k in range(KP):
                        mm = three(bank[:, m * HALF:(m + 1) * HALF], [p[:, k, f] for p in w],
                                   [a[:, k, :] for a in xc], m == 0 and k == 0, k == KP - 1)
                mm.then_inc(filled, 1)

            def cols(kind, b, r, n):
                pe.wait_ge(exp_rows_ready, 2 * n + 1)
                bank, filled = take(kind, b, ("cols", r, 0))
                settle(pe, pe_settled)
                for c in range(2):
                    mm = pe.transpose(bank[:, c * 40:(c + 1) * 40], rows_aw[:, c * T:(c + 1) * T], ident[0:40, 0:40])
                mm.then_inc(filled, 1)

            def tokens(kind, b, h, c, use, act, w, nk, bias):
                bank, filled = take(kind, b, (use, h, c))
                t = slice(c * T, (c + 1) * T)
                for k in range(nk):
                    lhs = [a[:, k, t] for a in act]
                    pe.matmul(bank, lhs[0], w[0][:, k, :], start=k == 0, stop=False)
                    pe.matmul(bank, lhs[0], w[1][:, k, :], start=False, stop=False)
                    mm = pe.matmul(bank, lhs[1], w[0][:, k, :], start=False, stop=k == nk - 1 and bias is None)
                if bias is not None:
                    mm = pe.matmul(bank, ones_r[bias, 0:T], bias_rows[bias, :], start=False, stop=True)
                mm.then_inc(filled, 1)

            def maxima(b, h, c, n):
                pe.wait_ge(parts_ready, 2 * n + 1)
                for j in range(2):
                    pe.wait_ge(sc_emptied[j], sc_free(b, h, c, 0))
                    for i in range(4):
                        mm = pe.matmul(sc_ps[:, j, i * T:(i + 1) * T], sel[:, (2 * i + j) * T:(2 * i + j + 1) * T],
                                       m_parts[:, c * T:(c + 1) * T], start=i == 0, stop=True, skip_group_check=True)
                    mm.then_inc(sc_filled[j], 1)

            def scores(b, h, c):
                t = slice(c * T, (c + 1) * T)
                for j in range(2):
                    pe.wait_ge(sc_emptied[j], sc_free(b, h, c, 1))
                for i in range(PAIRS):
                    for j in range(2):
                        p = slice(HD * j, HD * (j + 1))
                        mm = pe.matmul(sc_ps[:, j, i * T:(i + 1) * T], k_t[p, i, t], q_t[p, i, t],
                                       start=i == 0, stop=True, skip_group_check=True)
                        if i == PAIRS - 1:
                            mm.then_inc(sc_filled[j], 1)

            def decay(kind, b, h, c, n):
                pe.wait_ge(parts_ready, 2 * n + 2)
                bank, filled = take(kind, b, ("decay", h, c))
                for j in range(PAIRS):
                    at = 2 * j * T + HD
                    mm = pe.matmul(bank[:, j * T:(j + 1) * T], sel[:, at:at + T], g_parts[:, c * T:(c + 1) * T],
                                   start=j == 0, stop=True, skip_group_check=True)
                mm.then_inc(filled, 1)

            def k_tokens(kind, b, h, c):
                bank, filled = take(kind, b, ("kt", h, c))
                for j in range(PAIRS):
                    mm = pe.transpose(bank[:, j * T:(j + 1) * T], k_t[:, j, c * T:(c + 1) * T], ident[:])
                mm.then_inc(filled, 1)

            def numerators(kind, b, h, c):
                t = tile_of(b, h, c)
                if h == 0 and c == 0:
                    pe.wait_ge(state_reset, b + 1)
                pe.wait_ge(num_emptied, t + 1)
                emptied(kind, b, ("decay", h, c))
                for j in range(PAIRS):
                    pe.matmul(num_ps[:, j // 2, j % 2 * PW:(j % 2 + 1) * PW], q_dec[:, j, :], state[:, j, :],
                              start=j % 2 == 0, stop=False, skip_group_check=True)
                emptied(kind, b, ("v", h, c))
                for i in range(2):
                    pe.wait_ge(sc_emptied[i], sc_free(b, h, c, 2))
                    for j in range(PAIRS):
                        hd = 2 * j + i
                        at = (HD + 1) + PW * hd - (HD + 1) * i
                        mm = pe.matmul(num_ps[:, j // 2, j % 2 * PW:(j % 2 + 1) * PW], dec[:, i, j, :],
                                       v_sb[:, at:at + PW], start=False, stop=i == 1, skip_group_check=True)
                mm.then_inc(num_filled, 1)

            def state_update(kind, b, h, c):
                emptied(kind, b, ("kt", h, c))
                for j in range(2):
                    for i in range(2):
                        pr = 2 * j + i
                        at = (HD + 1) + PW * 2 * pr
                        rhs = v_sb[:, at:at + 2 * PW].rearrange("p (s w) -> p s w", s=2)[:, :, 0:HD + 1]
                        mm = pe.matmul(sc_ps[:, j, i * PW:(i + 1) * PW], k_w[:, pr * T:(pr + 1) * T], rhs,
                                       start=i == 0, stop=True, skip_group_check=True)
                    mm.then_inc(sc_filled[j], 1)

            def gt_transposes(kind, b, h, c, n):
                pe.wait_ge(out_ready[c], n + 2)
                bank, filled = take(kind, b, ("gt", h, c))
                src = hid[c][:].rearrange("p h d -> p (h d)")
                for j in range(KP):
                    mm = pe.transpose(bank[:, j * T:(j + 1) * T], src[:, j * T:(j + 1) * T], ident[:])
                mm.then_inc(filled, 1)

            def down(kind, b, h, c):
                emptied(kind, b, ("gt", h, c))
                bank, filled = take(kind, b, ("down", h, c))
                for k in range(KP):
                    mm = three(bank[:, 0:D], [a[:, k, :] for a in gt], [w[:, k, :] for w in wd], k == 0, k == KP - 1)
                mm.then_inc(filled, 1)

            def ffn_v(kind, b, r, n):
                pe.wait_ge(kact_lo_ready, n + 1)
                ffn_tokens(kind, b, r, "ffn_v", kact_halves, fv)

            def half_end(kind, b, h, n):
                front = kind != "last" or h == 0
                ahead = (kind, b, h + 1)
                gt_transposes(kind, b, h, 0, n)
                if front:
                    conv(*ahead, (h + 1) % 2)
                    ffn_k(*ahead, n + 1)
                down(kind, b, h, 0)
                if front:
                    ffn_r(*ahead, n + 1)
                    gates(*ahead, n + 1)
                    heads(*ahead, "q", wq, 0)
                    heads(*ahead, "q", wq, 1)
                    heads(*ahead, "k", wk, 0)
                    ffn_v(*ahead, n + 1)
                gt_transposes(kind, b, h, 1, n)
                if front:
                    heads(*ahead, "k", wk, 1)
                    cols(*ahead, n + 1)
                down(kind, b, h, 1)

            def first_front():
                first = ("first", 0, 0)
                transposes_x(*first, 0)
                conv(*first, 0)
                ffn_k(*first, 0)
                ffn_r(*first, 0)
                gates(*first, 0)
                heads(*first, "q", wq, 0)
                heads(*first, "q", wq, 1)
                heads(*first, "k", wk, 0)
                ffn_v(*first, 0)
                heads(*first, "k", wk, 1)
                cols(*first, 0)

            def body(b, last):
                kind = "last" if last else "body"
                for h in range(2):
                    n = b * 2 + h
                    front = not (last and h == 1)
                    for c in range(2):
                        tokens(kind, b, h, c, "o", xa_t[h], wo, KD, OB)
                        tokens(kind, b, h, c, "r", xa_t[h], wr, KD, RB)
                        maxima(b, h, c, n)
                        tokens(kind, b, h, c, "skip", xc, ws, KP, None)
                        decay(kind, b, h, c, n)
                        k_tokens(kind, b, h, c)
                        scores(b, h, c)
                        if c == 1 and front:
                            transposes_x(kind, b, h + 1, n + 1)
                        tokens(kind, b, h, c, "v", xa_t[h], wv, KD, None)
                        numerators(kind, b, h, c)
                        if not (h == 1 and c == 1):
                            state_update(kind, b, h, c)
                    half_end(kind, b, h, n)

            first_front()
            pe.wait_ge(buffers_ready, 1)
            with pe.Fori(0, B - 1) as b:
                body(b, False)
            body(B - 1, True)

        @block.scalar
        def _(act):
            def filled(kind, b, use):
                bank, before = ring_use(kind, b, use)
                act.wait_ge(ring_filled[bank], before + 1)
                return ring[:, bank, :], ring_emptied[bank]

            def front_x(kind, b, r, n, h):
                if kind != "first":
                    act.wait_ge(mix_ready, n)
                prev = zero2[:] if h == 0 else xf_t[:, :, HALF:HALF + 1]
                nc.scalar.activation(xf_t[:, :, 0:1], prev, ACT.Copy).then_inc(xf_t_carried, 1)
                bank, emptied = filled(kind, b, ("xf", r, 0))
                act.wait_ge(xf_t_carried, n + 1)
                nc.scalar.activation(xf_t[:, :, 1:1 + HALF], bank.rearrange("p (k t) -> p k t", k=KD),
                                     ACT.Copy).then_inc(emptied, 1)
                bank, _ = filled(kind, b, ("xa", r, 0))
                nc.scalar.activation(xa_t[h][0][:].rearrange("p k t -> p (k t)"), bank,
                                     ACT.Copy).then_inc(xa_hi_ready, 1)

            def front_conv(kind, b, r, n):
                for j in range(2):
                    bank, _ = filled(kind, b, (f"conv{j}", r, 0))
                    if kind != "first":
                        act.wait_ge(xc_lo_ready, 2 * n)
                    nc.scalar.activation(conv_act[j], bank, ACT.Tanh, scale=0.5).then_inc(conv_tanh_ready, 1)

            def front_conv_high(kind, b, r, n):
                for j in range(2):
                    bank, before = ring_use(kind, b, (f"conv{j}", r, 0))
                    act.wait_ge(ring_emptied[bank], before + 1)
                    nc.scalar.activation(xc[0][:, 2 * j:2 * j + 2, :].rearrange("p k t -> p (k t)"), conv_act[j],
                                         ACT.Copy).then_inc(xc_hi_ready, 1)

            def front_mix_high(n):
                act.wait_ge(mix_ready, n + 1)
                for mix, (hi, _) in ((mix_k, mix_k_halves), (mix_r, mix_r_halves)):
                    nc.scalar.activation(flat(hi[:]), flat(mix[:]), ACT.Copy).then_inc(mix_hi_ready, 1)

            def front_kact_high(n):
                act.wait_ge(kact_ready, n + 1)
                nc.scalar.activation(flat(kact_halves[0][:]), flat(kact[:]), ACT.Copy).then_inc(kact_hi_ready, 1)

            def front_ffn(kind, b, r, n):
                if kind != "first":
                    act.wait_ge(base_ready, n)
                bank, emptied = filled(kind, b, ("ffn_k", r, 0))
                nc.scalar.activation(flat(kact[:]), bank, ACT.Relu).then_inc(emptied, 1)
                bank, emptied = filled(kind, b, ("ffn_r", r, 0))
                nc.scalar.activation(ffn[:].rearrange("p c d -> p (c d)"), bank, ACT.Tanh,
                                     scale=0.5).then_inc(emptied, 1)

            def front_gates(kind, b, r, n):
                bank, emptied = filled(kind, b, ("gates", r, 0))
                if kind != "first":
                    act.wait_ge(parts_ready, 2 * n)
                nc.scalar.activation(row_i[:], bank[0:H, 0:HALF], ACT.Tanh, scale=1.0 / CAP,
                                     bias=if_bias[0:H, :])
                nc.scalar.activation(row_f[:], bank[32:32 + H, 0:HALF], ACT.Tanh, scale=1.0 / CAP,
                                     bias=if_bias[32:32 + H, :]).then_inc(emptied, 1)

            def front_exps(kind, b, r, n):
                act.wait_ge(exp_args_ready, n + 1)
                if kind != "first":
                    act.wait_ge(cols_ready, n)
                nc.scalar.activation(rows_aw[32:32 + H, :], row_f[:], ACT.Exp).then_inc(exp_rows_ready, 1)
                nc.scalar.activation(row_g[:], row_i[:], ACT.Exp).then_inc(exp_rows_ready, 1)

            def front_q(kind, b, r, j):
                bank, emptied = filled(kind, b, (f"q{j}", r, 0))
                for m in range(2):
                    ins = nc.scalar.activation(q_t[:, 2 * j + m, :], bank[:, m * HALF:(m + 1) * HALF],
                                               ACT.Identity, bias=q_bias[:, 2 * j + m:2 * j + m + 1])
                ins.then_inc(emptied, 1)

            def front_rest(kind, b, r, n):
                front_gates(kind, b, r, n)
                front_q(kind, b, r, 0)
                front_exps(kind, b, r, n)
                front_kact_high(n)
                front_q(kind, b, r, 1)

            def gt_copy(kind, b, h, c):
                bank, _ = filled(kind, b, ("gt", h, c))
                nc.scalar.activation(flat(gt[0][:]), bank, ACT.Copy).then_inc(gt_hi_ready, 1)

            def tile(kind, b, h, c, n):
                bank, emptied = filled(kind, b, ("o", h, c))
                act.wait_ge(gated[c], n + 1)
                nc.scalar.activation(th_o[c][:], bank, ACT.Tanh, scale=0.5).then_inc(emptied, 1)
                bank, _ = filled(kind, b, ("r", h, c))
                act.wait_ge(out_ready[c], n + 1)
                nc.scalar.activation(sr[c][:], bank, ACT.Tanh, scale=0.5).then_inc(r_tanh_ready, 1)
                if c == 0:
                    act.wait_ge(cols_ready, n + 1)
                for j in range(2):
                    act.wait_ge(sc_filled[j], sc_use(b, h, c, 1))
                    for i in range(4):
                        hd = 2 * i + j
                        ins = nc.scalar.activation(dec[:, j, i, :], sc_ps[:, j, i * T:(i + 1) * T], ACT.Exp,
                                                   scale=-1.0, bias=cols_aw[:, c, hd:hd + 1])
                    ins.then_inc(sc_emptied[j], 1)

            def body(b, last):
                kind = "last" if last else "body"
                for h in range(2):
                    n = b * 2 + h
                    front = not (last and h == 1)
                    tile(kind, b, h, 0, n)
                    tile(kind, b, h, 1, n)
                    if front:
                        front_x(kind, b, h + 1, n + 1, (h + 1) % 2)
                        front_mix_high(n + 1)
                    gt_copy(kind, b, h, 0)
                    if front:
                        front_conv(kind, b, h + 1, n + 1)
                        front_conv_high(kind, b, h + 1, n + 1)
                        front_ffn(kind, b, h + 1, n + 1)
                        front_rest(kind, b, h + 1, n + 1)
                    gt_copy(kind, b, h, 1)

            front_x("first", 0, 0, 0, 0)
            front_mix_high(0)
            front_conv("first", 0, 0, 0)
            front_conv_high("first", 0, 0, 0)
            front_ffn("first", 0, 0, 0)
            front_rest("first", 0, 0, 0)
            with act.Fori(0, B - 1) as b:
                body(b, False)
            body(B - 1, True)

        @block.gpsimd
        def _(pool):
            FRONT_STEPS, TILE_STEPS = 7, 8

            def front_scale(kind, n):
                k = [0]

                def link(ins, settled=False):
                    k[0] += 1
                    ins.then_inc(pool_front_step, 1)
                    pool.wait_ge(pool_front_step, n * FRONT_STEPS + k[0])
                    if settled:
                        settle(pool, pool_settled)

                used = k
                pool.wait_ge(stats_ready, n + 1)
                settle(pool, pool_settled)
                var = ln_mv[:, :, 1]
                rstd, t, both, e = (ln_sc[:, i, :] for i in range(4))
                link(nc.gpsimd.tensor_scalar(t, var, EPS_OUTER, None, ALU.add))
                link(nc.gpsimd.tensor_tensor(rstd, t, minus_half[:, 0:2], ALU.pow))
                link(nc.gpsimd.tensor_tensor(t, rstd, rstd, ALU.mult))
                link(nc.gpsimd.tensor_tensor(t, t, var, ALU.mult), settled=True)
                link(nc.gpsimd.tensor_scalar(t, t, EPS_ATTN, None, ALU.add))
                link(nc.gpsimd.tensor_tensor(e, t, minus_half[:, 0:2], ALU.pow))
                nc.gpsimd.tensor_tensor(both, rstd, e, ALU.mult).then_inc(scale_ready, 1)
                return link, used

            def front_base(kind, n, h, link, used):
                pool.wait_ge(xh_ready, n + 1)
                if kind != "first":
                    for c in range(2):
                        pool.wait_ge(out_stored[c], 16 * n)
                nc.gpsimd.tensor_tensor(base[h][:], xin[:], xf[:], ALU.add).then_inc(x_used, 1)
                pool.wait_ge(x_used, n + 1)
                link(nc.gpsimd.tensor_tensor(base[h][:], base[h][:], bd_all[:].unsqueeze(1).to_broadcast([T, 2, D]),
                                             ALU.add))
                assert used[0] == FRONT_STEPS

            def front_mix(kind, b, r, n):
                bank, before = ring_use(kind, b, ("xf", r, 0))
                pool.wait_ge(ring_emptied[bank], before + 1)
                settle(pool, pool_settled)
                for i, dst in enumerate((mix_r, mix_k)):
                    for k in range(KD):
                        ins = nc.gpsimd.tensor_scalar(dst[:, k, :], xf_t[:, k, 0:HALF], one_mu[:, i, k:k + 1], 0.0,
                                                      ALU.mult, ALU.add)
                ins.then_inc(mix_prev_ready, 1)

            def front_kact(kind, b, r, n):
                bank, before = ring_use(kind, b, ("ffn_k", r, 0))
                pool.wait_ge(ring_emptied[bank], before + 1)
                nc.gpsimd.tensor_tensor(kact[:], kact[:], kact[:], ALU.mult).then_inc(kact_ready, 1)

            def front_kact_low(n):
                pool.wait_ge(kact_hi_ready, n + 1)
                hi, lo = (a[:] for a in kact_halves)
                nc.gpsimd.tensor_tensor(lo, kact[:], hi.bitcast(F32), ALU.subtract).then_inc(kact_lo_ready, 1)

            def front_add(kind, b, r, h):
                bank, before = ring_use(kind, b, ("ffn_v", r, 0))
                pool.wait_ge(ring_emptied[bank], before + 1)
                nc.gpsimd.tensor_tensor(base[h][:], base[h][:], ffn[:], ALU.add).then_inc(base_ready, 1)

            def mask(b, h, c):
                for j in range(2):
                    pool.wait_ge(sc_emptied[j], sc_free(b, h, c, 1))
                settle(pool, pool_settled)
                d = dec[:].rearrange("p j i t -> p (j i) t")
                nc.gpsimd.affine_select(out=d, in_=d, compare_op=ALU.is_ge, fill=0.0, base=0,
                                        pattern=[[0, H], [1, T]], channel_multiplier=-1).then_inc(masked, 1)

            def norm_scale(b, h, c):
                t = tile_of(b, h, c)
                k = [0]

                def link(ins, settled=False):
                    k[0] += 1
                    ins.then_inc(pool_tile_step, 1)
                    pool.wait_ge(pool_tile_step, t * TILE_STEPS + k[0])
                    if settled:
                        settle(pool, pool_settled)

                pool.wait_ge(mh_stats_ready, t + 1)
                s, d, q, mean, rstd, dd = (mh_sc[:, i, :] for i in range(6))
                mean_e, m2_e, mean_o, m2_o = (mh_st[:, :, i] for i in (1, 2, 4, 5))
                nc.gpsimd.tensor_tensor(s, mean_e, mean_o, ALU.add)
                nc.gpsimd.tensor_tensor(q, m2_e, m2_o, ALU.add)
                link(nc.gpsimd.tensor_tensor(d, mean_e, mean_o, ALU.subtract), settled=True)
                nc.gpsimd.tensor_scalar(mean, s, 0.5, 0.0, ALU.mult, ALU.add)
                nc.gpsimd.tensor_scalar(q, q, 1.0 / HD, 4.0 * EPS_ATTN, ALU.mult, ALU.add)
                link(nc.gpsimd.tensor_tensor(dd, d, d, ALU.mult), settled=True)
                link(nc.gpsimd.tensor_scalar(dd, dd, 0.25, 0.0, ALU.mult, ALU.add))
                link(nc.gpsimd.tensor_tensor(q, q, dd, ALU.add))
                link(nc.gpsimd.tensor_tensor(rstd, q, minus_half[:], ALU.pow))
                return link, k, mean, rstd

            def norm(c, link, k, mean, rstd):
                bc = [T, H, HD]
                link(nc.gpsimd.tensor_tensor(hid[c][:], hid[c][:], mean.unsqueeze(2).to_broadcast(bc), ALU.subtract))
                link(nc.gpsimd.tensor_tensor(hid[c][:], hid[c][:], rstd.unsqueeze(2).to_broadcast(bc), ALU.mult))
                flat = hid[c][:].rearrange("p h d -> p (h d)")
                link(nc.gpsimd.tensor_tensor(flat, flat, mhg_all[:], ALU.mult))
                nc.gpsimd.tensor_tensor(flat, flat, sk[c][:], ALU.add).then_inc(normed, 1)
                assert k[0] == TILE_STEPS

            def front_first():
                link, used = front_scale("first", 0)
                front_mix("first", 0, 0, 0)
                front_base("first", 0, 0, link, used)
                front_kact("first", 0, 0, 0)
                front_kact_low(0)
                front_add("first", 0, 0, 0)

            def body(b, last):
                kind = "last" if last else "body"
                for h in range(2):
                    n = b * 2 + h
                    front = not (last and h == 1)
                    mask(b, h, 0)
                    if front:
                        link, used = front_scale(kind, n + 1)
                    scaled = norm_scale(b, h, 0)
                    mask(b, h, 1)
                    norm(0, *scaled)
                    if front:
                        front_mix(kind, b, h + 1, n + 1)
                        front_base(kind, n + 1, (h + 1) % 2, link, used)
                    norm(1, *norm_scale(b, h, 1))
                    if front:
                        front_kact(kind, b, h + 1, n + 1)
                        front_kact_low(n + 1)
                        front_add(kind, b, h + 1, (h + 1) % 2)

            front_first()
            with pool.Fori(0, B - 1) as b:
                body(b, False)
            body(B - 1, True)

        @block.vector
        def _(dve):
            FRONT_STEPS, TILE_STEPS = 11, 2

            def filled(kind, b, use):
                bank, before = ring_use(kind, b, use)
                dve.wait_ge(ring_filled[bank], before + 1)
                return ring[:, bank, :], ring_emptied[bank]

            def front_link(n, used):
                def link(ins, settled=False):
                    used[0] += 1
                    ins.then_inc(dve_front_step, 1)
                    dve.wait_ge(dve_front_step, n * FRONT_STEPS + used[0])
                    if settled:
                        settle(dve, dve_settled)
                return link

            def x_stats(n, link):
                dve.wait_ge(x_loaded, 16 * n + 16)
                nc.vector.bn_stats(ln_st[:, 0, :], xin[:, 0, :])
                link(nc.vector.bn_stats(ln_st[:, 1, :], xin[:, 1, :]), settled=True)
                nc.vector.bn_aggr(ln_mv[:, 0, :], ln_st[:, 0, :])
                nc.vector.bn_aggr(ln_mv[:, 1, :], ln_st[:, 1, :]).then_inc(stats_ready, 1)

            def x_normalise(kind, n):
                dve.wait_ge(scale_ready, n + 1)
                if kind != "first":
                    dve.wait_ge(x_used, n)
                for c in range(2):
                    for dst, k in ((xf, 0), (xa, 2)):
                        ins = nc.vector.tensor_scalar(dst[:, c, :], xin[:, c, :], ln_mv[:, c, 0:1],
                                                      ln_sc[:, k, c:c + 1], ALU.subtract, ALU.mult)
                ins.then_inc(xh_ready, 1)

            def x_low(kind, b, r, n, h):
                bank, emptied = filled(kind, b, ("xa", r, 0))
                dve.wait_ge(xa_hi_ready, n + 1)
                hi, lo = (a[:].rearrange("p k t -> p (k t)") for a in xa_t[h])
                nc.vector.tensor_tensor(lo, bank, hi.bitcast(F32), ALU.subtract).then_inc(emptied, 1)

            def mix(n):
                dve.wait_ge(mix_prev_ready, n + 1)
                for i, dst in enumerate((mix_r, mix_k)):
                    for k in range(KD):
                        ins = nc.vector.scalar_tensor_tensor(out=dst[:, k, :], in0=xf_t[:, k, 1:1 + HALF],
                                                             scalar=mu[:, i, k:k + 1], in1=dst[:, k, :],
                                                             op0=ALU.mult, op1=ALU.add)
                ins.then_inc(mix_ready, 1)

            def mix_low(n, j):
                dve.wait_ge(mix_hi_ready, 2 * n + (j + 1))
                mix, (hi, lo) = ((mix_k, mix_k_halves), (mix_r, mix_r_halves))[j]
                nc.vector.tensor_tensor(flat(lo[:]), flat(mix[:]), flat(hi[:]).bitcast(F32), ALU.subtract).then_inc(mix_lo_ready, 1)

            def gt_low(kind, b, h, c):
                bank, emptied = filled(kind, b, ("gt", h, c))
                dve.wait_ge(gt_hi_ready, tile_of(b, h, c) + 1)
                hi, lo = (flat(a[:]) for a in gt)
                nc.vector.tensor_tensor(lo, bank, hi.bitcast(F32), ALU.subtract).then_inc(emptied, 1)

            def conv_silu(kind, b, r, n):
                for j in range(2):
                    bank, emptied = filled(kind, b, (f"conv{j}", r, 0))
                    dve.wait_ge(conv_tanh_ready, 2 * n + j + 1)
                    nc.vector.scalar_tensor_tensor(out=conv_act[j], in0=conv_act[j], scalar=1.0, in1=bank,
                                                   op0=ALU.add, op1=ALU.mult).then_inc(emptied, 1)

            def conv_low(n):
                for j in range(2):
                    dve.wait_ge(xc_hi_ready, 2 * n + j + 1)
                    hi, lo = (a[:, 2 * j:2 * j + 2, :].rearrange("p k t -> p (k t)") for a in xc)
                    nc.vector.tensor_tensor(lo, conv_act[j], hi.bitcast(F32), ALU.subtract).then_inc(xc_lo_ready, 1)

            def gate_rows(kind, b, r, n, h, link):
                bank, before = ring_use(kind, b, ("gates", r, 0))
                dve.wait_ge(ring_emptied[bank], before + 1)
                nc.vector.tensor_scalar(row_i[:], row_i[:], CAP, None, ALU.mult)
                link(nc.vector.tensor_scalar(row_f[:], row_f[:], CAP, None, ALU.mult))
                if h == 1:
                    nc.vector.tensor_copy(row_m[1][:, 0:1], row_m[0][:, HALF:HALF + 1])
                link(nc.vector.tensor_tensor_scan(out=row_F[:], data0=chunk_keep[:], data1=row_f[:], initial=0.0,
                                                  op0=ALU.mult, op1=ALU.add))
                link(nc.vector.tensor_tensor_scan(out=row_m[h][:, 1:], data0=row_f[:], data1=row_i[:],
                                                  initial=row_m[h][:, 0:1], op0=ALU.add, op1=ALU.max))
                nc.vector.tensor_tensor(rows_aw[0:H, :], row_i[:], row_F[:], ALU.subtract)
                link(nc.vector.tensor_tensor(row_M[:], row_m[h][:, 1:], row_F[:], ALU.subtract))

                def chunks(a):
                    return a.rearrange("h (c t) -> h c t", c=2)

                def each_chunk(a):
                    return a.unsqueeze(2).to_broadcast([H, 2, T])

                nc.vector.tensor_tensor(chunks(row_f[:]), chunks(rows_aw[0:H, :]),
                                        each_chunk(row_M[:, T - 1:HALF:T]), ALU.subtract)
                nc.vector.tensor_tensor(chunks(row_i[:]), each_chunk(row_m[h][:, 0:HALF:T]), chunks(row_M[:]),
                                        ALU.subtract).then_inc(exp_args_ready, 1)

            def parts(dst, src, link):
                link(nc.vector.tensor_copy(dst[0:H, :], src))
                link(nc.vector.tensor_tensor(row_rem[:], src, dst[0:H, :], ALU.subtract))
                link(nc.vector.tensor_copy(row_mid[:], row_rem[:]))
                nc.vector.tensor_copy(dst[32:32 + H, :], row_mid[:])
                nc.vector.tensor_tensor(dst[64:64 + H, :], row_rem[:], row_mid[:], ALU.subtract).then_inc(parts_ready, 1)

            def ffn_gate(kind, b, r):
                rbank, before = ring_use(kind, b, ("ffn_r", r, 0))
                dve.wait_ge(ring_emptied[rbank], before + 1)
                bank, emptied = filled(kind, b, ("ffn_v", r, 0))
                f = ffn[:].rearrange("p c d -> p (c d)")
                nc.vector.scalar_tensor_tensor(out=f, in0=f, scalar=1.0, in1=bank, op0=ALU.add,
                                               op1=ALU.mult).then_inc(emptied, 1)

            def k_copy(kind, b, r, j):
                bank, emptied = filled(kind, b, (f"k{j}", r, 0))
                for m in range(2):
                    ins = nc.vector.tensor_scalar(k_t[:, 2 * j + m, :], bank[:, m * HALF:(m + 1) * HALF],
                                                  k_bias[:, 2 * j + m:2 * j + m + 1], None, ALU.add)
                ins.then_inc(emptied, 1)

            def cols_copy(kind, b, r, n):
                bank, emptied = filled(kind, b, ("cols", r, 0))
                nc.vector.tensor_copy(cols_aw[:, 0, :], bank[:, 0:40]).then_inc(cols_ready, 1)
                nc.vector.tensor_copy(cols_aw[:, 1, :], bank[:, 40:80]).then_inc(emptied, 1)

            def reset_state(b):
                nc.vector.memset(state[:], 0.0).then_inc(state_cleared, 1)
                dve.wait_ge(state_cleared, b + 1)
                nc.vector.memset(state[0:HD, :, HD:HD + 1], 1.0)
                nc.vector.memset(state[HD:T, :, PW - 1:PW], 1.0).then_inc(state_reset, 1)

            def silu_r(kind, b, h, c):
                bank, emptied = filled(kind, b, ("r", h, c))
                dve.wait_ge(r_tanh_ready, tile_of(b, h, c) + 1)
                nc.vector.scalar_tensor_tensor(out=sr[c][:], in0=sr[c][:], scalar=1.0, in1=bank, op0=ALU.add,
                                               op1=ALU.mult).then_inc(emptied, 1)

            def skip(kind, b, h, c):
                bank, emptied = filled(kind, b, ("skip", h, c))
                nc.vector.tensor_tensor(sk[c][:], bank, bs_all[:], ALU.add).then_inc(emptied, 1)

            def q_decayed(kind, b, h, c):
                bank, emptied = filled(kind, b, ("decay", h, c))
                d = bank.rearrange("p (j t) -> p j t", j=PAIRS)
                nc.vector.tensor_copy(carry[:], d[:, :, T - 1])
                nc.vector.tensor_tensor(q_dec[:], q_t[:, :, c * T:(c + 1) * T], d, ALU.mult).then_inc(emptied, 1)

            def k_weighted(kind, b, h, c):
                bank, emptied = filled(kind, b, ("kt", h, c))
                if c == 0:
                    dve.wait_ge(cols_ready, b * 2 + (h + 1))
                nc.vector.tensor_tensor(k_w[:].rearrange("p (h e) -> p h e", h=H),
                                        bank.rearrange("p (h e) -> p h e", h=H),
                                        cols_aw[:, c, 32:32 + H].unsqueeze(2).to_broadcast([T, H, HD]),
                                        ALU.mult).then_inc(emptied, 1)

            def weigh_scores(b, h, c):
                dve.wait_ge(masked, tile_of(b, h, c) + 1)
                for j in range(2):
                    dve.wait_ge(sc_filled[j], sc_use(b, h, c, 2))
                    nc.vector.tensor_tensor(dec[:, j], sc_ps[:, j, :].rearrange("p (i t) -> p i t", i=PAIRS),
                                            dec[:, j], ALU.mult).then_inc(sc_emptied[j], 1)

            def v_copy(kind, b, h, c):
                bank, emptied = filled(kind, b, ("v", h, c))
                dst = v_sb[:, HD + 1:].rearrange("p (h w) -> p h w", h=H)[:, :, 0:HD]
                nc.vector.tensor_tensor(dst, bank.rearrange("p (h d) -> p h d", h=H),
                                        bv_all[:].rearrange("p (h d) -> p h d", h=H), ALU.add).then_inc(emptied, 1)

            def divide_and_gate(kind, b, h, c):
                t = tile_of(b, h, c)
                used = [0]

                def link(ins):
                    used[0] += 1
                    ins.then_inc(dve_tile_step, 1)
                    dve.wait_ge(dve_tile_step, t * TILE_STEPS + used[0])

                dve.wait_ge(num_filled, t + 1)
                num = num_ps[:, :, 0:4 * (HD + 1)].rearrange("p j (i w) -> p j i w", i=4)
                link(nc.vector.tensor_scalar(den[:], num[:, :, :, HD], 1.0, None, ALU.max))
                link(nc.vector.reciprocal(den[:], den[:]))
                assert used[0] == TILE_STEPS
                nc.vector.tensor_tensor(hid[c][:].rearrange("p (j i) d -> p j i d", j=2), num[:, :, :, 0:HD],
                                        den[:].unsqueeze(3).to_broadcast([T, 2, 4, HD]),
                                        ALU.mult).then_inc(num_emptied, 1)
                dve.wait_ge(num_emptied, t + 2)
                obank, before = ring_use(kind, b, ("o", h, c))
                dve.wait_ge(ring_emptied[obank], before + 1)
                flat = hid[c][:].rearrange("p h d -> p (h d)")
                nc.vector.scalar_tensor_tensor(out=flat, in0=th_o[c][:], scalar=1.0, in1=flat, op0=ALU.add,
                                               op1=ALU.mult).then_inc(gated[c], 1)

            def update_state(b, h, c):
                for j in range(2):
                    dve.wait_ge(sc_filled[j], sc_use(b, h, c, 3))
                    for i in range(2):
                        pr = 2 * j + i
                        for s in range(2):
                            p = slice(s * HD, (s + 1) * HD)
                            w = slice(s * (HD + 1), (s + 1) * (HD + 1))
                            ins = nc.vector.scalar_tensor_tensor(
                                out=state[p, pr, w], in0=state[p, pr, w], scalar=carry[p, pr:pr + 1],
                                in1=sc_ps[p, j, i * PW + s * (HD + 1):i * PW + (s + 1) * (HD + 1)],
                                op0=ALU.mult, op1=ALU.add)
                    ins.then_inc(sc_emptied[j], 1)

            def head_stats(b, h, c):
                dve.wait_ge(gated[c], b * 2 + (h + 2))
                for i in range(H):
                    ins = nc.vector.bn_stats(mh_st[:, i, :], hid[c][:, i, :])
                ins.then_inc(mh_stats_ready, 1)

            def gate_out(b, h, c):
                dve.wait_ge(normed, tile_of(b, h, c) + 1)
                flat = hid[c][:].rearrange("p h d -> p (h d)")
                nc.vector.tensor_tensor(flat, flat, sr[c][:], ALU.mult).then_inc(out_ready[c], 1)

            def result(kind, b, h, c):
                bank, emptied = filled(kind, b, ("down", h, c))
                dve.wait_ge(base_ready, b * 2 + (h + 1))
                nc.vector.tensor_tensor(base[h][:, c, :], bank[:, 0:D], base[h][:, c, :], ALU.add).then_inc(emptied, 1)

            def front_gates(kind, b, r, n, h, link):
                gate_rows(kind, b, r, n, h, link)
                parts(m_parts, row_M[:], link)
                dve.wait_ge(exp_rows_ready, 2 * n + 2)
                parts(g_parts, row_g[:], link)

            def front_end(kind, b, r, n, between):
                k_copy(kind, b, r, 0)
                ffn_gate(kind, b, r)
                between()
                k_copy(kind, b, r, 1)
                cols_copy(kind, b, r, n)

            def body(b, last):
                kind = "last" if last else "body"
                reset_state(b)
                for h in range(2):
                    n = b * 2 + h
                    front = not (last and h == 1)
                    h2 = (h + 1) % 2
                    used = [0]
                    link = front_link(n + 1, used)
                    if front:
                        x_stats(n + 1, link)
                    for c in range(2):
                        silu_r(kind, b, h, c)
                        if c == 1 and front:
                            x_normalise(kind, n + 1)
                        skip(kind, b, h, c)
                        q_decayed(kind, b, h, c)
                        k_weighted(kind, b, h, c)
                        weigh_scores(b, h, c)
                        if c == 1 and front:
                            x_low(kind, b, h + 1, n + 1, h2)
                        v_copy(kind, b, h, c)
                        if c == 1:
                            gate_out(b, h, 0)
                            if front:
                                mix(n + 1)
                        divide_and_gate(kind, b, h, c)
                        if c == 1 and front:
                            mix_low(n + 1, 0)
                        head_stats(b, h, c)
                        if c == 0:
                            update_state(b, h, 0)
                    gt_low(kind, b, h, 0)
                    if front:
                        conv_silu(kind, b, h + 1, n + 1)
                        mix_low(n + 1, 1)
                        conv_low(n + 1)
                    if h == 0:
                        update_state(b, 0, 1)
                    result(kind, b, h, 0)
                    if front:
                        front_gates(kind, b, h + 1, n + 1, h2, link)
                    gate_out(b, h, 1)
                    if front:
                        front_end(kind, b, h + 1, n + 1, lambda: gt_low(kind, b, h, 1))
                        assert used[0] == FRONT_STEPS, used
                    else:
                        gt_low(kind, b, h, 1)
                    result(kind, b, h, 1)

            for c in range(2):
                dve.sem_inc(sc_emptied[c], 1)
                dve.sem_inc(gated[c], 1)
                dve.sem_inc(out_ready[c], 1)
                dve.sem_inc(out_stored[c], 16)
            dve.sem_inc(num_emptied, 1)
            used = [0]
            link = front_link(0, used)
            x_stats(0, link)
            x_normalise("first", 0)
            nc.vector.memset(rows_aw[:], 0.0)
            nc.vector.memset(m_parts[:], 0.0)
            nc.vector.memset(g_parts[:], 0.0)
            nc.vector.memset(row_m[0][:, 0:1], 0.0)
            nc.vector.memset(v_sb[:], 0.0).then_inc(buffers_cleared, 1)
            dve.wait_ge(buffers_cleared, 1)
            nc.vector.memset(v_sb[:, HD + 1:].rearrange("p (h w) -> p h w", h=H)[:, :, HD:HD + 1],
                             1.0).then_inc(buffers_ready, 1)
            x_low("first", 0, 0, 0, 0)
            mix(0)
            mix_low(0, 0)
            conv_silu("first", 0, 0, 0)
            mix_low(0, 1)
            conv_low(0)
            front_gates("first", 0, 0, 0, 0, link)
            front_end("first", 0, 0, 0, lambda: None)
            with dve.Fori(0, B - 1) as b:
                body(b, False)
            body(B - 1, True)


_INS = ["L0_attn_x", "L0_attn_ln_g", "L0_attn_ln_b", "L0_attn_mh_g", "L0_attn_mh_b", "L0_attn_W_up_l",
        "L0_attn_b_up_l", "L0_attn_W_up_r", "L0_attn_b_up_r", "L0_attn_W_down", "L0_attn_b_down",
        "L0_attn_conv_w", "L0_attn_conv_b", "L0_attn_W_skip", "L0_attn_b_skip", "L0_attn_W_i", "L0_attn_b_i",
        "L0_attn_W_f", "L0_attn_b_f", "L0_attn_W_o", "L0_attn_b_o", "L0_attn_W_q", "L0_attn_b_q",
        "L0_attn_W_k", "L0_attn_b_k", "L0_attn_W_v", "L0_attn_b_v", "L0_ffn_W_r", "L0_ffn_W_k", "L0_ffn_W_v",
        "L0_ffn_mu_r", "L0_ffn_mu_k"]


def kernel(**inputs):
    import numpy as _np
    import concourse.bacc as _bacc
    from concourse import mybir as _mybir
    from concourse.bass_utils import run_bass_kernel_spmd as _run

    nc = _bacc.Bacc("TRN2", target_bir_lowering=False, num_devices=1)
    arrays, args = {}, []
    for name in _INS:
        a = _np.ascontiguousarray(inputs[name])
        arrays[f"in_{name}_dram"] = a
        args.append(nc.dram_tensor(f"in_{name}_dram", a.shape, _mybir.dt.from_np(a.dtype), kind="ExternalInput").ap())
    out = nc.dram_tensor("out_0_dram", arrays["in_L0_attn_x_dram"].shape, _mybir.dt.float32,
                         kind="ExternalOutput").ap()
    mlstm_rwkv_block(nc, *args, out)
    r = _run(nc, [arrays], core_ids=[0])
    return r.results[0]["out_0_dram"]
```

```python
from contextlib import ExitStack

import concourse.bass as bass
from concourse import mybir

F32 = mybir.dt.float32
F32R = mybir.dt.float32r
BF16 = mybir.dt.bfloat16
ALU = mybir.AluOpType
ACT = mybir.ActivationFunctionType

EPS_OUTER = 1e-5
EPS_ATTN = 1e-6
CAP = 15.0
TAPS = 4

RING = 4
FRONT = ["conv0", "conv1", "ffn_k", "ffn_r", "o", "gates", "q0", "q1", "k0", "ffn_v", "k1", "cols"]
HALF_END = [("gt", 0), None, None, None, ("down", 0), None, None, None, None, None, None, None, ("gt", 1), None, None,
            ("down", 1)]


def ring_order(kind):
    if kind == "first":
        return [(p, 0, 0) for p in ["xf", "xa"] + FRONT]
    out = []
    for h in range(2):
        front = kind == "body" or h == 0
        out += [(p, h, 0) for p in ("r", "skip", "decay", "kt", "v")]
        out += [(p, h, 1) for p in ("o", "r", "skip", "decay", "kt")]
        out += [(p, h + 1, 0) for p in ("xf", "xa")] if front else []
        out += [("v", h, 1)]
        ahead = iter(FRONT)
        for end in HALF_END:
            if end:
                out += [(end[0], h, end[1])]
            elif front:
                out += [(next(ahead), h + 1, 0)]
    return out


def ring_places(kind):
    at, out = [0] * RING, {}
    for i, use in enumerate(ring_order(kind)):
        out[use] = (i % RING, at[i % RING])
        at[i % RING] += 1
    return out, at


FIRST_PLACES, FIRST_USES = ring_places("first")
BODY_PLACES, BODY_USES = ring_places("body")
LAST_PLACES, _ = ring_places("last")


def ring_use(kind, b, use):
    if kind == "first":
        return FIRST_PLACES[use]
    bank, before = (BODY_PLACES if kind == "body" else LAST_PLACES)[use]
    return bank, b * BODY_USES[bank] + (FIRST_USES[bank] + before)


def mlstm_rwkv_block(nc, x, ln_g, ln_b, mh_g, mh_b, W_up_l, b_up_l, W_up_r, b_up_r, W_down, b_down,
                     conv_w, conv_b, W_skip, b_skip, W_i, b_i, W_f, b_f, W_o, b_o, W_q, b_q, W_k, b_k,
                     W_v, b_v, F_r, F_k, F_v, mu_r, mu_k, out):
    B, S, D = x.shape
    P = W_up_l.shape[0]
    H, HD = mh_g.shape
    HID = H * HD
    T = 128
    KD, KP = D // T, P // T
    HALF = 2 * T
    HALVES = S // HALF
    PAIRS = H // 2
    PW = 2 * (HD + 1)
    assert HALVES == 2 and D == 256 and P == 512 and HID == 512 and HD == 64 and H == 8

    x_dram = x.rearrange("b (h c p) d -> (b h) p c d", c=2, p=T)
    out_dram = out.rearrange("b (t p) d -> (b t) p d", p=T)

    keep = ExitStack()
    with keep:
        def sb(name, shape, dt=F32, stack=keep):
            return stack.enter_context(nc.sbuf_tensor(name, shape, dt))

        def sem(name):
            return keep.enter_context(nc.semaphore(name))

        ring = keep.enter_context(nc.psum_tensor("ring", [T, RING, 512], F32))
        sc_ps = keep.enter_context(nc.psum_tensor("sc_ps", [T, 2, 512], F32))
        num_ps = keep.enter_context(nc.psum_tensor("num_ps", [T, 2, 512], F32))

        def halves(name, shape):
            return sb(name + "_hi", shape, F32R), sb(name + "_lo", shape, F32R)

        wc = halves("wc", [T, KD, P])
        wv = halves("wv", [T, KD, HID])
        wo = halves("wo", [T, KD, HID])
        wr = halves("wr", [T, KD, HID])
        wq = halves("wq", [T, KP, HID])
        wk = halves("wk", [T, KP, HID])
        ws = halves("ws", [T, KP, HID])
        LOW = 64
        wif = sb("wif", [T, KP, LOW + 40], F32R)
        wd = halves("wd", [T, KP, D])
        fr = halves("fr", [T, KD, D])
        fk = halves("fk", [T, KD, D])
        fv = halves("fv", [T, KD, D])

        ident = sb("ident", [T, T])
        sel = sb("sel", [72, H * T], BF16)
        bo_all = sb("bo_all", [T, HID])
        br_all = sb("br_all", [T, HID])
        bv_all = sb("bv_all", [T, HID])
        bs_all = sb("bs_all", [T, HID])
        mhg_all = sb("mhg_all", [T, HID])
        bd_all = sb("bd_all", [T, D])
        q_bias = sb("q_bias", [T, KP])
        k_bias = sb("k_bias", [T, KP])
        conv_bias = sb("conv_bias", [T, KP])
        if_bias = sb("if_bias", [H, 2])
        mu = sb("mu", [T, 2, KD])
        one_mu = sb("one_mu", [T, 2, KD])
        chunk_keep = sb("chunk_keep", [H, HALF], BF16)
        zero2 = sb("zero2", [T, KD, 1])
        minus_half = sb("minus_half", [T, H])
        xin = sb("xin", [T, 2, D])
        ln_st = sb("ln_st", [T, 2, 6])
        ln_mv = sb("ln_mv", [T, 2, 2])
        ln_sc = sb("ln_sc", [T, 4, 2])

        small_loaded = sem("small_loaded")
        rows_loaded = sem("rows_loaded")
        up_bias_loaded = sem("up_bias_loaded")
        ln_b_ready = sem("ln_b_ready")
        pool_prep = sem("pool_prep")
        conv_bias_folded = sem("conv_bias_folded")
        x_loaded = sem("x_loaded")
        const_ready = sem("const_ready")
        dve_prep = sem("dve_prep")
        prep_filled = sem("prep_filled")
        prep_hi = sem("prep_hi")
        prep_act = sem("prep_act")
        prep_dve = sem("prep_dve")

        stats_step = sem("stats_step")
        stats_ready = sem("stats_ready")
        scale_step = sem("scale_step")
        scale_ready = sem("scale_ready")
        dve_settled = sem("dve_settled")
        pool_settled = sem("pool_settled")
        SCALE_STEPS = 6

        def settle(eng, count):
            eng.sem_inc(count, 1)

        def x_stats(dve, n):
            dve.wait_ge(x_loaded, 16 * n + 16)
            nc.vector.bn_stats(ln_st[:, 0, :], xin[:, 0, :])
            nc.vector.bn_stats(ln_st[:, 1, :], xin[:, 1, :]).then_inc(stats_step, 1)
            dve.wait_ge(stats_step, n + 1)
            settle(dve, dve_settled)
            nc.vector.bn_aggr(ln_mv[:, 0, :], ln_st[:, 0, :])
            nc.vector.bn_aggr(ln_mv[:, 1, :], ln_st[:, 1, :]).then_inc(stats_ready, 1)

        def front_scale(pool, n):
            k = [0]

            def link(ins):
                k[0] += 1
                ins.then_inc(scale_step, 1)
                pool.wait_ge(scale_step, n * SCALE_STEPS + k[0])

            pool.wait_ge(stats_ready, n + 1)
            settle(pool, pool_settled)
            var = ln_mv[:, :, 1]
            rstd, t, both, e = (ln_sc[:, i, :] for i in range(4))
            link(nc.gpsimd.tensor_scalar(t, var, EPS_OUTER, None, ALU.add))
            link(nc.gpsimd.tensor_tensor(rstd, t, minus_half[:, 0:2], ALU.pow))
            link(nc.gpsimd.tensor_tensor(t, rstd, rstd, ALU.mult))
            link(nc.gpsimd.tensor_tensor(t, t, var, ALU.mult))
            settle(pool, pool_settled)
            link(nc.gpsimd.tensor_scalar(t, t, EPS_ATTN, None, ALU.add))
            link(nc.gpsimd.tensor_tensor(e, t, minus_half[:, 0:2], ALU.pow))
            assert k[0] == SCALE_STEPS
            nc.gpsimd.tensor_tensor(both, rstd, e, ALU.mult).then_inc(scale_ready, 1)

        prep = ExitStack()
        with prep:
            def tmp(name, shape, dt=F32):
                return sb(name, shape, dt, prep)

            ul = tmp("ul", [T, KP, D])
            SLOTS = 5
            stage = tmp("stage", [T, SLOTS, KP * P])
            wt = tmp("wt", [T, KP, HID])
            wt2 = tmp("wt2", [T, KP, HID])
            ult = tmp("ult", [T, KD, 3 + P])
            bl = tmp("bl", [T, 3 + P])
            bl_t = tmp("bl_t", [T, KP, T])
            lnb_rep = tmp("lnb_rep", [T, KD, T])
            lng = tmp("lng", [T, KD])
            lnb = tmp("lnb", [T, KD])
            cw = tmp("cw", [T, TAPS])
            cb = tmp("cb", [T, 1])
            fold = tmp("fold", [T, P])
            tap = tmp("tap", [T, P])
            bup_l_all = tmp("bup_l_all", [T, P])
            ones = tmp("ones", [T, T])
            b0_all = tmp("b0_all", [T, 3, HID])
            mhb_all = tmp("mhb_all", [T, HID])

            def turns(last, *whats):
                return [(what, int(which), last) for what, which in (w.split(":") for w in whats)]

            TURNS = turns("dve", "ult:0", "ult:1")
            TURNS += turns("split", "wt_q:0", "wt_q:1", "wt_q:2", "wt_q:3", "wt_k:0", "wt_k:1", "wt_k:2", "wt_k:3")
            TURNS += turns("dve", "bl:0") + turns("act", "wt_v:0", "wt_v:1", "wt_v:2", "wt_v:3")
            TURNS += turns("dve", "bl_t:0") + turns("act", "wt_o:0", "wt_o:1", "wt_o:2", "wt_o:3")
            TURNS += turns("split", "fold_v:0", "wt_s:0", "wt_s:1", "fold_v:1", "wt_s:2", "wt_s:3")
            TURNS += turns("dve", "bias_v:0") + turns("split", "wt_r:0", "wt_r:1", "fold_o:0", "wt_if:0", "wt_d:0")
            TURNS += turns("split", "fold_o:1", "wt_d:1", "wt_fr:0") + turns("dve", "bias_o:0")
            TURNS += turns("split", "wt_fk:0", "wt_fv:0") + turns("dve", "bias_r:0", "conv_bias:0")

            act_count, dve_count, hi_count = [], [], []
            a = d = hi = 0
            for _, _, last in TURNS:
                a += last == "act"
                d += last in ("dve", "split")
                hi += last == "split"
                act_count.append(a)
                dve_count.append(d)
                hi_count.append(hi)

            def turn_of(what, which=0):
                return next(i for i, t in enumerate(TURNS) if t[:2] == (what, which))

            def wait_emptied(eng, i):
                if TURNS[i][2] == "act":
                    eng.wait_ge(prep_act, act_count[i])
                else:
                    eng.wait_ge(prep_dve, dve_count[i])

            STAGED = ["q", "k", "v", "o", "s", "r", "if", "d", "fr", "fk", "fv"]
            SOURCE = {"v": W_v, "o": W_o, "r": W_up_r, "q": W_q, "k": W_k, "s": W_skip, "d": W_down,
                      "fr": F_r, "fk": F_k, "fv": F_v}
            LAST_TURN = {"v": ("wt_v", 3), "o": ("wt_o", 3), "r": ("wt_r", 1), "q": ("wt_q", 3),
                         "k": ("wt_k", 3), "s": ("wt_s", 3), "if": ("wt_if", 0), "d": ("wt_d", 1),
                         "fr": ("wt_fr", 0), "fk": ("wt_fk", 0), "fv": ("wt_fv", 0)}

            def staged(name):
                slot = stage[:, STAGED.index(name) % SLOTS, :]
                if name == "if":
                    return slot[0:40, 0:P]
                o, i = SOURCE[name].shape
                return slot[:, 0:o // T * i].rearrange("p (o i) -> p o i", i=i)

            ul_loaded = sem("ul_loaded")
            stage_loaded = {name: sem("stage_loaded_" + name) for name in STAGED}

            def split_source(what, bank):
                return bank[:, 0:KP * 40].rearrange("p (k o) -> p k o", k=KP) if what == "wt_if" else bank

            def split_target(what, k, part):
                if what == "fold_v":
                    return wv[part][:, k, :], lng[:, k:k + 1]
                if what == "fold_o":
                    return wo[part][:, k, :], lng[:, k:k + 1]
                if what == "wt_r":
                    return wr[part][:, k, :], lng[:, k:k + 1]
                if what == "wt_if":
                    return wif[:, :, LOW * part:LOW * part + 40], 0.5
                if what == "wt_d":
                    return wd[part][:, 2 * k:2 * k + 2, :].rearrange("p k o -> p (k o)"), 0.5
                if what in ("wt_fr", "wt_fk", "wt_fv"):
                    w, scale = {"wt_fr": (fr, 1.0), "wt_fk": (fk, 1.0), "wt_fv": (fv, 0.5)}[what]
                    return w[part][:].rearrange("p k o -> p (k o)"), scale
                w, scale = {"wt_q": (wq, 0.5), "wt_k": (wk, 0.5 / HD ** 0.5), "wt_s": (ws, 0.5)}[what]
                return w[part][:, k, :], scale

            block = prep.enter_context(nc.Block())

            @block.sync
            def _(sp):
                def rows(v):
                    return v.partition_broadcast(T)

                sp.dma_start(ul[:], W_up_l.rearrange("(o p) i -> p o i", p=T)).then_inc(ul_loaded, 16)
                for k, name in enumerate(STAGED):
                    if name == "v":
                        sp.wait_ge(small_loaded, 160)
                        sp.dma_start(bup_l_all[:], rows(b_up_l)).then_inc(up_bias_loaded, 16)
                    if k == SLOTS:
                        for dst, src in ((b0_all[:, 0, :], b_v), (b0_all[:, 1, :], b_o), (b0_all[:, 2, :], b_up_r),
                                         (bs_all[:], b_skip), (mhb_all[:], mh_b.rearrange("h d -> (h d)")),
                                         (mhg_all[:], mh_g.rearrange("h d -> (h d)")), (bd_all[:], b_down)):
                            sp.dma_start(dst, rows(src)).then_inc(rows_loaded, 16)
                        sp.dma_start(xin[:], x_dram[0]).then_inc(x_loaded, 16)
                    if k >= SLOTS:
                        i = turn_of(*LAST_TURN[STAGED[k - SLOTS]])
                        sp.wait_ge(prep_filled, i + 1)
                    if name == "if":
                        sp.dma_start(staged(name)[0:H, :], W_i).then_inc(stage_loaded[name], 16)
                        sp.dma_start(staged(name)[32:32 + H, :], W_f).then_inc(stage_loaded[name], 16)
                    else:
                        sp.dma_start(staged(name), SOURCE[name].rearrange("(o p) i -> p o i", p=T)
                                     ).then_inc(stage_loaded[name], 16)

            @block.gpsimd
            def _(pool):
                nc.gpsimd.memset(ident[:], 0.0).then_inc(const_ready, 1)
                nc.gpsimd.memset(sel[:], 0.0).then_inc(const_ready, 1)
                pool.wait_ge(const_ready, 2)
                nc.gpsimd.affine_select(out=ident[:], in_=ident[:], compare_op=ALU.not_equal, fill=1.0, base=0,
                                        pattern=[[-1, T]], channel_multiplier=1).then_inc(const_ready, 1)
                for part in range(3):
                    nc.gpsimd.affine_select(out=sel[:], in_=sel[:], compare_op=ALU.not_equal, fill=1.0,
                                            base=-32 * part, pattern=[[-1, H], [0, T]],
                                            channel_multiplier=1).then_inc(const_ready, 1)
                    pool.wait_ge(const_ready, 4 + part)

                steps = [0]

                def link(ins):
                    steps[0] += 1
                    ins.then_inc(pool_prep, 1)
                    pool.wait_ge(pool_prep, steps[0])

                def convolve(src):
                    link(nc.gpsimd.tensor_scalar(fold[:], src[:, 0:P], cw[:, 0:1], 0.0, ALU.mult, ALU.add))
                    for m in range(1, TAPS):
                        link(nc.gpsimd.tensor_scalar(tap[:], src[:, m:m + P], cw[:, m:m + 1], 0.0, ALU.mult, ALU.add))
                        link(nc.gpsimd.tensor_tensor(fold[:], fold[:], tap[:], ALU.add))

                pool.wait_ge(small_loaded, 160)
                for j in range(KD):
                    pool.wait_ge(prep_dve, dve_count[turn_of("ult", j)])
                    convolve(ult[:, j, :])
                    link(nc.gpsimd.tensor_scalar(fold[:], fold[:], lng[:, j:j + 1], 0.0, ALU.mult, ALU.add))
                    link(nc.gpsimd.tensor_scalar(wc[0][:, j, :], fold[:], 1.0, 0.0, ALU.mult, ALU.add))
                    link(nc.gpsimd.tensor_tensor(wc[1][:, j, :], fold[:], wc[0][:, j, :].bitcast(F32), ALU.subtract))
                pool.wait_ge(prep_dve, dve_count[turn_of("bl")])
                convolve(bl[:])
                nc.gpsimd.tensor_scalar(fold[:], fold[:], cb[:, 0:1], 0.0, ALU.add,
                                        ALU.add).then_inc(conv_bias_folded, 1)
                front_scale(pool, 0)

            @block.scalar
            def _(act):
                def col(v, n):
                    return v.rearrange("(k p) -> p k", p=T)

                for dst, src in ((lng[:], col(ln_g, KD)), (lnb[:], col(ln_b, KD)), (mu[:, 0, :], col(mu_r, KD)),
                                 (mu[:, 1, :], col(mu_k, KD)), (q_bias[:], col(b_q, KP)),
                                 (k_bias[:], col(b_k, KP)),
                                 (if_bias[:, 0:1], b_i.rearrange("(h a) -> h a", a=1)),
                                 (if_bias[:, 1:2], b_f.rearrange("(h a) -> h a", a=1)),
                                 (cw[:], conv_w.partition_broadcast(T)),
                                 (cb[:], conv_b.partition_broadcast(T))):
                    act.dma_start(dst, src, allow_slow_non_contiguous=True).then_inc(small_loaded, 16)

                for i, (what, k, last) in enumerate(TURNS):
                    if last == "dve":
                        continue
                    act.wait_ge(prep_filled, i + 1)
                    bank = ring[:, i % RING, :]
                    if last == "split":
                        dst, scale = split_target(what, k, 0)
                        if what in ("fold_v", "fold_o", "wt_r"):
                            act.wait_ge(small_loaded, 160)
                        nc.scalar.activation(dst, split_source(what, bank), ACT.Copy, scale=scale).then_inc(prep_hi, 1)
                        continue
                    w = wt if what == "wt_v" else wt2
                    nc.scalar.activation(w[:, k, :], bank, ACT.Copy).then_inc(prep_act, 1)

            @block.tensor
            def _(pe):
                pe.wait_ge(const_ready, 3)
                for i, (what, k, last) in enumerate(TURNS):
                    if i >= RING:
                        wait_emptied(pe, i - RING)
                    bank = ring[:, i % RING, :]
                    if what == "ult":
                        pe.wait_ge(ul_loaded, 16)
                        for o in range(KP):
                            mm = pe.transpose(bank[:, o * T:(o + 1) * T], ul[:, o, k * T:(k + 1) * T], ident[:])
                    elif what == "bl":
                        pe.wait_ge(ln_b_ready, KD)
                        for j in range(KD):
                            mm = pe.matmul(bank, lnb_rep[:, j, :], ult[:, j, 3:], start=j == 0, stop=j == KD - 1)
                    elif what == "bl_t":
                        pe.wait_ge(prep_dve, dve_count[turn_of("bl")])
                        for o in range(KP):
                            mm = pe.transpose(bank[:, o * T:(o + 1) * T], bl[:, 3 + o * T:3 + (o + 1) * T], ident[:])
                    elif what == "conv_bias":
                        pe.wait_ge(conv_bias_folded, 1)
                        for o in range(KP):
                            mm = pe.transpose(bank[:, o * T:(o + 1) * T], fold[:, o * T:(o + 1) * T], ident[:])
                    elif what in ("fold_v", "fold_o"):
                        pe.wait_ge(prep_act, act_count[turn_of("wt_" + what[-1], KP - 1)])
                        w = wt if what == "fold_v" else wt2
                        for j in range(KP):
                            mm = pe.matmul(bank, ul[:, j, k * T:(k + 1) * T], w[:, j, :],
                                           start=j == 0, stop=j == KP - 1)
                    elif what in ("bias_v", "bias_o"):
                        pe.wait_ge(prep_dve, dve_count[turn_of("bl_t")])
                        w = wt if what == "bias_v" else wt2
                        for j in range(KP):
                            mm = pe.matmul(bank, bl_t[:, j, :], w[:, j, :], start=j == 0, stop=j == KP - 1)
                    elif what == "bias_r":
                        pe.wait_ge(prep_dve, dve_count[turn_of("wt_r", 1)])
                        for j in range(KD):
                            mm = pe.matmul(bank, lnb_rep[:, j, :], wt[:, j, :], start=j == 0, stop=j == KD - 1)
                    else:
                        name = what[3:]
                        src = staged(name)
                        pe.wait_ge(stage_loaded[name], 32 if name == "if" else 16)
                        if name == "if":
                            for j in range(KP):
                                mm = pe.transpose(bank[:, j * 40:(j + 1) * 40], src[:, j * T:(j + 1) * T],
                                                  ident[0:40, 0:40])
                        elif name in ("d", "fr", "fk", "fv"):
                            for j in range(2):
                                for o in range(2):
                                    kk = 2 * k + j
                                    mm = pe.transpose(bank[:, j * D + o * T:j * D + (o + 1) * T],
                                                      src[:, o, kk * T:(kk + 1) * T], ident[:])
                        else:
                            for o in range(KP):
                                mm = pe.transpose(bank[:, o * T:(o + 1) * T], src[:, o, k * T:(k + 1) * T], ident[:])
                    mm.then_inc(prep_filled, 1)

            @block.vector
            def _(dve):
                steps = [0]

                def link(ins):
                    steps[0] += 1
                    ins.then_inc(dve_prep, 1)
                    dve.wait_ge(dve_prep, steps[0])

                nc.vector.memset(ult[:, :, 0:3], 0.0)
                nc.vector.memset(bl[:, 0:3], 0.0)
                nc.vector.memset(zero2[:], 0.0)
                nc.vector.memset(minus_half[:], -0.5)
                nc.vector.memset(wif[:, :, 40:LOW].bitcast(F32), 0.0)
                nc.vector.memset(chunk_keep[:], 1.0)
                link(nc.vector.memset(ones[:], 1.0))
                nc.vector.memset(chunk_keep[:, 0:HALF:T], 0.0)

                def small_vectors():
                    dve.wait_ge(small_loaded, 160)
                    for k in range(KD):
                        nc.vector.tensor_scalar(lnb_rep[:, k, :], ones[:], lnb[:, k:k + 1], None,
                                                ALU.mult).then_inc(ln_b_ready, 1)
                    nc.vector.tensor_scalar(one_mu[:], mu[:], -1.0, 1.0, ALU.mult, ALU.add)
                    nc.vector.tensor_scalar(k_bias[:], k_bias[:], HD ** -0.5, None, ALU.mult)

                for i, (what, k, last) in enumerate(TURNS):
                    if last == "act":
                        continue
                    if (what, k) == ("wt_k", 0):
                        small_vectors()
                    if what == "bias_v":
                        dve.wait_ge(rows_loaded, 7 * 16)
                        nc.vector.tensor_tensor(bs_all[:], bs_all[:], mhb_all[:], ALU.add)
                    if what == "bias_o":
                        x_stats(dve, 0)
                    dve.wait_ge(prep_filled, i + 1)
                    bank = ring[:, i % RING, :]
                    if last == "split":
                        hi_dst, _ = split_target(what, k, 0)
                        lo_dst, scale = split_target(what, k, 1)
                        dve.wait_ge(prep_hi, hi_count[i])
                        if what == "wt_r":
                            nc.vector.tensor_copy(wt[:, k, :], bank)
                        nc.vector.scalar_tensor_tensor(out=lo_dst, in0=split_source(what, bank), scalar=scale,
                                                       in1=hi_dst.bitcast(F32), op0=ALU.mult,
                                                       op1=ALU.subtract).then_inc(prep_dve, 1)
                    elif what == "ult":
                        nc.vector.tensor_copy(ult[:, k, 3:], bank).then_inc(prep_dve, 1)
                    elif what == "bl":
                        dve.wait_ge(up_bias_loaded, 16)
                        nc.vector.tensor_tensor(bl[:, 3:], bank, bup_l_all[:], ALU.add).then_inc(prep_dve, 1)
                    elif what == "bl_t":
                        nc.vector.tensor_copy(bl_t[:].rearrange("p k j -> p (k j)"), bank).then_inc(prep_dve, 1)
                    elif what == "bias_v":
                        nc.vector.tensor_tensor(bv_all[:], bank, b0_all[:, 0, :], ALU.add).then_inc(prep_dve, 1)
                    elif what == "conv_bias":
                        nc.vector.tensor_copy(conv_bias[:], bank[:, 0:KP * T:T]).then_inc(prep_dve, 1)
                    else:
                        dst, i0 = (bo_all, 1) if what == "bias_o" else (br_all, 2)
                        nc.vector.tensor_tensor(dst[:], bank, b0_all[:, i0, :], ALU.add).then_inc(prep_dve, 1)

        xf = sb("xf", [T, 2, D])
        xa = sb("xa", [T, 2, D])
        xa_t = [halves(f"xa_t{h}", [T, KD, HALF]) for h in range(2)]
        xf_t = sb("xf_t", [T, KD, 1 + HALF])

        def in_place_of(name, shape):
            with ExitStack() as place:
                return sb(name, shape, F32, place)

        def whole_and_halves(name, shape):
            hi = sb(name + "_hi", shape, F32R)
            whole = in_place_of(name, shape)
            return whole, (hi, sb(name + "_lo", shape, F32R))

        mix_r, mix_r_halves = whole_and_halves("mix_r", [T, KD, HALF])
        mix_k, mix_k_halves = whole_and_halves("mix_k", [T, KD, HALF])
        kact, kact_halves = whole_and_halves("kact", [T, KD, HALF])
        ffn = xa
        base = [sb(f"base{h}", [T, 2, D]) for h in range(2)]
        conv_tanh = in_place_of("conv_tanh", [T, KP, HALF])
        xc_whole, xc = whole_and_halves("xc", [T, KP, HALF])

        def flat(a):
            return a.rearrange("p k t -> p (k t)")

        conv_act = [flat(xc_whole[:, 2 * j:2 * j + 2, :]) for j in range(2)]
        q_t = sb("q_t", [T, PAIRS, HALF])
        k_t = sb("k_t", [T, PAIRS, HALF])
        q_dec = sb("q_dec", [T, PAIRS, T])
        k_w = sb("k_w", [T, HID])
        th_r = k_w
        dec = sb("dec", [T, 2, PAIRS, T])
        v_sb = sb("v_sb", [T, H * PW + HD + 1])
        th_o = [sb(f"th_o{c}", [T, HID]) for c in range(2)]
        sr = [sb(f"sr{c}", [T, HID]) for c in range(2)]
        sk = [sb(f"sk{c}", [T, HID]) for c in range(2)]
        hid = [sb(f"hid{c}", [T, H, HD]) for c in range(2)]
        gt = halves("gt", [T, KP, T])
        state = sb("state", [T, PAIRS, PW])
        carry = sb("carry", [T, PAIRS])
        den = sb("den", [T, 2, 4])
        mh_st = sb("mh_st", [T, H, 6])
        mh_sc = sb("mh_sc", [T, 5, H])
        row_i = sb("row_i", [H, HALF])
        row_f = sb("row_f", [H, HALF])
        row_F = sb("row_F", [H, HALF])
        row_rem, row_g = row_F, row_i
        row_m = [sb(f"row_m{h}", [H, 1 + HALF]) for h in range(2)]
        row_M = sb("row_M", [H, HALF])
        row_mid = sb("row_mid", [H, HALF], BF16)
        rows_aw = sb("rows_aw", [40, HALF])
        cols_aw = sb("cols_aw", [T, 2, 40])
        m_parts = sb("m_parts", [72, HALF], BF16)
        g_parts = sb("g_parts", [72, HALF], BF16)

        x_used = sem("x_used")
        xh_ready = sem("xh_ready")
        xa_hi_ready = sem("xa_hi_ready")
        xf_t_carried = sem("xf_t_carried")
        mix_prev_ready = sem("mix_prev_ready")
        mix_ready = sem("mix_ready")
        mix_hi_ready = sem("mix_hi_ready")
        mix_lo_ready = sem("mix_lo_ready")
        kact_ready = sem("kact_ready")
        kact_hi_ready = sem("kact_hi_ready")
        kact_lo_ready = sem("kact_lo_ready")
        gt_hi_ready = sem("gt_hi_ready")
        base_ready = sem("base_ready")
        xc_hi_ready = sem("xc_hi_ready")
        xc_lo_ready = sem("xc_lo_ready")
        gates_low_ready = sem("gates_low_ready")
        gates_ready = sem("gates_ready")
        exp_args_ready = sem("exp_args_ready")
        exp_rows_ready = sem("exp_rows_ready")
        parts_ready = sem("parts_ready")
        sc_filled = [sem(f"sc_filled{j}") for j in range(2)]
        sc_emptied = [sem(f"sc_emptied{j}") for j in range(2)]
        masked = sem("masked")
        num_filled = sem("num_filled")
        num_emptied = sem("num_emptied")
        state_reset = sem("state_reset")
        cols_ready = sem("cols_ready")
        r_tanh_ready = sem("r_tanh_ready")
        o_tanh_ready = sem("o_tanh_ready")
        silu_ready = sem("silu_ready")
        conv_tanh_ready = sem("conv_tanh_ready")
        conv_ready = sem("conv_ready")
        gated = [sem(f"gated{c}") for c in range(2)]
        mh_stats_ready = sem("mh_stats_ready")
        skip_gated = sem("skip_gated")
        gain_ready = sem("gain_ready")
        out_ready = [sem(f"out_ready{c}") for c in range(2)]
        out_stored = [sem(f"out_stored{c}") for c in range(2)]
        buffers_cleared = sem("buffers_cleared")
        buffers_ready = sem("buffers_ready")
        pe_settled = sem("pe_settled")
        state_cleared = sem("state_cleared")
        ring_filled = [sem(f"ring_filled{j}") for j in range(RING)]
        ring_emptied = [sem(f"ring_emptied{j}") for j in range(RING)]
        dve_front_step = sem("dve_front_step")
        den_ready = sem("den_ready")
        state_decayed = sem("state_decayed")
        base_step = sem("base_step")
        pool_tile_step = sem("pool_tile_step")

        SC_USES = 3 * 4 - 1

        def sc_use(b, h, c, k):
            return b * SC_USES + (3 * (2 * h + c) + k)

        def sc_free(b, h, c, k):
            return b * SC_USES + (3 * (2 * h + c) + k + 1)

        def tile_of(b, h, c):
            return b * 4 + (2 * h + c)

        main = nc.Block()
        block = keep.enter_context(main)

        @block.sync
        def _(sp):
            def load_x(n):
                sp.wait_ge(x_used, n)
                sp.dma_start(xin[:], x_dram[n]).then_inc(x_loaded, 16)

            def body(b, last):
                for h in range(2):
                    if not last:
                        load_x(b * 2 + (h + 2))
                    for c in range(2):
                        bank, before = ring_use("last" if last else "body", b, ("down", h, c))
                        sp.wait_ge(ring_emptied[bank], before + 1)
                        sp.dma_start(out_dram[tile_of(b, h, c)], base[h][:, c, :]).then_inc(out_stored[c], 16)

            load_x(1)
            with sp.Fori(0, B - 1) as b:
                body(b, False)
            body(B - 1, True)
            for c in range(2):
                sp.wait_ge(out_stored[c], 16 * (2 * B + 1))

        @block.tensor
        def _(pe):
            def take(kind, b, use):
                bank, before = ring_use(kind, b, use)
                pe.wait_ge(ring_emptied[bank], before)
                return ring[:, bank, :], ring_filled[bank]

            def emptied(kind, b, use):
                bank, before = ring_use(kind, b, use)
                pe.wait_ge(ring_emptied[bank], before + 1)

            def transposes_x(kind, b, r, n):
                pe.wait_ge(xh_ready, n + 1)
                for use, src in (("xf", xf), ("xa", xa)):
                    bank, filled = take(kind, b, (use, r, 0))
                    for k in range(KD):
                        for c in range(2):
                            mm = pe.transpose(bank[:, k * HALF + c * T:k * HALF + (c + 1) * T],
                                              src[:, c, k * T:(k + 1) * T], ident[:])
                    mm.then_inc(filled, 1)

            def three(dst, w, act, first, last):
                pe.matmul(dst, w[0], act[0], start=first, stop=False, skip_group_check=True)
                pe.matmul(dst, w[0], act[1], start=False, stop=False, skip_group_check=True)
                return pe.matmul(dst, w[1], act[0], start=False, stop=last, skip_group_check=True)

            def conv(kind, b, r, h):
                emptied(kind, b, ("xa", r, 0))
                for j in range(2):
                    bank, filled = take(kind, b, (f"conv{j}", r, 0))
                    for m in range(2):
                        f = slice((2 * j + m) * T, (2 * j + m + 1) * T)
                        dst = bank[:, m * HALF:(m + 1) * HALF]
                        for k in range(KD):
                            mm = three(dst, [w[:, k, f] for w in wc], [a[:, k, :] for a in xa_t[h]],
                                       m == 0 and k == 0, k == KD - 1)
                    mm.then_inc(filled, 1)

            def ffn_k(kind, b, r, n):
                pe.wait_ge(mix_lo_ready, 2 * n + 1)
                bank, filled = take(kind, b, ("ffn_k", r, 0))
                for m in range(KD):
                    for k in range(KD):
                        mm = three(bank[:, m * HALF:(m + 1) * HALF], [w[:, k, m * T:(m + 1) * T] for w in fk],
                                   [a[:, k, :] for a in mix_k_halves], k == 0 and m == 0, k == KD - 1)
                mm.then_inc(filled, 1)

            def ffn_tokens(kind, b, r, use, act, w):
                bank, filled = take(kind, b, (use, r, 0))
                for c in range(2):
                    for k in range(KD):
                        mm = three(bank[:, c * D:(c + 1) * D], [a[:, k, c * T:(c + 1) * T] for a in act],
                                   [p[:, k, :] for p in w], k == 0 and c == 0, k == KD - 1)
                mm.then_inc(filled, 1)

            def ffn_r(kind, b, r, n):
                pe.wait_ge(mix_lo_ready, 2 * n + 2)
                ffn_tokens(kind, b, r, "ffn_r", mix_r_halves, fr)

            def gates(kind, b, r, n):
                pe.wait_ge(xc_lo_ready, 2 * (n + 1))
                bank, filled = take(kind, b, ("gates", r, 0))
                for k in range(KP):
                    pe.matmul(bank[0:LOW + 40, 0:HALF], wif[:, k, :], xc[0][:, k, :], start=k == 0, stop=False,
                              skip_group_check=True)
                    mm = pe.matmul(bank[0:40, 0:HALF], wif[:, k, 0:40], xc[1][:, k, :], start=False,
                                   stop=k == KP - 1, skip_group_check=True)
                mm.then_inc(filled, 1)

            def heads(kind, b, r, use, w, j):
                bank, filled = take(kind, b, (f"{use}{j}", r, 0))
                for m in range(2):
                    f = slice((2 * j + m) * T, (2 * j + m + 1) * T)
                    for k in range(KP):
                        mm = three(bank[:, m * HALF:(m + 1) * HALF], [p[:, k, f] for p in w],
                                   [a[:, k, :] for a in xc], m == 0 and k == 0, k == KP - 1)
                mm.then_inc(filled, 1)

            def cols(kind, b, r, n):
                pe.wait_ge(exp_rows_ready, 2 * n + 1)
                bank, filled = take(kind, b, ("cols", r, 0))
                settle(pe, pe_settled)
                for c in range(2):
                    mm = pe.transpose(bank[:, c * 40:(c + 1) * 40], rows_aw[:, c * T:(c + 1) * T], ident[0:40, 0:40])
                mm.then_inc(filled, 1)

            def tokens(kind, b, h, c, use, act, w, nk):
                bank, filled = take(kind, b, (use, h, c))
                t = slice(c * T, (c + 1) * T)
                for k in range(nk):
                    lhs = [a[:, k, t] for a in act]
                    pe.matmul(bank, lhs[0], w[0][:, k, :], start=k == 0, stop=False)
                    pe.matmul(bank, lhs[0], w[1][:, k, :], start=False, stop=False)
                    mm = pe.matmul(bank, lhs[1], w[0][:, k, :], start=False, stop=k == nk - 1)
                mm.then_inc(filled, 1)

            def maxima(b, h, c, n):
                pe.wait_ge(parts_ready, 2 * n + 1)
                for j in range(2):
                    pe.wait_ge(sc_emptied[j], sc_free(b, h, c, 0))
                    for i in range(4):
                        mm = pe.matmul(sc_ps[:, j, i * T:(i + 1) * T], sel[:, (2 * i + j) * T:(2 * i + j + 1) * T],
                                       m_parts[:, c * T:(c + 1) * T], start=i == 0, stop=True, skip_group_check=True)
                    mm.then_inc(sc_filled[j], 1)

            def scores(b, h, c):
                t = slice(c * T, (c + 1) * T)
                for j in range(2):
                    pe.wait_ge(sc_emptied[j], sc_free(b, h, c, 1))
                for i in range(PAIRS):
                    for j in range(2):
                        p = slice(HD * j, HD * (j + 1))
                        mm = pe.matmul(sc_ps[:, j, i * T:(i + 1) * T], k_t[p, i, t], q_t[p, i, t],
                                       start=i == 0, stop=True, skip_group_check=True)
                        if i == PAIRS - 1:
                            mm.then_inc(sc_filled[j], 1)

            def decay(kind, b, h, c, n):
                pe.wait_ge(parts_ready, 2 * n + 2)
                bank, filled = take(kind, b, ("decay", h, c))
                for j in range(PAIRS):
                    at = 2 * j * T + HD
                    mm = pe.matmul(bank[:, j * T:(j + 1) * T], sel[:, at:at + T], g_parts[:, c * T:(c + 1) * T],
                                   start=j == 0, stop=True, skip_group_check=True)
                mm.then_inc(filled, 1)

            def k_tokens(kind, b, h, c):
                bank, filled = take(kind, b, ("kt", h, c))
                for j in range(PAIRS):
                    mm = pe.transpose(bank[:, j * T:(j + 1) * T], k_t[:, j, c * T:(c + 1) * T], ident[:])
                mm.then_inc(filled, 1)

            def numerators(kind, b, h, c):
                t = tile_of(b, h, c)
                if h == 0 and c == 0:
                    pe.wait_ge(state_reset, b + 1)
                pe.wait_ge(num_emptied, t + 1)
                emptied(kind, b, ("decay", h, c))
                for j in range(PAIRS):
                    pe.matmul(num_ps[:, j // 2, j % 2 * PW:(j % 2 + 1) * PW], q_dec[:, j, :], state[:, j, :],
                              start=j % 2 == 0, stop=False, skip_group_check=True)
                emptied(kind, b, ("v", h, c))
                for i in range(2):
                    pe.wait_ge(sc_emptied[i], sc_free(b, h, c, 2))
                    for j in range(PAIRS):
                        hd = 2 * j + i
                        at = (HD + 1) + PW * hd - (HD + 1) * i
                        mm = pe.matmul(num_ps[:, j // 2, j % 2 * PW:(j % 2 + 1) * PW], dec[:, i, j, :],
                                       v_sb[:, at:at + PW], start=False, stop=i == 1, skip_group_check=True)
                mm.then_inc(num_filled, 1)

            def state_update(kind, b, h, c):
                emptied(kind, b, ("kt", h, c))
                for j in range(2):
                    for i in range(2):
                        pr = 2 * j + i
                        at = (HD + 1) + PW * 2 * pr
                        rhs = v_sb[:, at:at + 2 * PW].rearrange("p (s w) -> p s w", s=2)[:, :, 0:HD + 1]
                        mm = pe.matmul(sc_ps[:, j, i * PW:(i + 1) * PW], k_w[:, pr * T:(pr + 1) * T], rhs,
                                       start=i == 0, stop=True, skip_group_check=True)
                    mm.then_inc(sc_filled[j], 1)

            def gt_transposes(kind, b, h, c, n):
                pe.wait_ge(out_ready[c], n + 1)
                bank, filled = take(kind, b, ("gt", h, c))
                src = hid[c][:].rearrange("p h d -> p (h d)")
                for j in range(KP):
                    mm = pe.transpose(bank[:, j * T:(j + 1) * T], src[:, j * T:(j + 1) * T], ident[:])
                mm.then_inc(filled, 1)

            def down(kind, b, h, c):
                emptied(kind, b, ("gt", h, c))
                bank, filled = take(kind, b, ("down", h, c))
                for k in range(KP):
                    mm = three(bank[:, 0:D], [a[:, k, :] for a in gt], [w[:, k, :] for w in wd], k == 0, k == KP - 1)
                mm.then_inc(filled, 1)

            def ffn_v(kind, b, r, n):
                pe.wait_ge(kact_lo_ready, n + 1)
                ffn_tokens(kind, b, r, "ffn_v", kact_halves, fv)

            def half_end(kind, b, h, n):
                front = kind != "last" or h == 0
                ahead = (kind, b, h + 1)
                gt_transposes(kind, b, h, 0, n)
                if front:
                    conv(*ahead, (h + 1) % 2)
                    ffn_k(*ahead, n + 1)
                down(kind, b, h, 0)
                if front:
                    ffn_r(*ahead, n + 1)
                    tokens(*ahead, 0, "o", xa_t[(h + 1) % 2], wo, KD)
                    gates(*ahead, n + 1)
                    heads(*ahead, "q", wq, 0)
                    heads(*ahead, "q", wq, 1)
                    heads(*ahead, "k", wk, 0)
                    ffn_v(*ahead, n + 1)
                gt_transposes(kind, b, h, 1, n)
                if front:
                    heads(*ahead, "k", wk, 1)
                    cols(*ahead, n + 1)
                down(kind, b, h, 1)

            def first_front():
                first = ("first", 0, 0)
                transposes_x(*first, 0)
                conv(*first, 0)
                ffn_k(*first, 0)
                ffn_r(*first, 0)
                tokens(*first, 0, "o", xa_t[0], wo, KD)
                gates(*first, 0)
                heads(*first, "q", wq, 0)
                heads(*first, "q", wq, 1)
                heads(*first, "k", wk, 0)
                ffn_v(*first, 0)
                heads(*first, "k", wk, 1)
                cols(*first, 0)

            def body(b, last):
                kind = "last" if last else "body"
                for h in range(2):
                    n = b * 2 + h
                    front = not (last and h == 1)
                    for c in range(2):
                        if c == 1:
                            tokens(kind, b, h, c, "o", xa_t[h], wo, KD)
                        tokens(kind, b, h, c, "r", xa_t[h], wr, KD)
                        maxima(b, h, c, n)
                        tokens(kind, b, h, c, "skip", xc, ws, KP)
                        decay(kind, b, h, c, n)
                        k_tokens(kind, b, h, c)
                        if c == 0:
                            tokens(kind, b, h, 0, "v", xa_t[h], wv, KD)
                        scores(b, h, c)
                        if c == 1:
                            if front:
                                transposes_x(kind, b, h + 1, n + 1)
                            tokens(kind, b, h, 1, "v", xa_t[h], wv, KD)
                        numerators(kind, b, h, c)
                        if not (h == 1 and c == 1):
                            state_update(kind, b, h, c)
                    half_end(kind, b, h, n)

            first_front()
            pe.wait_ge(buffers_ready, 1)
            with pe.Fori(0, B - 1) as b:
                body(b, False)
            body(B - 1, True)

        @block.scalar
        def _(act):
            def filled(kind, b, use):
                bank, before = ring_use(kind, b, use)
                act.wait_ge(ring_filled[bank], before + 1)
                return ring[:, bank, :], ring_emptied[bank]

            def front_x(kind, b, r, n, h):
                if kind != "first":
                    act.wait_ge(mix_ready, n)
                prev = zero2[:] if h == 0 else xf_t[:, :, HALF:HALF + 1]
                nc.scalar.activation(xf_t[:, :, 0:1], prev, ACT.Copy).then_inc(xf_t_carried, 1)
                bank, emptied = filled(kind, b, ("xf", r, 0))
                act.wait_ge(xf_t_carried, n + 1)
                nc.scalar.activation(xf_t[:, :, 1:1 + HALF], bank.rearrange("p (k t) -> p k t", k=KD),
                                     ACT.Copy).then_inc(emptied, 1)
                bank, _ = filled(kind, b, ("xa", r, 0))
                nc.scalar.activation(xa_t[h][0][:].rearrange("p k t -> p (k t)"), bank,
                                     ACT.Copy).then_inc(xa_hi_ready, 1)

            def front_mix_prev(kind, b, r, n):
                bank, before = ring_use(kind, b, ("xf", r, 0))
                act.wait_ge(ring_emptied[bank], before + 1)
                for i, dst in enumerate((mix_r, mix_k)):
                    for k in range(KD):
                        ins = nc.scalar.activation(dst[:, k, :], xf_t[:, k, 0:HALF], ACT.Copy,
                                                   scale=one_mu[:, i, k:k + 1])
                ins.then_inc(mix_prev_ready, 1)

            def front_conv(kind, b, r, n):
                if kind != "first":
                    act.wait_ge(xc_lo_ready, 2 * n)
                for j in range(2):
                    bank, emptied = filled(kind, b, (f"conv{j}", r, 0))
                    for m in range(2):
                        k = 2 * j + m
                        ins = nc.scalar.activation(xc_whole[:, k, :], bank[:, m * HALF:(m + 1) * HALF], ACT.Identity,
                                                   bias=conv_bias[:, k:k + 1])
                    ins.then_inc(emptied, 1)
                for j in range(2):
                    bank, before = ring_use(kind, b, (f"conv{j}", r, 0))
                    act.wait_ge(ring_emptied[bank], before + 1)
                    nc.scalar.activation(flat(conv_tanh[:, 2 * j:2 * j + 2, :]), conv_act[j], ACT.Tanh,
                                         scale=0.5).then_inc(conv_tanh_ready, 1)

            def front_conv_high(n):
                for j in range(2):
                    act.wait_ge(conv_ready, 2 * n + j + 1)
                    nc.scalar.activation(flat(xc[0][:, 2 * j:2 * j + 2, :]), conv_act[j], ACT.Copy
                                         ).then_inc(xc_hi_ready, 1)

            def front_mix_high(n):
                act.wait_ge(mix_ready, n + 1)
                for mix, (hi, _) in ((mix_k, mix_k_halves), (mix_r, mix_r_halves)):
                    nc.scalar.activation(flat(hi[:]), flat(mix[:]), ACT.Copy).then_inc(mix_hi_ready, 1)

            def front_kact_high(n):
                act.wait_ge(kact_ready, n + 1)
                nc.scalar.activation(flat(kact_halves[0][:]), flat(kact[:]), ACT.Copy).then_inc(kact_hi_ready, 1)

            def front_ffn(kind, b, r, n):
                if kind != "first":
                    act.wait_ge(base_ready, n)
                bank, emptied = filled(kind, b, ("ffn_k", r, 0))
                nc.scalar.activation(flat(kact[:]), bank, ACT.Relu).then_inc(emptied, 1)
                bank, emptied = filled(kind, b, ("ffn_r", r, 0))
                nc.scalar.activation(ffn[:].rearrange("p c d -> p (c d)"), bank, ACT.Tanh,
                                     scale=0.5).then_inc(emptied, 1)

            def front_gates_low(kind, b, r, n):
                bank, _ = filled(kind, b, ("gates", r, 0))
                if kind != "first":
                    act.wait_ge(parts_ready, 2 * n)
                for i, row in enumerate((row_i, row_f)):
                    at = LOW + 32 * i
                    ins = nc.scalar.activation(row[:], bank[at:at + H, 0:HALF], ACT.Identity, bias=if_bias[:, i:i + 1])
                ins.then_inc(gates_low_ready, 1)

            def front_gates(kind, b, r):
                bank, before = ring_use(kind, b, ("gates", r, 0))
                act.wait_ge(ring_emptied[bank], before + 1)
                for row in (row_i, row_f):
                    ins = nc.scalar.activation(row[:], row[:], ACT.Tanh, scale=1.0 / CAP)
                ins.then_inc(gates_ready, 1)

            def front_exps(kind, b, r, n):
                act.wait_ge(exp_args_ready, n + 1)
                if kind != "first":
                    act.wait_ge(cols_ready, n)
                nc.scalar.activation(rows_aw[32:32 + H, :], row_f[:], ACT.Exp).then_inc(exp_rows_ready, 1)
                nc.scalar.activation(row_g[:], row_i[:], ACT.Exp).then_inc(exp_rows_ready, 1)

            def front_heads(kind, b, r, use, j):
                dst, bias = (q_t, q_bias) if use == "q" else (k_t, k_bias)
                bank, emptied = filled(kind, b, (f"{use}{j}", r, 0))
                for m in range(2):
                    ins = nc.scalar.activation(dst[:, 2 * j + m, :], bank[:, m * HALF:(m + 1) * HALF],
                                               ACT.Identity, bias=bias[:, 2 * j + m:2 * j + m + 1])
                ins.then_inc(emptied, 1)

            def front_rest(kind, b, r, n):
                front_gates_low(kind, b, r, n)
                front_gates(kind, b, r)
                front_heads(kind, b, r, "q", 0)
                front_kact_high(n)
                front_exps(kind, b, r, n)
                front_heads(kind, b, r, "q", 1)
                front_heads(kind, b, r, "k", 0)

            def gt_copy(kind, b, h, c):
                bank, _ = filled(kind, b, ("gt", h, c))
                nc.scalar.activation(flat(gt[0][:]), bank, ACT.Copy).then_inc(gt_hi_ready, 1)

            def tile(kind, b, h, c, n):
                if c == 0:
                    act.wait_ge(cols_ready, n + 1)
                for j in range(2):
                    act.wait_ge(sc_filled[j], sc_use(b, h, c, 1))
                    for i in range(4):
                        hd = 2 * i + j
                        ins = nc.scalar.activation(dec[:, j, i, :], sc_ps[:, j, i * T:(i + 1) * T], ACT.Exp,
                                                   scale=-1.0, bias=cols_aw[:, c, hd:hd + 1])
                    ins.then_inc(sc_emptied[j], 1)
                bank, before = ring_use(kind, b, ("r", h, c))
                act.wait_ge(ring_emptied[bank], before + 1)
                nc.scalar.activation(th_r[:], sr[c][:], ACT.Tanh, scale=0.5).then_inc(r_tanh_ready, 1)
                nc.scalar.activation(th_o[c][:], th_o[c][:], ACT.Tanh, scale=0.5).then_inc(o_tanh_ready, 1)

            def body(b, last):
                kind = "last" if last else "body"
                for h in range(2):
                    n = b * 2 + h
                    front = not (last and h == 1)
                    tile(kind, b, h, 0, n)
                    tile(kind, b, h, 1, n)
                    if front:
                        front_x(kind, b, h + 1, n + 1, (h + 1) % 2)
                        front_mix_prev(kind, b, h + 1, n + 1)
                        front_mix_high(n + 1)
                    gt_copy(kind, b, h, 0)
                    if front:
                        front_conv(kind, b, h + 1, n + 1)
                        front_conv_high(n + 1)
                        front_ffn(kind, b, h + 1, n + 1)
                        front_rest(kind, b, h + 1, n + 1)
                    gt_copy(kind, b, h, 1)
                    if front:
                        front_heads(kind, b, h + 1, "k", 1)

            front_x("first", 0, 0, 0, 0)
            front_mix_prev("first", 0, 0, 0)
            front_mix_high(0)
            front_conv("first", 0, 0, 0)
            front_conv_high(0)
            front_ffn("first", 0, 0, 0)
            front_rest("first", 0, 0, 0)
            front_heads("first", 0, 0, "k", 1)
            with act.Fori(0, B - 1) as b:
                body(b, False)
            body(B - 1, True)

        @block.gpsimd
        def _(pool):
            TILE_STEPS = 8

            def front_base(kind, n, h):
                pool.wait_ge(xh_ready, n + 1)
                if kind != "first":
                    for c in range(2):
                        pool.wait_ge(out_stored[c], 16 * n)
                nc.gpsimd.tensor_tensor(base[h][:], xin[:], xf[:], ALU.add).then_inc(x_used, 1)
                pool.wait_ge(x_used, n + 1)
                nc.gpsimd.tensor_tensor(base[h][:], base[h][:], bd_all[:].unsqueeze(1).to_broadcast([T, 2, D]),
                                        ALU.add).then_inc(base_step, 1)
                pool.wait_ge(base_step, n + 1)

            def front_kact(kind, b, r, n):
                bank, before = ring_use(kind, b, ("ffn_k", r, 0))
                pool.wait_ge(ring_emptied[bank], before + 1)
                nc.gpsimd.tensor_tensor(kact[:], kact[:], kact[:], ALU.mult).then_inc(kact_ready, 1)

            def front_kact_low(n):
                pool.wait_ge(kact_hi_ready, n + 1)
                hi, lo = (a[:] for a in kact_halves)
                nc.gpsimd.tensor_tensor(lo, kact[:], hi.bitcast(F32), ALU.subtract).then_inc(kact_lo_ready, 1)

            def front_add(kind, b, r, h):
                bank, before = ring_use(kind, b, ("ffn_v", r, 0))
                pool.wait_ge(ring_emptied[bank], before + 1)
                nc.gpsimd.tensor_tensor(base[h][:], base[h][:], ffn[:], ALU.add).then_inc(base_ready, 1)

            def mask(b, h, c):
                for j in range(2):
                    pool.wait_ge(sc_emptied[j], sc_free(b, h, c, 1))
                settle(pool, pool_settled)
                d = dec[:].rearrange("p j i t -> p (j i) t")
                nc.gpsimd.affine_select(out=d, in_=d, compare_op=ALU.is_ge, fill=0.0, base=0,
                                        pattern=[[0, H], [1, T]], channel_multiplier=-1).then_inc(masked, 1)

            def gain(b, h, c):
                pool.wait_ge(skip_gated, tile_of(b, h, c) + 1)
                nc.gpsimd.tensor_tensor(sr[c][:], sr[c][:], mhg_all[:], ALU.mult).then_inc(gain_ready, 1)

            def norm_scale(b, h, c):
                t = tile_of(b, h, c)
                k = [0]

                def link(ins, settled=False):
                    k[0] += 1
                    ins.then_inc(pool_tile_step, 1)
                    pool.wait_ge(pool_tile_step, t * TILE_STEPS + k[0])
                    if settled:
                        settle(pool, pool_settled)

                pool.wait_ge(mh_stats_ready, t + 1)
                s, d, q, mean, rstd = (mh_sc[:, i, :] for i in range(5))
                mean_e, m2_e, mean_o, m2_o = (mh_st[:, :, i] for i in (1, 2, 4, 5))
                nc.gpsimd.tensor_tensor(s, mean_e, mean_o, ALU.add)
                nc.gpsimd.tensor_tensor(q, m2_e, m2_o, ALU.add)
                link(nc.gpsimd.tensor_tensor(d, mean_e, mean_o, ALU.subtract), settled=True)
                nc.gpsimd.tensor_scalar(mean, s, 0.5, 0.0, ALU.mult, ALU.add)
                nc.gpsimd.tensor_scalar(q, q, 1.0 / HD, 4.0 * EPS_ATTN, ALU.mult, ALU.add)
                link(nc.gpsimd.tensor_tensor(d, d, d, ALU.mult), settled=True)
                link(nc.gpsimd.tensor_scalar(d, d, 0.25, 0.0, ALU.mult, ALU.add))
                link(nc.gpsimd.tensor_tensor(q, q, d, ALU.add))
                link(nc.gpsimd.tensor_tensor(rstd, q, minus_half[:], ALU.pow))
                return link, k, mean, rstd

            def norm(b, h, c, link, k, mean, rstd):
                bc = [T, H, HD]
                link(nc.gpsimd.tensor_tensor(hid[c][:], hid[c][:], mean.unsqueeze(2).to_broadcast(bc), ALU.subtract))
                link(nc.gpsimd.tensor_tensor(hid[c][:], hid[c][:], rstd.unsqueeze(2).to_broadcast(bc), ALU.mult))
                flat = hid[c][:].rearrange("p h d -> p (h d)")
                pool.wait_ge(gain_ready, tile_of(b, h, c) + 1)
                link(nc.gpsimd.tensor_tensor(flat, flat, sr[c][:], ALU.mult))
                nc.gpsimd.tensor_tensor(flat, flat, sk[c][:], ALU.add).then_inc(out_ready[c], 1)
                assert k[0] == TILE_STEPS

            def front_first():
                front_base("first", 0, 0)
                front_kact("first", 0, 0, 0)
                front_kact_low(0)
                front_add("first", 0, 0, 0)

            def body(b, last):
                kind = "last" if last else "body"
                for h in range(2):
                    n = b * 2 + h
                    front = not (last and h == 1)
                    mask(b, h, 0)
                    if front:
                        front_scale(pool, n + 1)
                    gain(b, h, 0)
                    scaled = norm_scale(b, h, 0)
                    mask(b, h, 1)
                    norm(b, h, 0, *scaled)
                    if front:
                        front_base(kind, n + 1, (h + 1) % 2)
                    gain(b, h, 1)
                    norm(b, h, 1, *norm_scale(b, h, 1))
                    if front:
                        front_kact(kind, b, h + 1, n + 1)
                        front_kact_low(n + 1)
                        front_add(kind, b, h + 1, (h + 1) % 2)

            front_first()
            with pool.Fori(0, B - 1) as b:
                body(b, False)
            body(B - 1, True)

        @block.vector
        def _(dve):
            FRONT_STEPS = 10

            def filled(kind, b, use):
                bank, before = ring_use(kind, b, use)
                dve.wait_ge(ring_filled[bank], before + 1)
                return ring[:, bank, :], ring_emptied[bank]

            def front_link(n, used):
                def link(ins):
                    used[0] += 1
                    ins.then_inc(dve_front_step, 1)
                    dve.wait_ge(dve_front_step, n * FRONT_STEPS + used[0])
                return link

            def x_normalise(kind, n):
                dve.wait_ge(scale_ready, n + 1)
                if kind != "first":
                    dve.wait_ge(x_used, n)
                for c in range(2):
                    for dst, k in ((xf, 0), (xa, 2)):
                        ins = nc.vector.tensor_scalar(dst[:, c, :], xin[:, c, :], ln_mv[:, c, 0:1],
                                                      ln_sc[:, k, c:c + 1], ALU.subtract, ALU.mult)
                ins.then_inc(xh_ready, 1)

            def x_low(kind, b, r, n, h):
                bank, emptied = filled(kind, b, ("xa", r, 0))
                dve.wait_ge(xa_hi_ready, n + 1)
                hi, lo = (a[:].rearrange("p k t -> p (k t)") for a in xa_t[h])
                nc.vector.tensor_tensor(lo, bank, hi.bitcast(F32), ALU.subtract).then_inc(emptied, 1)

            def mix(n):
                dve.wait_ge(mix_prev_ready, n + 1)
                for i, dst in enumerate((mix_r, mix_k)):
                    for k in range(KD):
                        ins = nc.vector.scalar_tensor_tensor(out=dst[:, k, :], in0=xf_t[:, k, 1:1 + HALF],
                                                             scalar=mu[:, i, k:k + 1], in1=dst[:, k, :],
                                                             op0=ALU.mult, op1=ALU.add)
                ins.then_inc(mix_ready, 1)

            def mix_low(n, j):
                dve.wait_ge(mix_hi_ready, 2 * n + (j + 1))
                mix, (hi, lo) = ((mix_k, mix_k_halves), (mix_r, mix_r_halves))[j]
                nc.vector.tensor_tensor(flat(lo[:]), flat(mix[:]), flat(hi[:]).bitcast(F32),
                                        ALU.subtract).then_inc(mix_lo_ready, 1)

            def gt_low(kind, b, h, c):
                bank, emptied = filled(kind, b, ("gt", h, c))
                dve.wait_ge(gt_hi_ready, tile_of(b, h, c) + 1)
                hi, lo = (flat(a[:]) for a in gt)
                nc.vector.tensor_tensor(lo, bank, hi.bitcast(F32), ALU.subtract).then_inc(emptied, 1)

            def conv_silu(n):
                for j in range(2):
                    dve.wait_ge(conv_tanh_ready, 2 * n + j + 1)
                    nc.vector.scalar_tensor_tensor(out=conv_act[j], in0=flat(conv_tanh[:, 2 * j:2 * j + 2, :]),
                                                   scalar=1.0, in1=conv_act[j], op0=ALU.add,
                                                   op1=ALU.mult).then_inc(conv_ready, 1)

            def conv_low(n):
                for j in range(2):
                    dve.wait_ge(xc_hi_ready, 2 * n + j + 1)
                    hi, lo = (a[:, 2 * j:2 * j + 2, :].rearrange("p k t -> p (k t)") for a in xc)
                    nc.vector.tensor_tensor(lo, conv_act[j], hi.bitcast(F32), ALU.subtract).then_inc(xc_lo_ready, 1)

            def gate_rows(kind, b, r, n, h, link):
                bank, emptied = filled(kind, b, ("gates", r, 0))
                dve.wait_ge(gates_low_ready, n + 1)
                for row, at in ((row_i, 0), (row_f, 32)):
                    ins = nc.vector.tensor_tensor(row[:], bank[at:at + H, 0:HALF], row[:], ALU.add)
                ins.then_inc(emptied, 1)
                dve.wait_ge(gates_ready, n + 1)
                nc.vector.tensor_scalar(row_i[:], row_i[:], CAP, None, ALU.mult)
                link(nc.vector.tensor_scalar(row_f[:], row_f[:], CAP, None, ALU.mult))
                if h == 1:
                    nc.vector.tensor_copy(row_m[1][:, 0:1], row_m[0][:, HALF:HALF + 1])
                link(nc.vector.tensor_tensor_scan(out=row_F[:], data0=chunk_keep[:], data1=row_f[:], initial=0.0,
                                                  op0=ALU.mult, op1=ALU.add))
                link(nc.vector.tensor_tensor_scan(out=row_m[h][:, 1:], data0=row_f[:], data1=row_i[:],
                                                  initial=row_m[h][:, 0:1], op0=ALU.add, op1=ALU.max))
                nc.vector.tensor_tensor(rows_aw[0:H, :], row_i[:], row_F[:], ALU.subtract)
                link(nc.vector.tensor_tensor(row_M[:], row_m[h][:, 1:], row_F[:], ALU.subtract))

                def chunks(a):
                    return a.rearrange("h (c t) -> h c t", c=2)

                def each_chunk(a):
                    return a.unsqueeze(2).to_broadcast([H, 2, T])

                nc.vector.tensor_tensor(chunks(row_f[:]), chunks(rows_aw[0:H, :]),
                                        each_chunk(row_M[:, T - 1:HALF:T]), ALU.subtract)
                nc.vector.tensor_tensor(chunks(row_i[:]), each_chunk(row_m[h][:, 0:HALF:T]), chunks(row_M[:]),
                                        ALU.subtract).then_inc(exp_args_ready, 1)

            def parts(dst, src, link):
                link(nc.vector.tensor_copy(dst[0:H, :], src))
                link(nc.vector.tensor_tensor(row_rem[:], src, dst[0:H, :], ALU.subtract))
                link(nc.vector.tensor_copy(row_mid[:], row_rem[:]))
                nc.vector.tensor_copy(dst[32:32 + H, :], row_mid[:])
                nc.vector.tensor_tensor(dst[64:64 + H, :], row_rem[:], row_mid[:],
                                        ALU.subtract).then_inc(parts_ready, 1)

            def ffn_gate(kind, b, r):
                rbank, before = ring_use(kind, b, ("ffn_r", r, 0))
                dve.wait_ge(ring_emptied[rbank], before + 1)
                bank, emptied = filled(kind, b, ("ffn_v", r, 0))
                f = ffn[:].rearrange("p c d -> p (c d)")
                nc.vector.scalar_tensor_tensor(out=f, in0=f, scalar=1.0, in1=bank, op0=ALU.add,
                                               op1=ALU.mult).then_inc(emptied, 1)

            def cols_copy(kind, b, r, n):
                bank, emptied = filled(kind, b, ("cols", r, 0))
                nc.vector.tensor_copy(cols_aw[:, 0, :], bank[:, 0:40]).then_inc(cols_ready, 1)
                nc.vector.tensor_copy(cols_aw[:, 1, :], bank[:, 40:80]).then_inc(emptied, 1)

            def reset_state(b):
                nc.vector.memset(state[:], 0.0).then_inc(state_cleared, 1)
                dve.wait_ge(state_cleared, b + 1)
                nc.vector.memset(state[0:HD, :, HD:HD + 1], 1.0)
                nc.vector.memset(state[HD:T, :, PW - 1:PW], 1.0).then_inc(state_reset, 1)

            def add_bias(kind, b, h, c, use):
                dst, bias = (th_o[c], bo_all) if use == "o" else (sr[c], br_all)
                bank, emptied = filled(kind, b, (use, h, c))
                nc.vector.tensor_tensor(dst[:], bank, bias[:], ALU.add).then_inc(emptied, 1)

            def silu_r(b, h, c):
                dve.wait_ge(r_tanh_ready, tile_of(b, h, c) + 1)
                nc.vector.scalar_tensor_tensor(out=sr[c][:], in0=th_r[:], scalar=1.0, in1=sr[c][:], op0=ALU.add,
                                               op1=ALU.mult).then_inc(silu_ready, 1)

            def skip(kind, b, h, c):
                bank, emptied = filled(kind, b, ("skip", h, c))
                nc.vector.tensor_tensor(sk[c][:], bank, bs_all[:], ALU.add).then_inc(emptied, 1)

            def gate_skip(b, h, c):
                nc.vector.tensor_tensor(sk[c][:], sk[c][:], sr[c][:], ALU.mult).then_inc(skip_gated, 1)

            def q_decayed(kind, b, h, c):
                bank, emptied = filled(kind, b, ("decay", h, c))
                d = bank.rearrange("p (j t) -> p j t", j=PAIRS)
                nc.vector.tensor_copy(carry[:], d[:, :, T - 1])
                nc.vector.tensor_tensor(q_dec[:], q_t[:, :, c * T:(c + 1) * T], d, ALU.mult).then_inc(emptied, 1)

            def k_weighted(kind, b, h, c):
                bank, emptied = filled(kind, b, ("kt", h, c))
                if c == 0:
                    dve.wait_ge(cols_ready, b * 2 + (h + 1))
                dve.wait_ge(silu_ready, tile_of(b, h, c) + 1)
                nc.vector.tensor_tensor(k_w[:].rearrange("p (h e) -> p h e", h=H),
                                        bank.rearrange("p (h e) -> p h e", h=H),
                                        cols_aw[:, c, 32:32 + H].unsqueeze(2).to_broadcast([T, H, HD]),
                                        ALU.mult).then_inc(emptied, 1)

            def weigh_scores(b, h, c):
                dve.wait_ge(masked, tile_of(b, h, c) + 1)
                for j in range(2):
                    dve.wait_ge(sc_filled[j], sc_use(b, h, c, 2))
                    nc.vector.tensor_tensor(dec[:, j], sc_ps[:, j, :].rearrange("p (i t) -> p i t", i=PAIRS),
                                            dec[:, j], ALU.mult).then_inc(sc_emptied[j], 1)

            def v_copy(kind, b, h, c):
                bank, emptied = filled(kind, b, ("v", h, c))
                dst = v_sb[:, HD + 1:].rearrange("p (h w) -> p h w", h=H)[:, :, 0:HD]
                nc.vector.tensor_tensor(dst, bank.rearrange("p (h d) -> p h d", h=H),
                                        bv_all[:].rearrange("p (h d) -> p h d", h=H), ALU.add).then_inc(emptied, 1)

            def divide_and_gate(kind, b, h, c):
                t = tile_of(b, h, c)
                dve.wait_ge(num_filled, t + 1)
                num = num_ps[:, :, 0:4 * (HD + 1)].rearrange("p j (i w) -> p j i w", i=4)
                nc.vector.tensor_scalar(den[:], num[:, :, :, HD], 1.0, None, ALU.max).then_inc(den_ready, 1)
                if not (h == 1 and c == 1):
                    nc.vector.tensor_tensor(state[:], state[:], carry[:].unsqueeze(2).to_broadcast([T, PAIRS, PW]),
                                            ALU.mult).then_inc(state_decayed, 1)
                dve.wait_ge(den_ready, 2 * t + 1)
                nc.vector.reciprocal(den[:], den[:]).then_inc(den_ready, 1)
                dve.wait_ge(den_ready, 2 * t + 2)
                nc.vector.tensor_tensor(hid[c][:].rearrange("p (j i) d -> p j i d", j=2), num[:, :, :, 0:HD],
                                        den[:].unsqueeze(3).to_broadcast([T, 2, 4, HD]),
                                        ALU.mult).then_inc(num_emptied, 1)
                dve.wait_ge(num_emptied, t + 2)
                dve.wait_ge(o_tanh_ready, t + 1)
                flat = hid[c][:].rearrange("p h d -> p (h d)")
                nc.vector.scalar_tensor_tensor(out=flat, in0=th_o[c][:], scalar=1.0, in1=flat, op0=ALU.add,
                                               op1=ALU.mult).then_inc(gated[c], 1)

            def update_state(b, h, c):
                dve.wait_ge(state_decayed, b * 3 + (2 * h + c + 1))
                for j in range(2):
                    dve.wait_ge(sc_filled[j], sc_use(b, h, c, 3))
                    chunk = sc_ps[:, j, 0:2 * PW].rearrange("p (i w) -> p i w", i=2)
                    for s in range(2):
                        p = slice(s * HD, (s + 1) * HD)
                        w = slice(s * (HD + 1), (s + 1) * (HD + 1))
                        own = state[p, 2 * j:2 * j + 2, w]
                        ins = nc.vector.tensor_tensor(own, own, chunk[p, :, w], ALU.add)
                    ins.then_inc(sc_emptied[j], 1)

            def head_stats(b, h, c):
                dve.wait_ge(gated[c], b * 2 + (h + 1))
                if c == 1:
                    dve.wait_ge(out_ready[0], b * 2 + (h + 1))
                for i in range(H):
                    ins = nc.vector.bn_stats(mh_st[:, i, :], hid[c][:, i, :])
                ins.then_inc(mh_stats_ready, 1)

            def result(kind, b, h, c):
                bank, emptied = filled(kind, b, ("down", h, c))
                dve.wait_ge(base_ready, b * 2 + (h + 1))
                nc.vector.tensor_tensor(base[h][:, c, :], bank[:, 0:D], base[h][:, c, :], ALU.add).then_inc(emptied, 1)

            def front_gates(kind, b, r, n, h, link):
                gate_rows(kind, b, r, n, h, link)
                parts(m_parts, row_M[:], link)
                dve.wait_ge(exp_rows_ready, 2 * n + 2)
                parts(g_parts, row_g[:], link)

            def front_end(kind, b, r, n, between):
                ffn_gate(kind, b, r)
                between()
                cols_copy(kind, b, r, n)

            def body(b, last):
                kind = "last" if last else "body"
                reset_state(b)
                for h in range(2):
                    n = b * 2 + h
                    front = not (last and h == 1)
                    h2 = (h + 1) % 2
                    used = [0]
                    link = front_link(n + 1, used)
                    if front:
                        x_stats(dve, n + 1)
                    for c in range(2):
                        if c == 1:
                            add_bias(kind, b, h, 1, "o")
                        add_bias(kind, b, h, c, "r")
                        if c == 1 and front:
                            x_normalise(kind, n + 1)
                        skip(kind, b, h, c)
                        silu_r(b, h, c)
                        q_decayed(kind, b, h, c)
                        k_weighted(kind, b, h, c)
                        if c == 0:
                            v_copy(kind, b, h, 0)
                        weigh_scores(b, h, c)
                        gate_skip(b, h, c)
                        if c == 1:
                            v_copy(kind, b, h, 1)
                            if front:
                                x_low(kind, b, h + 1, n + 1, h2)
                                mix(n + 1)
                        divide_and_gate(kind, b, h, c)
                        if c == 1 and front:
                            mix_low(n + 1, 0)
                        if c == 0:
                            update_state(b, h, 0)
                        head_stats(b, h, c)
                    gt_low(kind, b, h, 0)
                    if front:
                        mix_low(n + 1, 1)
                        conv_silu(n + 1)
                        conv_low(n + 1)
                    result(kind, b, h, 0)
                    if front:
                        add_bias(kind, b, h + 1, 0, "o")
                    if h == 0:
                        update_state(b, 0, 1)
                    if front:
                        front_gates(kind, b, h + 1, n + 1, h2, link)
                        front_end(kind, b, h + 1, n + 1, lambda: gt_low(kind, b, h, 1))
                        assert used[0] == FRONT_STEPS, used
                    else:
                        gt_low(kind, b, h, 1)
                    result(kind, b, h, 1)

            for c in range(2):
                dve.sem_inc(sc_emptied[c], 1)
                dve.sem_inc(out_stored[c], 16)
            dve.sem_inc(num_emptied, 1)
            used = [0]
            link = front_link(0, used)
            x_normalise("first", 0)
            nc.vector.memset(rows_aw[:], 0.0)
            nc.vector.memset(m_parts[:], 0.0)
            nc.vector.memset(g_parts[:], 0.0)
            nc.vector.memset(row_m[0][:, 0:1], 0.0)
            nc.vector.memset(v_sb[:], 0.0).then_inc(buffers_cleared, 1)
            dve.wait_ge(buffers_cleared, 1)
            nc.vector.memset(v_sb[:, HD + 1:].rearrange("p (h w) -> p h w", h=H)[:, :, HD:HD + 1],
                             1.0).then_inc(buffers_ready, 1)
            x_low("first", 0, 0, 0, 0)
            mix(0)
            mix_low(0, 0)
            mix_low(0, 1)
            conv_silu(0)
            conv_low(0)
            add_bias("first", 0, 0, 0, "o")
            front_gates("first", 0, 0, 0, 0, link)
            front_end("first", 0, 0, 0, lambda: None)
            with dve.Fori(0, B - 1) as b:
                body(b, False)
            body(B - 1, True)


_INS = ["L0_attn_x", "L0_attn_ln_g", "L0_attn_ln_b", "L0_attn_mh_g", "L0_attn_mh_b", "L0_attn_W_up_l",
        "L0_attn_b_up_l", "L0_attn_W_up_r", "L0_attn_b_up_r", "L0_attn_W_down", "L0_attn_b_down",
        "L0_attn_conv_w", "L0_attn_conv_b", "L0_attn_W_skip", "L0_attn_b_skip", "L0_attn_W_i", "L0_attn_b_i",
        "L0_attn_W_f", "L0_attn_b_f", "L0_attn_W_o", "L0_attn_b_o", "L0_attn_W_q", "L0_attn_b_q",
        "L0_attn_W_k", "L0_attn_b_k", "L0_attn_W_v", "L0_attn_b_v", "L0_ffn_W_r", "L0_ffn_W_k", "L0_ffn_W_v",
        "L0_ffn_mu_r", "L0_ffn_mu_k"]


def kernel(**inputs):
    import numpy as _np
    import concourse.bacc as _bacc
    from concourse import mybir as _mybir
    from concourse.bass_utils import run_bass_kernel_spmd as _run

    nc = _bacc.Bacc("TRN2", target_bir_lowering=False, num_devices=1)
    arrays, args = {}, []
    for name in _INS:
        a = _np.ascontiguousarray(inputs[name])
        arrays[f"in_{name}_dram"] = a
        args.append(nc.dram_tensor(f"in_{name}_dram", a.shape, _mybir.dt.from_np(a.dtype), kind="ExternalInput").ap())
    out = nc.dram_tensor("out_0_dram", arrays["in_L0_attn_x_dram"].shape, _mybir.dt.float32,
                         kind="ExternalOutput").ap()
    mlstm_rwkv_block(nc, *args, out)
    r = _run(nc, [arrays], core_ids=[0])
    return r.results[0]["out_0_dram"]
```
